# Optimizing a Trainium2 kernel written in Bass

```python
import numpy as np
import jax
import jax.numpy as jnp

def _softmax(x, axis=-1):
    return jax.nn.softmax(x, axis=axis)

def _gelu(x):
    return jax.nn.gelu(x, approximate=True)

def _silu(x):
    return jax.nn.silu(x)

def _sigmoid(x):
    return jax.nn.sigmoid(x)

def _layernorm(x, axis=-1, eps=1e-05):
    m = jnp.mean(x, axis=axis, keepdims=True)
    v = jnp.var(x, axis=axis, keepdims=True)
    return (x - m) / jnp.sqrt(v + eps)

def _scatter_add(tgt, idx, src, axis=0):
    return tgt.at[idx].add(src)

def _segment_sum(src, seg, n):
    return jax.ops.segment_sum(src, seg, n)
kernel_name = 'mk_flamingo_gated_d2_seqx_r8_ba69bd'

def setup_inputs(seed: int=0):
    np.random.seed(seed)
    _w = jnp.asarray

    def _rec_inputs():
        import jax
        import jax.numpy as jnp
        _rk = jax.random.key(seed)
        x = -0.0002928 + 1 * jax.random.normal(jax.random.fold_in(_rk, 1), (128, 64, 128), jnp.float32)
        _lenS = 64 - jax.random.randint(jax.random.fold_in(_rk, 7), (128,), 0, max(1, 64 // 4) + 1, jnp.int32)
        _lenS2 = 64 - jax.random.randint(jax.random.fold_in(_rk, 8), (128,), 0, max(1, 64 // 4) + 1, jnp.int32)
        _ctx_1024P = jax.random.normal(jax.random.fold_in(_rk, 11), (128, 16, 128), jnp.float32)
        _ctx_1024c = jax.random.dirichlet(jax.random.fold_in(_rk, 511), 0.3 * jnp.ones((16,), jnp.float32), (128, 64))
        _ctx_1024t = jnp.einsum('bsk,bkd->bsd', _ctx_1024c, _ctx_1024P)
        _ctx_1024t = _ctx_1024t * jax.lax.rsqrt(jnp.mean(jnp.square(_ctx_1024t)) + 1e-12) * 0.953939
        ctx_1024 = -1.39393e-06 + 0.999914 * (_ctx_1024t + 0.3 * jax.random.normal(jax.random.fold_in(_rk, 611), (128, 64, 128), jnp.float32))
        _validS = jnp.arange(64)[None, :] < _lenS[:, None]
        _validS2 = jnp.arange(64)[None, :] < _lenS2[:, None]
        _causal = jnp.tril(jnp.ones((64, 64), dtype=bool))
        mask_Bx1x1xS2_if1 = jnp.where(jnp.ones((128, 1, 1, 64), dtype=bool), 1, 0).astype(jnp.int32)
        _g = jax.random.normal(jax.random.fold_in(_rk, 9001), (2, 2), jnp.float32)
        _g = jnp.sign(_g) * jnp.maximum(jnp.abs(_g), 1.0) + (_g == 0) * 1.0
        g_xattn = _g[0]
        g_ffn = _g[1]
        return (x, ctx_1024, mask_Bx1x1xS2_if1, g_xattn, g_ffn)
    x, ctx_1024, mask_Bx1x1xS2_if1, g_xattn, g_ffn = _rec_inputs()

    def _L0_xattn_setup():
        import jax, jax.numpy as jnp
        import numpy as np
        D_MODEL = 128
        N_HEADS = 16
        D_K = D_MODEL // N_HEADS
        WINDOW = 128
        NEG = -1000000000.0
        key = jax.random.key(seed)
        ks = jax.random.split(key, 11)
        B, S = (2, 256)
        scale = 1.0 / np.sqrt(D_MODEL)
        inp = {'Q': jax.random.normal(ks[0], (B, S, D_MODEL), jnp.float32), 'K': jax.random.normal(ks[1], (B, S, D_MODEL), jnp.float32), 'V': jax.random.normal(ks[2], (B, S, D_MODEL), jnp.float32), 'Wq': jax.random.normal(ks[3], (D_MODEL, D_MODEL), jnp.float32) * scale, 'bq': jnp.zeros((D_MODEL,), jnp.float32), 'Wk': jax.random.normal(ks[4], (D_MODEL, D_MODEL), jnp.float32) * scale, 'bk': jnp.zeros((D_MODEL,), jnp.float32), 'Wv': jax.random.normal(ks[5], (D_MODEL, D_MODEL), jnp.float32) * scale, 'bv': jnp.zeros((D_MODEL,), jnp.float32), 'Wo': jax.random.normal(ks[6], (D_MODEL, D_MODEL), jnp.float32) * scale, 'bo': jnp.zeros((D_MODEL,), jnp.float32)}
        return inp
    _L0_xattn_all = _L0_xattn_setup()
    _L0_xattn_in = {k: v for k, v in _L0_xattn_all.items() if k in ('Wq', 'bq', 'Wk', 'bk', 'Wv', 'bv', 'Wo', 'bo')}
    del _L0_xattn_all

    def _L0_ffn_setup():
        import jax, jax.numpy as jnp
        import numpy as np
        B, S, D, F, E, K = (4, 256, 128, 512, 8, 2)
        key = jax.random.key(seed)
        ks = jax.random.split(key, 6)
        std = 0.02
        x = jax.random.normal(ks[0], (B, S, D), dtype=jnp.float32)
        router_w = jax.random.normal(ks[1], (E, D), dtype=jnp.float32) * std
        W1 = jax.random.normal(ks[2], (E, D, F), dtype=jnp.float32) * std
        b1 = jnp.zeros((E, F), dtype=jnp.float32)
        W2 = jax.random.normal(ks[3], (E, F, D), dtype=jnp.float32) * std
        b2 = jnp.zeros((E, D), dtype=jnp.float32)
        return {'x': x, 'router_w': router_w, 'W1': W1, 'b1': b1, 'W2': W2, 'b2': b2}
    _L0_ffn_all = _L0_ffn_setup()
    _L0_ffn_in = {k: v for k, v in _L0_ffn_all.items() if k in ('router_w', 'W1', 'b1', 'W2', 'b2')}
    del _L0_ffn_all

    def _L1_xattn_setup():
        import jax, jax.numpy as jnp
        import numpy as np
        EMBED = 128
        HEADS = 16
        HEAD_DIM = EMBED // HEADS
        B, S = (4, 256)
        key = jax.random.key(seed)
        ks = jax.random.split(key, 8)
        values = jax.random.normal(ks[0], (B, S, EMBED), dtype=jnp.float32)
        keys_in = jax.random.normal(ks[1], (B, S, EMBED), dtype=jnp.float32)
        query = jax.random.normal(ks[2], (B, S, EMBED), dtype=jnp.float32)
        mask = jnp.ones((B, 1, 1, S), dtype=jnp.int32)
        sc = 1.0 / np.sqrt(HEAD_DIM)
        Wv = jax.random.normal(ks[3], (HEAD_DIM, HEAD_DIM), dtype=jnp.float32) * sc
        Wk = jax.random.normal(ks[4], (HEAD_DIM, HEAD_DIM), dtype=jnp.float32) * sc
        Wq = jax.random.normal(ks[5], (HEAD_DIM, HEAD_DIM), dtype=jnp.float32) * sc
        Wo = jax.random.normal(ks[6], (EMBED, EMBED), dtype=jnp.float32) * (1.0 / np.sqrt(EMBED))
        bo = jnp.zeros((EMBED,), dtype=jnp.float32)
        return {'values': values, 'keys': keys_in, 'query': query, 'mask': mask, 'Wv': Wv, 'Wk': Wk, 'Wq': Wq, 'Wo': Wo, 'bo': bo}
    _L1_xattn_all = _L1_xattn_setup()
    _L1_xattn_in = {k: v for k, v in _L1_xattn_all.items() if k in ('Wv', 'Wk', 'Wq', 'Wo', 'bo')}
    del _L1_xattn_all

    def _L1_ffn_setup():
        import jax, jax.numpy as jnp
        import numpy as np
        D_MODEL = 128
        E = 4
        MIN_E = 1
        TH_LO = 0.5
        TH_HI = 2.0
        key = jax.random.key(seed)
        ks = jax.random.split(key, 12)
        B, N, D, H = (4, 256, D_MODEL, 2 * D_MODEL)
        s = 0.02
        return {'x': jax.random.normal(ks[0], (B, N, D), dtype=jnp.float32), 'gate_w': jax.random.normal(ks[1], (D, E), dtype=jnp.float32) * s, 'gate_b': jnp.zeros((E,), dtype=jnp.float32), 'dp_w1': jax.random.normal(ks[2], (D, D // 2), dtype=jnp.float32) * s, 'dp_b1': jnp.zeros((D // 2,), dtype=jnp.float32), 'dp_w2': jax.random.normal(ks[3], (D // 2, 1), dtype=jnp.float32) * s, 'dp_b2': jnp.zeros((1,), dtype=jnp.float32), 'ew1': jax.random.normal(ks[4], (E, D, H), dtype=jnp.float32) * s, 'eb1': jnp.zeros((E, H), dtype=jnp.float32), 'ew2': jax.random.normal(ks[5], (E, H, D), dtype=jnp.float32) * s, 'eb2': jnp.zeros((E, D), dtype=jnp.float32)}
    _L1_ffn_all = _L1_ffn_setup()
    _L1_ffn_in = {k: v for k, v in _L1_ffn_all.items() if k in ('gate_w', 'gate_b', 'dp_w1', 'dp_b1', 'dp_w2', 'dp_b2', 'ew1', 'eb1', 'ew2', 'eb2')}
    del _L1_ffn_all
    return {'x': x, 'ctx_1024': ctx_1024, 'mask_Bx1x1xS2_if1': mask_Bx1x1xS2_if1, 'g_xattn': g_xattn, 'g_ffn': g_ffn, 'L0_xattn_Wq': _L0_xattn_in['Wq'], 'L0_xattn_bq': _L0_xattn_in['bq'], 'L0_xattn_Wk': _L0_xattn_in['Wk'], 'L0_xattn_bk': _L0_xattn_in['bk'], 'L0_xattn_Wv': _L0_xattn_in['Wv'], 'L0_xattn_bv': _L0_xattn_in['bv'], 'L0_xattn_Wo': _L0_xattn_in['Wo'], 'L0_xattn_bo': _L0_xattn_in['bo'], 'L0_ffn_router_w': _L0_ffn_in['router_w'], 'L0_ffn_W1': _L0_ffn_in['W1'], 'L0_ffn_b1': _L0_ffn_in['b1'], 'L0_ffn_W2': _L0_ffn_in['W2'], 'L0_ffn_b2': _L0_ffn_in['b2'], 'L1_xattn_Wv': _L1_xattn_in['Wv'], 'L1_xattn_Wk': _L1_xattn_in['Wk'], 'L1_xattn_Wq': _L1_xattn_in['Wq'], 'L1_xattn_Wo': _L1_xattn_in['Wo'], 'L1_xattn_bo': _L1_xattn_in['bo'], 'L1_ffn_gate_w': _L1_ffn_in['gate_w'], 'L1_ffn_gate_b': _L1_ffn_in['gate_b'], 'L1_ffn_dp_w1': _L1_ffn_in['dp_w1'], 'L1_ffn_dp_b1': _L1_ffn_in['dp_b1'], 'L1_ffn_dp_w2': _L1_ffn_in['dp_w2'], 'L1_ffn_dp_b2': _L1_ffn_in['dp_b2'], 'L1_ffn_ew1': _L1_ffn_in['ew1'], 'L1_ffn_eb1': _L1_ffn_in['eb1'], 'L1_ffn_ew2': _L1_ffn_in['ew2'], 'L1_ffn_eb2': _L1_ffn_in['eb2']}

def reference(x, ctx_1024, mask_Bx1x1xS2_if1, g_xattn, g_ffn, L0_xattn_Wq, L0_xattn_bq, L0_xattn_Wk, L0_xattn_bk, L0_xattn_Wv, L0_xattn_bv, L0_xattn_Wo, L0_xattn_bo, L0_ffn_router_w, L0_ffn_W1, L0_ffn_b1, L0_ffn_W2, L0_ffn_b2, L1_xattn_Wv, L1_xattn_Wk, L1_xattn_Wq, L1_xattn_Wo, L1_xattn_bo, L1_ffn_gate_w, L1_ffn_gate_b, L1_ffn_dp_w1, L1_ffn_dp_b1, L1_ffn_dp_w2, L1_ffn_dp_b2, L1_ffn_ew1, L1_ffn_eb1, L1_ffn_ew2, L1_ffn_eb2):
    import jax
    import jax.numpy as jnp

    def _L0_xattn_ref(Q, K, V, Wq, bq, Wk, bk, Wv, bv, Wo, bo):
        import jax, jax.numpy as jnp
        import numpy as np
        D_MODEL = 128
        N_HEADS = 16
        D_K = D_MODEL // N_HEADS
        WINDOW = 128
        NEG = -1000000000.0
        B, S, _ = Q.shape
        q = Q @ Wq + bq
        k = K @ Wk + bk
        v = V @ Wv + bv
        q = q.reshape(B, S, N_HEADS, D_K).transpose(0, 2, 1, 3)
        k = k.reshape(B, S, N_HEADS, D_K).transpose(0, 2, 1, 3)
        v = v.reshape(B, S, N_HEADS, D_K).transpose(0, 2, 1, 3)
        scores = jnp.einsum('bhqd,bhkd->bhqk', q, k) / jnp.sqrt(jnp.float32(D_K))
        rel = jnp.arange(S)[None, :] - jnp.arange(S)[:, None]
        win = (rel >= -WINDOW) & (rel <= WINDOW)
        scores = jnp.where(win[None, None], scores, NEG)
        probs = jax.nn.softmax(scores, axis=-1)
        out = jnp.einsum('bhqk,bhkd->bhqd', probs, v)
        out = out.transpose(0, 2, 1, 3).reshape(B, S, D_MODEL)
        return out @ Wo + bo

    def _L0_ffn_ref(x, router_w, W1, b1, W2, b2):
        import jax, jax.numpy as jnp
        import numpy as np
        B, S, D, F, E, K = (4, 256, 128, 512, 8, 2)
        logits = jnp.einsum('bsd,ed->bse', x, router_w)
        probs = jax.nn.softmax(logits, axis=-1)
        top_p, top_i = jax.lax.top_k(probs, K)
        top_p = top_p / (jnp.sum(top_p, axis=-1, keepdims=True) + 1e-08)
        out = jnp.zeros_like(x)
        for e in range(E):
            w_e = jnp.sum(jnp.where(top_i == e, top_p, 0.0), axis=-1)
            h = jax.nn.gelu(jnp.einsum('bsd,df->bsf', x, W1[e]) + b1[e])
            y = jnp.einsum('bsf,fd->bsd', h, W2[e]) + b2[e]
            out = out + w_e[..., None] * y
        return out

    def _L1_xattn_ref(values, keys, query, mask, Wv, Wk, Wq, Wo, bo):
        import jax, jax.numpy as jnp
        import numpy as np
        EMBED = 128
        HEADS = 16
        HEAD_DIM = EMBED // HEADS
        B, S = (4, 256)
        n = query.shape[0]
        vl, kl, ql = (values.shape[1], keys.shape[1], query.shape[1])
        h, d = (HEADS, HEAD_DIM)
        v = values.reshape(n, vl, h, d)
        k = keys.reshape(n, kl, h, d)
        q = query.reshape(n, ql, h, d)
        v = jnp.einsum('nlhd,ed->nlhe', v, Wv)
        k = jnp.einsum('nlhd,ed->nlhe', k, Wk)
        q = jnp.einsum('nlhd,ed->nlhe', q, Wq)
        energy = jnp.einsum('nqhd,nkhd->nhqk', q, k)
        energy = jnp.where(mask == 0, jnp.float32(-1e+20), energy)
        attn = jax.nn.softmax(energy / jnp.sqrt(jnp.float32(EMBED)), axis=3)
        out = jnp.einsum('nhql,nlhd->nqhd', attn, v).reshape(n, ql, h * d)
        return out @ Wo.T + bo

    def _L1_ffn_ref(x, gate_w, gate_b, dp_w1, dp_b1, dp_w2, dp_b2, ew1, eb1, ew2, eb2):
        import jax, jax.numpy as jnp
        import numpy as np
        D_MODEL = 128
        E = 4
        MIN_E = 1
        TH_LO = 0.5
        TH_HI = 2.0
        B, N, D = x.shape
        xf = x.reshape(B * N, D)
        T = B * N
        h = jax.nn.relu(xf @ dp_w1 + dp_b1)
        entropy = jax.nn.softplus(h @ dp_w2 + dp_b2)[:, 0]
        norm = jnp.clip((entropy - TH_LO) / (TH_HI - TH_LO), 0.0, 1.0)
        k_tok = jnp.clip(jnp.round(MIN_E + norm * (E - MIN_E)).astype(jnp.int32), MIN_E, E)
        logits = xf @ gate_w + gate_b
        top_logits, top_idx = jax.lax.top_k(logits, E)
        pos = jnp.arange(E)
        sel = pos[None, :] < k_tok[:, None]
        masked = jnp.where(sel, top_logits, -jnp.inf)
        w_top = jax.nn.softmax(masked, axis=-1)
        dense_w = jnp.zeros((T, E), dtype=xf.dtype).at[jnp.arange(T)[:, None], top_idx].set(w_top)
        hid = jax.nn.relu(jnp.einsum('td,edh->teh', xf, ew1) + eb1[None, :, :])
        y = jnp.einsum('teh,ehd->ted', hid, ew2) + eb2[None, :, :]
        out = jnp.einsum('te,ted->td', dense_w, y)
        return out.reshape(B, N, D)
    x = x + jnp.tanh(g_xattn[0]) * _L0_xattn_ref(_layernorm(x, axis=-1), ctx_1024, ctx_1024, L0_xattn_Wq, L0_xattn_bq, L0_xattn_Wk, L0_xattn_bk, L0_xattn_Wv, L0_xattn_bv, L0_xattn_Wo, L0_xattn_bo)
    x = x + jnp.tanh(g_ffn[0]) * _L0_ffn_ref(_layernorm(x, axis=-1), L0_ffn_router_w, L0_ffn_W1, L0_ffn_b1, L0_ffn_W2, L0_ffn_b2)
    x = x + jnp.tanh(g_xattn[1]) * _L1_xattn_ref(ctx_1024, ctx_1024, _layernorm(x, axis=-1), mask_Bx1x1xS2_if1, L1_xattn_Wv, L1_xattn_Wk, L1_xattn_Wq, L1_xattn_Wo, L1_xattn_bo)
    x = x + jnp.tanh(g_ffn[1]) * _L1_ffn_ref(_layernorm(x, axis=-1), L1_ffn_gate_w, L1_ffn_gate_b, L1_ffn_dp_w1, L1_ffn_dp_b1, L1_ffn_dp_w2, L1_ffn_dp_b2, L1_ffn_ew1, L1_ffn_eb1, L1_ffn_ew2, L1_ffn_eb2)
    return x

_drawn_inputs = setup_inputs


def setup_inputs(seed=0):
    import zlib

    import numpy as np

    out = dict(_drawn_inputs(seed))
    spreads = {'g_ffn': (-1.0, 0.6),
     'L0_xattn_bq': (0.0, 0.373),
     'L0_xattn_bk': (0.0, 0.8),
     'L0_xattn_bv': (0.0, 0.1),
     'L0_xattn_bo': (0.0, 0.1),
     'L0_ffn_b1': (0.0, 0.575),
     'L0_ffn_b2': (0.0, 0.1),
     'L1_xattn_bo': (0.0, 0.1),
     'L1_ffn_gate_b': (0.0, 0.1),
     'L1_ffn_dp_b1': (0.0, 0.1),
     'L1_ffn_eb1': (0.0, 0.55),
     'L1_ffn_eb2': (0.0, 0.1)}
    factors = {}
    for name, (base, spread) in spreads.items():
        noise = np.random.default_rng([zlib.crc32(name.encode()), seed]).standard_normal(out[name].shape)
        drawn = base * np.exp(spread * noise) if base else spread * noise
        out[name] = jnp.asarray(drawn.astype(out[name].dtype))
    for name, factor in factors.items():
        out[name] = (out[name] * factor).astype(out[name].dtype)
    return out
```

```python
import numpy as np
import concourse.bass as bass
from concourse import mybir
from contextlib import ExitStack

F32 = mybir.dt.float32
BF16 = mybir.dt.bfloat16
I32 = mybir.dt.int32
ALU = mybir.AluOpType
ACT = mybir.ActivationFunctionType
AX = mybir.AxisListType.X

P = 128
B, S, DM = 128, 64, 128
H, DK = 16, 8
TOK = B * S
TILES = TOK // P
GROUPS = TILES // 2
GT = 2 * P
VW = 2 * DK + 2
E0, F0 = 8, 512
FB0 = F0 // P
E1, F1 = 4, 256
FB1 = F1 // P
HD1 = DM // 2
ET = 256
NT = 2 * TOK // ET + E0
RE = TOK + ET * (E0 + 1)
EPS = 1e-5
BIG = 3e38
NEG = -1e20
SCALES = (DK ** -0.5, DM ** -0.5)
ROUND = 12582912.0

C_ID, C_TRI, C_IND = 0, 128, 256
C_BLK = 384
C_DESC = C_BLK + 4
C_BASE = C_DESC + E0
C_ROW = C_BASE + E0
C_THR = C_ROW + NT
C_TIE = C_THR + TOK // ET
C_ALL = C_TIE + E1 * E1


def constants():
    c = np.zeros((P, C_ALL), np.float32)
    c[:, C_ID:C_ID + P] = np.eye(P)
    c[:, C_TRI:C_TRI + P] = np.triu(np.ones((P, P)), 1)
    c[0, C_IND:C_IND + S] = 1
    c[1, C_IND + S:C_IND + P] = 1
    for i in range(4):
        c[:, C_BLK + i] = (np.arange(P) % 32) // DK == i
    c[:, C_DESC:C_DESC + E0] = E0 - np.arange(E0)
    c[:, C_BASE:C_BASE + E0] = RE * np.arange(E0)
    c[:, C_ROW:C_ROW + NT] = ET * np.arange(NT)
    c[:, C_THR:C_THR + TOK // ET] = ET * np.arange(TOK // ET)
    c[:, C_TIE:C_ALL] = np.tril(np.ones((E1, E1)), -1).reshape(-1)
    return c


def at(u, k, mult=1, add=0):
    if isinstance(u, int):
        return mult * (2 * u + k) + add
    return u * (2 * mult) + (mult * k + add)


SETUP = 16 * 20
LOOP0, LOOP1 = 6, GROUPS - 4


def carry(touch, value):
    if not isinstance(value, int):
        touch()


class Group:

    def __init__(self, u, k, layer):
        self.u, self.k, self.layer, self.par = u, k, layer, k % 2

    def plus(self, d):
        return Group(self.u, self.k + d, self.layer)

    def real(self):
        return not isinstance(self.u, int) or 0 <= self.k < GROUPS

    def at(self, mult=1, add=0):
        return at(self.u, self.k, mult, add)

    def count(self, mult=1, add=0):
        return at(self.u, self.k, mult, add + mult * GROUPS * self.layer)

    def half_count(self):
        return self.u * 16 + 16 * (self.k // 2 + 1 + GROUPS // 2 * self.layer)

    def block(self, add=0):
        return self.u + (self.k // 2 + add)


def wait(eng, sem, value):
    if not isinstance(value, int) or value > 0:
        eng.wait_ge(sem, value)


def build(nc, A, out):
    with ExitStack() as ctx:
        def sb(name, shape, dt=F32):
            return ctx.enter_context(nc.sbuf_tensor(name, shape, dt))

        def sem(name):
            return ctx.enter_context(nc.semaphore(name))

        ps_s = ctx.enter_context(nc.psum_tensor("ps_s", [P, 4, 512], F32))
        ps_p = ctx.enter_context(nc.psum_tensor("ps_p", [P, 2, 512], F32))
        ps_m = ctx.enter_context(nc.psum_tensor("ps_m", [P, 2, 512], F32))

        x = sb("x", [P, TILES, DM])
        xn3T = sb("xn3T", [P, TOK])
        cst = sb("cst", [P, C_ALL])
        tri = sb("tri", [P, P], BF16)
        ones = sb("ones", [P, P], BF16)
        ind = sb("ind", [2, P], BF16)
        negm = sb("negm", [2, TILES, S], BF16)
        wq = [sb(f"wq{i}", [P, DM]) for i in range(2)]
        wk = [sb(f"wk{i}", [P, DM]) for i in range(2)]
        wv = [sb(f"wv{i}", [P, DM]) for i in range(2)]
        wo = [sb(f"wo{i}", [P, DM]) for i in range(2)]
        bcol = sb("bcol", [P, 3])
        zcol = sb("zcol", [P, 1])
        bo = [sb(f"bo{i}", [P, DM]) for i in range(2)]
        orow = [sb(f"orow{i}", [P, DM]) for i in range(2)]
        gates = sb("gates", [P, 4])
        tg = sb("tg", [P, 4])
        wr0 = sb("wr0", [P, E0])
        wr1 = sb("wr1", [P, E1 + HD1])
        gb1 = sb("gb1", [P, E1])
        db1 = sb("db1", [P, HD1])
        dw2 = sb("dw2", [P, HD1])
        db2 = sb("db2", [P, 1])
        w1a = sb("w1a", [P, E0 * F0])
        w2a = sb("w2a", [P, E0 * F0])
        b1a = sb("b1a", [P, E0 * FB0])
        b2a = sb("b2a", [P, E0, DM])
        v1 = sb("v1", [P, E1 * F1])
        v2 = sb("v2", [P, E1 * F1])
        c1 = sb("c1", [P, E1 * FB1])
        c2 = sb("c2", [P, E1, DM])
        ctxg = [sb(f"ctxg{i}", [P, 4, 2, S]) for i in range(2)]
        xn = [sb(f"xn{i}", [P, 2, DM]) for i in range(2)]
        xnT = [sb(f"xnT{i}", [P, GT]) for i in range(2)]
        qT = [sb(f"qT{i}", [P, GT]) for i in range(2)]
        kT = [sb(f"kT{i}", [P, GT]) for i in range(2)]
        Kbd = [sb(f"Kbd{i}", [P, 4, 4, S]) for i in range(2)]
        Vbd = [sb(f"Vbd{i}", [P, 4, 8, VW]) for i in range(2)]
        Pr = [sb(f"Pr{i}", [P, 4, 512]) for i in range(2)]
        mx = [sb(f"mx{i}", [P, 4, 8]) for i in range(2)]
        PT = [sb(f"PT{i}", [P, 512]) for i in range(4)]
        rden = sb("rden", [P, 2, 8, 2])
        On = [sb(f"On{i}", [P, 2, DM]) for i in range(2)]
        OT = [sb(f"OT{i}", [P, GT]) for i in range(2)]
        xc = [sb(f"xc{i}", [P, 2, DM]) for i in range(2)]
        xn2 = [sb(f"xn2{i}", [P, 2, DM]) for i in range(2)]
        xn2T = [sb(f"xn2T{i}", [P, GT]) for i in range(2)]
        stq, mvq, rsq = sb("stq", [P, 2, 6]), sb("mvq", [P, 2, 2]), sb("rsq", [P, 2])
        stf, mvf, rsf = sb("stf", [P, 2, 6]), sb("mvf", [P, 2, 2]), sb("rsf", [P, 2])
        veq, vef, mhalf = sb("veq", [P, 2]), sb("vef", [P, 2]), sb("mhalf", [P, 2])
        eps2, spare, spare_v = sb("eps2", [P, 2]), sb("spare", [1, 2]), sb("spare_v", [1, 1])
        lgb = sb("lgb", [P, 4, E0])
        m1 = sb("m1", [P, 4])
        dlt = sb("dlt", [P, 4, E0])
        cand = sb("cand", [P, 4, E0])
        top = sb("top", [P, 4])
        hot = sb("hot", [P, 2, 4, E0])
        dl2 = sb("dl2", [P, 4, E0])
        m2 = sb("m2", [P, 4])
        hotb = sb("hotb", [P, 4, E0], BF16)
        seen = sb("seen", [P, E0])
        seenb = sb("seenb", [P, E0], BF16)
        hsum = sb("hsum", [P, E0])
        rank = sb("rank", [P, 4, E0])
        rsel = sb("rsel", [P, 2, 4, E0])
        posf = sb("posf", [P, 2, 4])
        pos = sb("pos", [P, 2, 4], I32)
        pos_all = sb("pos_all", [P, TILES // 4, 8])
        moved = sb("moved", [P, TILES // 4, 8])
        place = sb("place", [P, TILES // 4, 8], I32)
        d_all = sb("d_all", [P, TILES, E0])
        m2_all = sb("m2_all", [P, TILES])
        xs = sb("xs", [P, 4, DM])
        w_all = sb("w_all", [P, TILES, 2])
        p2 = sb("p2", [P, TILES])
        den = sb("den", [P, TILES])
        cnt = sb("cnt", [P, E0])
        cnti = sb("cnti", [1, E0], I32)
        cge = sb("cge", [P, E0, TOK // ET])
        ntl = sb("ntl", [P, E0])
        nend = sb("nend", [1, E0])
        oneE = sb("oneE", [1, E0])
        jump = sb("jump", [P, E0])
        tge = sb("tge", [1, NT, E0 - 1])
        tjump = sb("tjump", [1, NT, E0 - 1])
        tef = sb("tef", [1, NT])
        trf = sb("trf", [1, NT])
        tei = sb("tei", [1, NT], I32)
        tri_row = sb("tri_row", [1, NT], I32)
        zero = sb("zero", [P, ET])
        def late(col, n):
            return xn3T[:, col:col + n]

        w1s = [late(F0 * i, F0) for i in range(2)]
        w2s = [late(2 * F0 + F0 * i, F0) for i in range(2)]
        hT = [late(4 * F0 + FB0 * ET * i, FB0 * ET).rearrange("p (f t) -> p f t", f=FB0) for i in range(2)]
        EX = 4 * F0 + 2 * FB0 * ET
        xin = [late(EX + ET * i, ET).rearrange("p (t d) -> p t d", t=2) for i in range(2)]
        xinT = [late(EX + 2 * ET + ET * i, ET) for i in range(2)]
        yo = [late(EX + 4 * ET + ET * i, ET).rearrange("p (t d) -> p t d", t=2) for i in range(2)]
        maskn = xn3T[0:2, 0:TILES * S].bitcast(I32).rearrange("b (t k) -> b t k", t=TILES)
        b1s = [sb(f"b1s{i}", [P, FB0]) for i in range(2)]
        ysb = [w1a[:, 2 * GT * i:2 * GT * (i + 1)].rearrange("p (s t d) -> p s t d", s=2, t=2) for i in range(2)]
        gi = [sb(f"gi{i}", [P, 4], I32) for i in range(2)]
        t1 = sb("t1", [P, 2, HD1])
        t2 = sb("t2", [P, 2, HD1])
        z_all = sb("z_all", [P, TILES])
        gl = sb("gl", [P, TILES, E1])
        big = [Pr[i][:, 0:2, :].rearrange("p a (t e f) -> p (a t) e f", e=E1, f=E1) for i in range(2)]
        sel = Pr[0][:, 2, 0:TILES * E1].rearrange("p (t e) -> p t e", e=E1)
        we = sb("we", [P, TILES, E1])
        ent, ent2, gmx, kt = (sb(n, [P, TILES]) for n in ("ent", "ent2", "gmx", "kt"))
        hD = [Kbd[i][:, :, :, :].rearrange("p a b k -> p (a b k)").rearrange("p (f t) -> p f t", f=FB1)
              for i in range(2)]

        lists = nc.dram_tensor("lists", [E0 * RE, DM], F32, kind="Internal").ap()
        louts = nc.dram_tensor("louts", [NT * ET, DM], F32, kind="Internal").ap()

        ident = cst[:, C_ID:C_ID + P]
        blk = cst[:, C_BLK:C_BLK + 4]
        desc = cst[:, C_DESC:C_DESC + E0]
        base = cst[:, C_BASE:C_BASE + E0]
        bank6, bank7 = ps_m[:, 0, :], ps_m[:, 1, :]

        setup_in, x_in0, x_in1, experts_in, mask_in = (sem(n) for n in (
            "setup_in", "x_in0", "x_in1", "experts_in", "mask_in"))
        ctx_in = [sem("ctx_in0"), sem("ctx_in1")]
        tanh_done, consts_done, wo_scaled, bv_done, orow_done = (sem(n) for n in (
            "tanh_done", "consts_done", "wo_scaled", "bv_done", "orow_done"))
        lnq_st, lnq_mv, lnq_rs, xn_ready = (sem(n) for n in ("lnq_st", "lnq_mv", "lnq_rs", "xn_ready"))
        lnq_ve, lnf_ve = sem("lnq_ve"), sem("lnf_ve")
        lnf_st, lnf_mv, lnf_rs, xn2_ready = (sem(n) for n in ("lnf_st", "lnf_mv", "lnf_rs", "xn2_ready"))
        xt_done, kq_done, v_done, s_done, pt_done, pv_done = (sem(n) for n in (
            "xt_done", "kq_done", "v_done", "s_done", "pt_done", "pv_done"))
        ot_done, out_done, xt2_done, lg_done, rk_done = (sem(n) for n in (
            "ot_done", "out_done", "xt2_done", "lg_done", "rk_done"))
        xnT_ready, k_ready, q_ready, kbd_ready, v_ready = (sem(n) for n in (
            "xnT_ready", "k_ready", "q_ready", "kbd_ready", "v_ready"))
        max_done, sub_done, exp_done, pt_ready = (sem(n) for n in ("max_done", "sub_done", "exp_done", "pt_ready"))
        rec_done, on_ready, ot_ready, xc_ready, x1_ready = (sem(n) for n in (
            "rec_done", "on_ready", "ot_ready", "xc_ready", "x1_ready"))
        xn2T_ready, lg_read, gate_step = (sem(n) for n in ("xn2T_ready", "lg_read", "gate_step"))
        route, hot_ready, rank_read, seen_ready, pos_ready, xs_ready, scattered = (sem(n) for n in (
            "route", "hot_ready", "rank_read", "seen_ready", "pos_ready", "xs_ready", "scattered"))
        place2, place_ready, move_step = sem("place2"), sem("place_ready"), sem("move_step")
        cnt_done, cnti_ready, plan_step, plan_ready, zeros_in = (sem(n) for n in (
            "cnt_done", "cnti_ready", "plan_step", "plan_ready", "zeros_in"))
        dexp_done, w_step, w_ready = (sem(n) for n in ("dexp_done", "w_step", "w_ready"))
        rows_in = [sem("rows_in0"), sem("rows_in1")]
        rows_out = [sem("rows_out0"), sem("rows_out1")]
        w1_ready, w2_ready, xinT_ready, yo_ready = (sem(n) for n in ("w1_ready", "w2_ready", "xinT_ready", "yo_ready"))
        et_done, h_done, gelu_done, y_done = (sem(n) for n in ("et_done", "h_done", "gelu_done", "y_done"))
        gathered = [sem("gathered0"), sem("gathered1")]
        gi_ready, comb_step, comb_done = (sem(n) for n in ("gi_ready", "comb_step", "comb_done"))
        ent_step, ent_act, gates_step, gates_act, gates_ready = (sem(n) for n in (
            "ent_step", "ent_act", "gates_step", "gates_act", "gates_ready"))
        h1_done, relu_done, y1_done, acc_b, acc_y, out_st = (sem(n) for n in (
            "h1_done", "relu_done", "y1_done", "acc_b", "acc_y", "out_st"))

        drained = {
            "OT": (ot_ready, 1, 1), "OUT": (x1_ready, 1, 1), "O0": (on_ready, 2, 1), "O1": (on_ready, 2, 2),
            "V": (v_ready, 1, 1), "LG": (lg_read, 1, 1), "XT": (xnT_ready, 1, 1), "KQ": (q_ready, 1, 1),
            "XT2": (xn2T_ready, 1, 1)}

        def jobs(bank, g):
            if bank == 6:
                found = [("OT", g.plus(-2)), ("OUT", g.plus(-2)), ("O1", g.plus(-1)), ("V", g.plus(1)),
                         ("LG", g.plus(-2))]
                if g.layer == 0 and g.k % 2:
                    found.append(("RK", g.plus(-2)))
            else:
                found = [("XT", g.plus(1)), ("O0", g.plus(-1)), ("KQ", g.plus(1)), ("XT2", g.plus(-2))]
            return [j for j in found if j[1].real()]

        def bank_free(pe, bank, g, name):
            names = jobs(bank, g)
            i = [n for n, _ in names].index(name)
            before = names[:i]
            for back in range(1, 4):
                before = before or jobs(bank, g.plus(-back))
            if not before:
                return
            last, m = before[-1]
            if last == "RK":
                pe.wait_ge(rank_read, m.block(1))
            else:
                s_, mult, add = drained[last]
                pe.wait_ge(s_, m.count(mult, add))

        def steps(eng, layer, step):
            for s in range(-3, LOOP0):
                step(Group(0, s, layer))
            with eng.Fori(0, (LOOP1 - LOOP0) // 2) as u:
                step(Group(u, LOOP0, layer))
                step(Group(u, LOOP0 + 1, layer))
            for s in range(LOOP1, GROUPS + 4):
                step(Group(0, s, layer))

        def sl(t, n=1):
            return slice(t, t + n) if isinstance(t, int) else bass.ds(t, n)

        block = ctx.enter_context(nc.Block())

        @block.sync
        def _(sp):
            xv = A["x"].rearrange("(t p) d -> p t d", p=P)
            sp.dma_start(x[:, 0:8, :], xv[:, 0:8, :]).then_inc(x_in0, 16)
            for dst, src in ((cst[:, :], A["consts"]), (wk[0][:, :], A["L0_xattn_Wk"]), (wq[0][:, :], A["L0_xattn_Wq"]),
                             (wv[0][:, :], A["L0_xattn_Wv"]), (wo[0][:, :], A["L0_xattn_Wo"]),
                             (bcol[:, :], A["bcol"]), (gates[:, :], A["gates"].partition_broadcast(P)),
                             (bo[0][:, :], A["L0_xattn_bo"].partition_broadcast(P)),
                             (bo[1][:, :], A["L1_xattn_bo"].partition_broadcast(P)),
                             (wq[1][:, :], A["wq1"]), (wk[1][:, :], A["wk1"]), (wv[1][:, :], A["wv1"]),
                             (wo[1][:, :], A["wo1"]), (wr0[:, :], A["wr0"]), (wr1[:, :], A["wr1"]),
                             (gb1[:, :], A["L1_ffn_gate_b"].partition_broadcast(P)),
                             (db1[:, :], A["L1_ffn_dp_b1"].partition_broadcast(P)),
                             (dw2[:, :], A["dw2"].partition_broadcast(P)),
                             (db2[:, :], A["L1_ffn_dp_b2"].partition_broadcast(P)),
                             (maskn, A["mask"].rearrange("(t b) k -> b t k", b=2))):
                sp.dma_start(dst, src).then_inc(setup_in, 16)
            sp.dma_start(x[:, 8:TILES, :], xv[:, 8:TILES, :]).then_inc(x_in1, 16)

            def load_ctx(g):
                wait(sp, v_done, g.count(1, -1))
                sp.dma_start(ctxg[g.par][:, :, :, :].rearrange("p b i k -> p (b i k)"), A["ctxT"][:, sl(g.at(2 * GT), 2 * GT)]).then_inc(ctx_in[g.par], 16)

            def step(g):
                if g.plus(2).real():
                    load_ctx(g.plus(2))
                if g.layer == 0 and isinstance(g.u, int) and g.k == 0:
                    for dst, src in ((w1a[:, :].rearrange("p (e f) -> p e f", e=E0), A["L0_ffn_W1"].rearrange("e d f -> d e f")),
                                     (w2a[:, :].rearrange("p (e f d) -> p (e f) d", e=E0, f=FB0),
                                      A["L0_ffn_W2"].rearrange("e (f p) d -> p (e f) d", p=P)),
                                     (b1a[:, :], A["b1a"]),
                                     (b2a[:, :, :].rearrange("p e d -> p (e d)"), A["b2a"].partition_broadcast(P)),
                                     (v1[:, :].rearrange("p (e f) -> p e f", e=E1), A["L1_ffn_ew1"].rearrange("e d f -> d e f")),
                                     (v2[:, :].rearrange("p (e f d) -> p (e f) d", e=E1, f=FB1),
                                      A["L1_ffn_ew2"].rearrange("e (f p) d -> p (e f) d", p=P)),
                                     (c1[:, :], A["c1"]),
                                     (c2[:, :, :].rearrange("p e d -> p (e d)"), A["c2"].partition_broadcast(P))):
                        sp.dma_start(dst, src).then_inc(experts_in, 16)

            steps(sp, 0, step)
            sp.wait_ge(cnti_ready, 1)
            for e in range(E0):
                n = sp.value_load(cnti[0:1, e:e + 1], min_val=0, max_val=TOK)
                for i in range(1 if e < E0 - 1 else E0 + 1):
                    sp.dma_start(lists[bass.ds(n + (e * RE + i * ET), ET), :].rearrange("(p b) d -> p (b d)", p=P),
                                 zero[:, :]).then_inc(zeros_in, 16)
            sp.wait_ge(zeros_in, 16 * (2 * E0))
            sp.wait_ge(plan_ready, 1)
            sp.wait_ge(scattered, 16 * 8 * (TILES // 4))

            def load_rows(u, k):
                wait(sp, et_done, at(u, k, 1, -1))
                r = sp.value_load(tri_row[0:1, sl(at(u, k))], min_val=0, max_val=E0 * RE - ET)
                sp.dma_start(xin[k % 2], lists[bass.ds(r, ET), :].rearrange("(t p) d -> p t d", p=P)).then_inc(
                    rows_in[k % 2], 16)

            def store_rows(u, k):
                sp.wait_ge(yo_ready, at(u, k, 1, 1))
                sp.dma_start(louts[sl(at(u, k, ET), ET), :].rearrange("(t p) d -> p t d", p=P), yo[k % 2]).then_inc(
                    rows_out[k % 2], 16)

            load_rows(0, 0)
            load_rows(0, 1)
            with sp.Fori(0, NT // 2 - 1) as u:
                load_rows(u, 2)
                store_rows(u, 0)
                load_rows(u, 3)
                store_rows(u, 1)
            store_rows(0, NT - 2)
            store_rows(0, NT - 1)

            steps(sp, 1, step)

            ov = out.rearrange("(t p) d -> p t d", p=P)

            def store_out(c):
                sp.wait_ge(acc_y, c * (4 * E1) + 4 * E1)
                sp.dma_start(ov[:, sl(c * 4, 4), :], x[:, sl(c * 4, 4), :]).then_inc(out_st, 16)

            with sp.Fori(0, TILES // 4) as c:
                store_out(c)
            sp.wait_ge(out_st, 16 * (TILES // 4))

        @block.gpsimd
        def _(pool):
            def touch():
                nc.gpsimd.tensor_tensor(spare[0:1, 0:1], spare[0:1, 1:2], spare[0:1, 1:2], ALU.add)

            def inverse_deviation(g, mv, ve, rs, s_mv, s_ve, s_rs):
                pool.wait_ge(s_mv, g.count(2, 2))
                nc.gpsimd.tensor_tensor(ve[:, :], mv[:, :, 1], eps2[:, :], ALU.add).then_inc(s_ve, 1)
                pool.wait_ge(s_ve, g.count(1, 1))
                nc.gpsimd.tensor_tensor(rs[:, :], ve[:, :], mhalf[:, :], ALU.pow).then_inc(s_rs, 1)

            def rows_plus_constant(g):
                if g.layer == 0:
                    if isinstance(g.u, int) and g.k == 4:
                        pool.wait_ge(x_in1, 16)
                else:
                    pool.wait_ge(comb_done, g.at(2, 2))
                wait(pool, x1_ready, g.count(1, -1))
                nc.gpsimd.tensor_tensor(xc[g.par][:, :, :], x[:, sl(g.at(2), 2), :],
                                        orow[g.layer][:, :].unsqueeze(1).to_broadcast([P, 2, DM]),
                                        ALU.add).then_inc(xc_ready, 1)

            def spread_keys(g):
                pool.wait_ge(k_ready, g.count(1, 1))
                wait(pool, s_done, g.count(4, -4))
                nc.gpsimd.tensor_tensor(Kbd[g.par][:, :, :, :],
                                        kT[g.par][:, :].rearrange("p (b k) -> p b k", b=4).unsqueeze(2).to_broadcast([P, 4, 4, S]),
                                        blk.unsqueeze(1).unsqueeze(3).to_broadcast([P, 4, 4, S]),
                                        ALU.mult).then_inc(kbd_ready, 1)

            def collect_rows(g):
                pool.wait_ge(xn2_ready, g.count(2, 2))
                wait(pool, scattered, g.block(0) * (16 * 8))
                carry(touch, g.block(0))
                for i in range(2):
                    nc.gpsimd.tensor_copy(xs[:, 2 * i:2 * i + 2, :], xn2[i][:, :, :]).then_inc(xs_ready, 1)

            def scatter(g, slot):
                pool.wait_ge(pos_ready, g.block(1))
                pool.wait_ge(xs_ready, g.block(1) * 2)
                carry(touch, g.block(1))
                for t in range(4):
                    nc.gpsimd.indirect_dma_start(lists, bass.IndirectOffsetOnAxis(ap=pos[:, slot, t:t + 1], axis=0),
                                                 xs[:, t, :], None).then_inc(scattered, 16)

            def gather(g):
                i = g.par
                wait(pool, comb_done, g.at(2, -2))
                carry(touch, g.at())
                nc.gpsimd.tensor_copy(gi[i][:, :].rearrange("p (b s t) -> p b s t", b=1, s=2),
                                      place[:, sl(g.block(0)), :].rearrange("p b (s t) -> p b s t", s=2)[:, :, :, 2 * i:2 * i + 2]
                                      ).then_inc(gi_ready, 1)
                pool.wait_ge(gi_ready, g.at(1, 1))
                carry(touch, g.at())
                for s_ in range(2):
                    for t in range(2):
                        c = 2 * s_ + t
                        nc.gpsimd.indirect_dma_start(ysb[i][:, s_, t, :], None, louts,
                                                     bass.IndirectOffsetOnAxis(ap=gi[i][:, c:c + 1], axis=0)
                                                     ).then_inc(gathered[i], 16)

            def step(g):
                if g.plus(-1).real():
                    rows_plus_constant(g.plus(-1))
                if g.layer == 1:
                    if g.plus(3).real():
                        gather(g.plus(3))
                elif g.par:
                    if g.plus(-4).real():
                        scatter(g.plus(-4), 1)
                if g.plus(-2).real():
                    inverse_deviation(g.plus(-2), mvf, vef, rsf, lnf_mv, lnf_ve, lnf_rs)
                if g.plus(1).real():
                    spread_keys(g.plus(1))
                if g.layer == 0:
                    if not g.par and g.plus(-3).real():
                        scatter(g.plus(-3), 0)
                    if g.par and g.plus(-2).real():
                        collect_rows(g.plus(-2))
                if g.plus(2).real():
                    inverse_deviation(g.plus(2), mvq, veq, rsq, lnq_mv, lnq_ve, lnq_rs)

            pool.wait_ge(setup_in, SETUP)
            pool.wait_ge(x_in0, 16)
            pool.wait_ge(orow_done, 2)
            steps(pool, 0, step)
            pool.wait_ge(rows_out[0], 16 * (NT // 2))
            pool.wait_ge(rows_out[1], 16 * (NT // 2))
            pool.wait_ge(place_ready, 1)
            steps(pool, 1, step)

        @block.scalar
        def _(act):
            def copy(dst, src, bias=None):
                if bias is None:
                    return nc.scalar.activation(dst, src, ACT.Copy)
                return nc.scalar.activation(dst, src, ACT.Identity, bias=bias)

            def heads_out(g):
                act.wait_ge(ot_done, g.count(1, 1))
                wait(act, out_done, g.count(1, -1))
                copy(OT[g.par][:, :], bank6[:, 0:GT]).then_inc(ot_ready, 1)

            def tokens_in(g):
                act.wait_ge(xt_done, g.count(1, 1))
                wait(act, kq_done, g.count(2, -2))
                copy(xnT[g.par][:, :], bank7[:, 0:GT]).then_inc(xnT_ready, 1)

            def probs_out(g, c):
                act.wait_ge(pt_done, g.count(4, c + 1))
                wait(act, pv_done, g.count(4, c - 3))
                copy(PT[c][:, :], ps_p[:, c % 2, :]).then_inc(pt_ready, 1)

            def exps(g, q):
                act.wait_ge(sub_done, g.count(4, q + 1))
                nc.scalar.activation(Pr[g.par][:, q, :], Pr[g.par][:, q, :], ACT.Exp,
                                     scale=SCALES[g.layer]).then_inc(exp_done, 1)

            def keys_queries(g):
                act.wait_ge(kq_done, g.count(2, 2))
                wait(act, kbd_ready, g.count(1, -1))
                copy(kT[g.par][:, :], bank7[:, 0:GT], bcol[:, 1:2] if g.layer == 0 else zcol[:, :]).then_inc(k_ready, 1)
                wait(act, s_done, g.count(4, -4))
                copy(qT[g.par][:, :], bank7[:, GT:2 * GT], bcol[:, 0:1] if g.layer == 0 else zcol[:, :]).then_inc(q_ready, 1)

            def tokens2(g):
                act.wait_ge(xt2_done, g.count(1, 1))
                wait(act, lg_done, g.count(1, -1))
                if g.layer == 1:
                    copy(xn3T[:, sl(g.at(GT), GT)], bank7[:, 0:GT])
                copy(xn2T[g.par][:, :], bank7[:, 0:GT]).then_inc(xn2T_ready, 1)

            def step(g):
                if g.plus(-2).real():
                    heads_out(g.plus(-2))
                if g.plus(1).real():
                    tokens_in(g.plus(1))
                for c in range(4):
                    if g.plus(-1).real():
                        probs_out(g.plus(-1), c)
                    if g.real():
                        exps(g, c)
                if g.plus(1).real():
                    keys_queries(g.plus(1))
                if g.plus(-2).real():
                    tokens2(g.plus(-2))

            act.wait_ge(setup_in, SETUP)
            nc.scalar.activation(tg[:, :], gates[:, :], ACT.Tanh).then_inc(tanh_done, 1)
            act.wait_ge(consts_done, 1)
            steps(act, 0, step)

            act.wait_ge(place2, TILES // 4)
            nc.scalar.activation(d_all[:, :, :], d_all[:, :, :], ACT.Exp).then_inc(dexp_done, 1)
            nc.scalar.activation(p2[:, :], m2_all[:, :], ACT.Exp).then_inc(dexp_done, 1)

            def gelu(u, k):
                i = k % 2
                act.wait_ge(w1_ready, at(u, k, 2, 2))
                wait(act, y_done, at(u, k, 1, -1))
                for f in range(FB0):
                    if f % 2 == 0:
                        act.wait_ge(h_done, at(u, k, 2, 1 + f // 2))
                    nc.scalar.activation(hT[i][:, f, :], ps_s[:, 2 * i + f // 2, ET * (f % 2):ET * (f % 2 + 1)],
                                         ACT.Gelu_apprx_tanh, bias=b1s[i][:, f:f + 1]).then_inc(gelu_done, 1)

            gelu(0, 0)
            gelu(0, 1)
            with act.Fori(1, NT // 2) as u:
                gelu(u, 0)
                gelu(u, 1)

            act.wait_ge(rows_out[0], 16 * (NT // 2))
            act.wait_ge(rows_out[1], 16 * (NT // 2))
            steps(act, 1, step)

            act.wait_ge(ent_step, 2)
            nc.scalar.activation(ent2[:, :], ent2[:, :], ACT.Exp, scale=-1.0).then_inc(ent_act, 1)
            act.wait_ge(gates_step, 2)
            nc.scalar.activation(we[:, :, :], we[:, :, :], ACT.Exp).then_inc(gates_act, 1)
            act.wait_ge(ent_act, 1)
            nc.scalar.activation(ent2[:, :], ent2[:, :], ACT.Ln, bias=1.0).then_inc(ent_act, 1)

            def relu(u, k):
                wait(act, y1_done, u * 4 + (k - 1))
                for f in range(FB1):
                    act.wait_ge(h1_done, u * 8 + (2 * k + f + 1))
                    nc.scalar.activation(hD[k % 2][:, f, :], ps_s[:, (2 * k + f) % 4, :], ACT.Relu,
                                         bias=c1[:, (k % 4) * FB1 + f:(k % 4) * FB1 + f + 1]).then_inc(relu_done, 1)

            for k in range(E1):
                relu(0, k)
            with act.Fori(1, TILES // 4) as u:
                for k in range(E1):
                    relu(u, k)

        @block.vector
        def _(dve):
            V = nc.vector

            def touch():
                V.memset(spare_v[:, :], 0.0)

            def flat(ap):
                return ap.rearrange("p a d -> p (a d)")

            def layernorm(g, dst, st, mv, rs, s_st, s_mv, s_rs, s_out):
                carry(touch, g.at())
                tiles = [flat(x[:, sl(g.at(2, j)), :]) for j in range(2)]
                for j in range(2):
                    V.bn_stats(st[:, j, :], tiles[j]).then_inc(s_st, 1)
                dve.wait_ge(s_st, g.count(2, 2))
                carry(touch, g.at())
                for j in range(2):
                    V.bn_aggr(mv[:, j, :], st[:, j, :]).then_inc(s_mv, 1)
                dve.wait_ge(s_rs, g.count(1, 1))
                for j in range(2):
                    V.tensor_scalar(dst[:, j, :], tiles[j], mv[:, j, 0:1], rs[:, j:j + 1],
                                    ALU.subtract, ALU.mult).then_inc(s_out, 1)

            def norm_in(g):
                if g.layer == 0:
                    if isinstance(g.u, int) and g.k in (0, 4):
                        dve.wait_ge(x_in0 if g.k == 0 else x_in1, 16)
                else:
                    dve.wait_ge(comb_done, g.at(2, 2))
                wait(dve, xt_done, g.count(1, -1))
                layernorm(g, xn[g.par], stq, mvq, rsq, lnq_st, lnq_mv, lnq_rs, xn_ready)

            def norm_mid(g):
                wait(dve, xt2_done, g.count(1, -1))
                if g.layer == 0:
                    wait(dve, xs_ready, g.block(0) * 2)
                wait(dve, x1_ready, g.count(1, 1))
                layernorm(g, xn2[g.par], stf, mvf, rsf, lnf_st, lnf_mv, lnf_rs, xn2_ready)

            def residual(g):
                dve.wait_ge(out_done, g.count(1, 1))
                dve.wait_ge(xc_ready, g.count(1, 1))
                V.tensor_tensor(x[:, sl(g.at(2), 2), :], bank6[:, 0:GT].rearrange("p (t d) -> p t d", t=2),
                                xc[g.par][:, :, :], ALU.add).then_inc(x1_ready, 1)

            def less_maximum(g):
                def view(ap):
                    return ap.rearrange("p (h k) -> p h k", k=S)

                def maximum(q):
                    dve.wait_ge(s_done, g.count(4, q + 1))
                    V.tensor_reduce(mx[g.par][:, q, :], view(ps_s[:, q, :]), AX, ALU.max).then_inc(max_done, 1)

                def subtract(q):
                    dve.wait_ge(max_done, g.count(4, q + 1))
                    wait(dve, pv_done, g.count(4, -4))
                    V.tensor_tensor(view(Pr[g.par][:, q, :]), view(ps_s[:, q, :]),
                                    mx[g.par][:, q, :].unsqueeze(2).to_broadcast([P, 8, S]),
                                    ALU.subtract).then_inc(sub_done, 1)

                maximum(0)
                for q in range(1, 4):
                    maximum(q)
                    subtract(q - 1)
                subtract(3)

            def heads(g, pr):
                o = (bank7, bank6)[pr][:, 0:8 * 2 * VW].rearrange("p (j b c) -> p j b c", j=8, b=2)
                dve.wait_ge(pv_done, g.count(4, 2 * pr + 2))
                for b in range(2):
                    r = slice(S * b, S * b + S)
                    V.reciprocal(rden[r, pr, :, :], o[r, :, b, 2 * DK:VW]).then_inc(rec_done, 1)
                dve.wait_ge(rec_done, g.count(4, 2 * pr + 2))
                wait(dve, ot_done, g.count(1, -1))
                for b in range(2):
                    r = slice(S * b, S * b + S)
                    ins = V.tensor_tensor(On[g.par][r, pr, :].rearrange("p (j h d) -> p j h d", j=8, h=2),
                                          o[r, :, b, 0:2 * DK].rearrange("p j (h d) -> p j h d", h=2),
                                          rden[r, pr, :, :].unsqueeze(3).to_broadcast([S, 8, 2, DK]), ALU.mult)
                ins.then_inc(on_ready, 1)

            def values(g):
                dve.wait_ge(v_done, g.count(1, 1))
                wait(dve, pv_done, g.count(4, -4))
                v = bank6.rearrange("p (b j c) -> p b j c", b=4, j=8)
                for i in range(2):
                    r = slice(S * i, S * i + S)
                    c = slice(DK * i, DK * i + DK)
                    ins = V.tensor_copy(Vbd[g.par][r, :, :, c], v[r, :, :, c])
                ins.then_inc(v_ready, 1)

            def router_logits(g):
                dve.wait_ge(lg_done, g.count(1, 1))
                V.tensor_copy(lgb[:, 2 * g.par:2 * g.par + 2, :],
                              bank6[:, 0:2 * E0].rearrange("p (t e) -> p t e", t=2)).then_inc(lg_read, 1)

            ROUTE = 15

            def chain(sem_, start):
                n = [0]

                def link(ins):
                    n[0] += 1
                    ins.then_inc(sem_, 1)
                    dve.wait_ge(sem_, start + n[0])
                return link

            def route_tops(g):
                link = chain(route, g.block(0) * ROUTE)
                desc4 = desc.unsqueeze(1).to_broadcast([P, 4, E0])

                def b4(ap):
                    return ap.unsqueeze(2).to_broadcast([P, 4, E0])

                dve.wait_ge(lg_read, g.count(1, 1))
                link(V.tensor_reduce(m1[:, :], lgb[:, :, :], AX, ALU.max))
                link(V.tensor_tensor(dlt[:, :, :], lgb[:, :, :], b4(m1[:, :]), ALU.subtract))
                link(V.scalar_tensor_tensor(cand[:, :, :], dlt[:, :, :], 0.0, desc4, ALU.is_equal, ALU.mult))
                link(V.tensor_reduce(top[:, :], cand[:, :, :], AX, ALU.max))
                link(V.tensor_tensor(hot[:, 0, :, :], desc4, b4(top[:, :]), ALU.is_equal))
                link(V.scalar_tensor_tensor(dl2[:, :, :], hot[:, 0, :, :], -BIG, dlt[:, :, :], ALU.mult, ALU.add))
                link(V.tensor_reduce(m2[:, :], dl2[:, :, :], AX, ALU.max))
                link(V.tensor_tensor(cand[:, :, :], dl2[:, :, :], b4(m2[:, :]), ALU.is_equal))
                link(V.tensor_tensor(cand[:, :, :], cand[:, :, :], desc4, ALU.mult))
                link(V.tensor_reduce(top[:, :], cand[:, :, :], AX, ALU.max))
                link(V.tensor_tensor(hot[:, 1, :, :], desc4, b4(top[:, :]), ALU.is_equal))
                V.tensor_tensor(hotb[:, :, :], hot[:, 0, :, :], hot[:, 1, :, :], ALU.add).then_inc(hot_ready, 1)
                V.tensor_reduce(hsum[:, :], hot[:, :, :, :].rearrange("p s t e -> p e (s t)"), AX, ALU.add).then_inc(route, 1)
                V.tensor_copy(d_all[:, sl(g.block(0) * 4, 4), :], dlt[:, :, :])
                V.tensor_copy(m2_all[:, sl(g.block(0) * 4, 4)], m2[:, :]).then_inc(place2, 1)

            def route_places(g):
                dve.wait_ge(rk_done, g.block(1))
                V.tensor_tensor(rank[:, :, :], bank6[:, 0:4 * E0].rearrange("p (t e) -> p t e", t=4),
                                base.unsqueeze(1).to_broadcast([P, 4, E0]), ALU.add).then_inc(rank_read, 1)
                dve.wait_ge(route, g.block(0) * ROUTE + 12)
                V.tensor_tensor(seen[:, :], seen[:, :], hsum[:, :], ALU.add).then_inc(route, 1)
                dve.wait_ge(rank_read, g.block(1))
                V.tensor_tensor(rsel[:, :, :, :].rearrange("p s t e -> p s (t e)"),
                                hot[:, :, :, :].rearrange("p s t e -> p s (t e)"),
                                rank[:, :, :].rearrange("p t e -> p (t e)").unsqueeze(1).to_broadcast([P, 2, 4 * E0]),
                                ALU.mult).then_inc(route, 1)
                dve.wait_ge(route, g.block(0) * ROUTE + 14)
                V.tensor_copy(seenb[:, :], seen[:, :]).then_inc(seen_ready, 1)
                V.tensor_reduce(posf[:, :, :], rsel[:, :, :, :], AX, ALU.add).then_inc(route, 1)
                dve.wait_ge(route, g.block(0) * ROUTE + 15)
                wait(dve, scattered, g.block(0) * (16 * 8))
                V.tensor_copy(pos[:, :, :], posf[:, :, :]).then_inc(pos_ready, 1)
                V.tensor_copy(pos_all[:, sl(g.block(0)), :], posf[:, :, :].rearrange("p (b s) t -> p b (s t)", b=1))

            def gate_logits(g):
                lg = bank6[:, 0:2 * (E1 + HD1)].rearrange("p (t e) -> p t e", t=2)
                dve.wait_ge(lg_done, g.count(1, 1))
                V.tensor_tensor(gl[:, sl(g.at(2), 2), :], lg[:, :, 0:E1],
                                gb1[:, :].unsqueeze(1).to_broadcast([P, 2, E1]), ALU.add)
                V.tensor_tensor(t1[:, :, :], lg[:, :, E1:], db1[:, :].unsqueeze(1).to_broadcast([P, 2, HD1]),
                                ALU.add).then_inc(lg_read, 1)
                dve.wait_ge(lg_read, g.count(1, 1))
                V.scalar_tensor_tensor(t2[:, :, :], t1[:, :, :], 0.0, dw2[:, :].unsqueeze(1).to_broadcast([P, 2, HD1]),
                                       ALU.max, ALU.mult).then_inc(gate_step, 1)
                dve.wait_ge(gate_step, g.at(2, 1))
                V.tensor_reduce(z_all[:, sl(g.at(2), 2)], t2[:, :, :], AX, ALU.add).then_inc(gate_step, 1)

            def combine(g):
                dve.wait_ge(gathered[g.par], g.u * 64 + 64 * (g.k // 2 + 1))
                for s_ in range(2):
                    for t in range(2):
                        tile = flat(x[:, sl(g.at(2, t)), :])
                        V.scalar_tensor_tensor(tile, ysb[g.par][:, s_, t, :], flat(w_all[:, sl(g.at(2, t)), s_:s_ + 1]), tile,
                                               ALU.mult, ALU.add).then_inc((comb_step, comb_done)[s_], 1)
                    if s_ == 0:
                        dve.wait_ge(comb_step, g.at(2, 2))

            def step(g):
                if g.layer == 0 and not g.par and g.plus(-3).real():
                    route_places(g.plus(-3))
                if g.plus(-2).real():
                    residual(g.plus(-2))
                if g.real():
                    less_maximum(g)
                if g.plus(-2).real():
                    norm_mid(g.plus(-2))
                if g.plus(-1).real():
                    heads(g.plus(-1), 0)
                    heads(g.plus(-1), 1)
                if g.plus(1).real():
                    values(g.plus(1))
                if g.plus(-2).real():
                    (router_logits, gate_logits)[g.layer](g.plus(-2))
                    if g.layer == 0 and g.par:
                        route_tops(g.plus(-2))
                if g.plus(2).real():
                    if g.layer == 1:
                        combine(g.plus(2))
                    norm_in(g.plus(2))

            for i in range(2):
                V.memset(Vbd[i][:, :, :, :], 0.0)
            V.memset(ones[:, :], 1.0)
            V.memset(zcol[:, :], 0.0)
            V.memset(mhalf[:, :], -0.5)
            V.memset(eps2[:, :], EPS)
            V.memset(spare[:, :], 0.0)
            V.memset(zero[:, :], 0.0)
            V.memset(seen[:, :], 0.0)
            V.memset(seenb[:, :], 0.0)
            V.memset(oneE[:, :], 1.0).then_inc(plan_step, 1)
            dve.wait_ge(plan_step, 1)
            for i in range(2):
                V.memset(Vbd[i][0:S, :, :, 2 * DK:2 * DK + 1], 1.0)
                V.memset(Vbd[i][S:P, :, :, 2 * DK + 1:VW], 1.0)
            dve.wait_ge(setup_in, SETUP)
            V.tensor_copy(tri[:, :], cst[:, C_TRI:C_TRI + P])
            V.tensor_copy(ind[:, :], cst[0:2, C_IND:C_IND + P])
            V.tensor_scalar(negm[:, :, :], maskn, 0, NEG, ALU.is_equal, ALU.mult).then_inc(consts_done, 1)
            dve.wait_ge(tanh_done, 1)
            for i in range(2):
                V.tensor_scalar(wo[i][:, :], wo[i][:, :], tg[:, i:i + 1], None, ALU.mult).then_inc(wo_scaled, 1)
            V.tensor_scalar(orow[1][:, :], bo[1][:, :], tg[:, 1:2], None, ALU.mult).then_inc(orow_done, 1)
            dve.wait_ge(bv_done, 1)
            V.scalar_tensor_tensor(orow[0][:, :], bo[0][:, :], tg[:, 0:1], bank6[:, 0:DM],
                                   ALU.mult, ALU.add).then_inc(orow_done, 1)
            steps(dve, 0, step)

            link = chain(plan_step, 1)
            dve.wait_ge(cnt_done, 1)
            link(V.tensor_copy(cnt[:, :], bank6[:, 0:E0]))
            V.tensor_copy(cnti[:, :], cnt[0:1, :]).then_inc(cnti_ready, 1)
            link(V.tensor_tensor(cge[:, :, :], cnt[:, :].unsqueeze(2).to_broadcast([P, E0, TOK // ET]),
                                 cst[:, C_THR:C_THR + TOK // ET].unsqueeze(1).to_broadcast([P, E0, TOK // ET]), ALU.is_gt))
            link(V.tensor_reduce(ntl[:, :], cge[:, :, :], AX, ALU.add))
            link(V.tensor_tensor_scan(nend[:, :], oneE[:, :], ntl[0:1, :], 0.0, ALU.mult, ALU.add))
            link(V.tensor_scalar(nend[:, :], nend[:, :], float(ET), None, ALU.mult))
            link(V.tensor_scalar(jump[:, :], ntl[:, :], -float(ET), float(RE), ALU.mult, ALU.add))
            rows = cst[0:1, C_ROW:C_ROW + NT]
            link(V.tensor_tensor(tge[:, :, :], rows.unsqueeze(2).to_broadcast([1, NT, E0 - 1]),
                                 nend[:, 0:E0 - 1].unsqueeze(1).to_broadcast([1, NT, E0 - 1]), ALU.is_ge))
            link(V.tensor_tensor(tjump[:, :, :], tge[:, :, :],
                                 jump[0:1, 0:E0 - 1].unsqueeze(1).to_broadcast([1, NT, E0 - 1]), ALU.mult))
            link(V.tensor_reduce(tef[:, :], tge[:, :, :], AX, ALU.add))
            link(V.tensor_reduce(trf[:, :], tjump[:, :, :], AX, ALU.add))
            link(V.tensor_tensor(trf[:, :], trf[:, :], rows, ALU.add))
            link(V.tensor_copy(tei[:, :], tef[:, :]))
            V.tensor_copy(tri_row[:, :], trf[:, :]).then_inc(plan_ready, 1)

            link = chain(move_step, 0)
            link(V.tensor_copy(place[:, :, :], pos_all[:, :, :]))
            for e in range(1, E0):
                link(V.tensor_scalar(moved[:, :, :], pos_all[:, :, :], float(e * RE), jump[:, e - 1:e], ALU.is_ge, ALU.mult))
                link(V.tensor_tensor(place[:, :, :], place[:, :, :], moved[:, :, :], ALU.subtract))
            V.tensor_copy(place[:, :, :], place[:, :, :]).then_inc(place_ready, 1)

            link = chain(w_step, 0)
            dve.wait_ge(dexp_done, 2)
            link(V.tensor_reduce(den[:, :], d_all[:, :, :], AX, ALU.add))
            link(V.reciprocal(ent[:, :], den[:, :]))
            link(V.tensor_tensor(p2[:, :], p2[:, :], ent[:, :], ALU.mult))
            link(V.scalar_tensor_tensor(den[:, :], ent[:, :], 1e-8, p2[:, :], ALU.add, ALU.add))
            link(V.reciprocal(den[:, :], den[:, :]))
            V.scalar_tensor_tensor(w_all[:, :, 0], ent[:, :], tg[:, 2:3], den[:, :], ALU.mult, ALU.mult)
            V.scalar_tensor_tensor(w_all[:, :, 1], p2[:, :], tg[:, 2:3], den[:, :], ALU.mult, ALU.mult).then_inc(w_ready, 1)

            def expert_of(u, k):
                return dve.value_load(tei[0:1, sl(at(u, k))], min_val=0, max_val=E0 - 1)

            def stage_w1(u, k):
                i = k % 2
                e = expert_of(u, k)
                wait(dve, gelu_done, at(u, k, FB0, -FB0))
                V.tensor_copy(w1s[i], w1a[:, bass.ds(e * F0, F0)]).then_inc(w1_ready, 1)
                V.tensor_copy(b1s[i][:, :], b1a[:, bass.ds(e * FB0, FB0)]).then_inc(w1_ready, 1)

            def stage_w2(u, k):
                e = expert_of(u, k)
                wait(dve, y_done, at(u, k, 1, -1))
                V.tensor_copy(w2s[k % 2], w2a[:, bass.ds(e * F0, F0)]).then_inc(w2_ready, 1)

            def rows_turned(u, k):
                dve.wait_ge(et_done, at(u, k, 1, 1))
                wait(dve, h_done, at(u, k, 2, -2))
                V.tensor_copy(xinT[k % 2], ps_p[:, k % 2, 0:ET]).then_inc(xinT_ready, 1)

            def rows_made(u, k):
                i = k % 2
                e = expert_of(u, k)
                dve.wait_ge(y_done, at(u, k, 1, 1))
                wait(dve, rows_out[i], u * 16 + 16 * (k // 2))
                V.tensor_tensor(yo[i], ps_m[:, i, 0:ET].rearrange("p (t d) -> p t d", t=2),
                                b2a[:, bass.ds(e, 1), :].to_broadcast([P, 2, DM]), ALU.add).then_inc(yo_ready, 1)

            def tile_step(u, k, first=False, more=True):
                if more:
                    stage_w1(u, k + 1)
                    rows_turned(u, k + 1)
                if not first:
                    rows_made(u, k - 1)
                if more:
                    stage_w2(u, k + 1)

            dve.wait_ge(experts_in, 16 * 8)
            tile_step(0, -1, first=True)
            tile_step(0, 0, first=True)
            with dve.Fori(0, NT // 2 - 1) as u:
                tile_step(u, 1)
                tile_step(u, 2)
            tile_step(0, NT - 1, more=False)
            tile_step(0, NT, more=False)

            steps(dve, 1, step)

            link = chain(ent_step, 0)
            dve.wait_ge(gate_step, 2 * GROUPS)
            link(V.tensor_scalar(ent[:, :], z_all[:, :], db2[:, 0:1], None, ALU.add))
            link(V.scalar_tensor_tensor(ent2[:, :], ent[:, :], -1.0, ent[:, :], ALU.mult, ALU.max))
            link = chain(gates_step, 0)

            def be(ap):
                return ap.unsqueeze(2).to_broadcast([P, TILES, E1])

            link(V.tensor_reduce(gmx[:, :], gl[:, :, :], AX, ALU.max))
            link(V.tensor_tensor(we[:, :, :], gl[:, :, :], be(gmx[:, :]), ALU.subtract))
            other = gl[:, :, :].unsqueeze(2).to_broadcast([P, TILES, E1, E1])
            own = gl[:, :, :].unsqueeze(3).to_broadcast([P, TILES, E1, E1])
            tie = cst[:, C_TIE:C_ALL].unsqueeze(1).to_broadcast([P, TILES, E1 * E1])
            link(V.tensor_tensor(big[0], other, own, ALU.is_gt))
            link(V.tensor_tensor(big[1], other, own, ALU.is_equal))
            flat1 = big[1].rearrange("p t e f -> p t (e f)")
            link(V.tensor_tensor(flat1, flat1, tie, ALU.mult))
            link(V.tensor_tensor(big[0], big[0], big[1], ALU.add))
            link(V.tensor_reduce(sel, big[0], AX, ALU.add))
            dve.wait_ge(ent_act, 2)
            link(V.scalar_tensor_tensor(ent[:, :], ent[:, :], 0.0, ent2[:, :], ALU.max, ALU.add))
            link(V.tensor_scalar(kt[:, :], ent[:, :], 0.5, 1 / 1.5, ALU.subtract, ALU.mult))
            link(V.tensor_scalar(kt[:, :], kt[:, :], 0.0, 1.0, ALU.max, ALU.min))
            link(V.tensor_scalar(kt[:, :], kt[:, :], float(E1 - 1), 1.0, ALU.mult, ALU.add))
            link(V.tensor_scalar(kt[:, :], kt[:, :], ROUND, None, ALU.add))
            link(V.tensor_scalar(kt[:, :], kt[:, :], ROUND, None, ALU.subtract))
            link(V.tensor_tensor(sel, sel, be(kt[:, :]), ALU.is_lt))
            dve.wait_ge(gates_act, 1)
            link(V.tensor_tensor(we[:, :, :], we[:, :, :], sel, ALU.mult))
            link(V.tensor_reduce(gmx[:, :], we[:, :, :], AX, ALU.add))
            link(V.reciprocal(gmx[:, :], gmx[:, :]))
            link(V.tensor_tensor(we[:, :, :], we[:, :, :], be(gmx[:, :]), ALU.mult))
            V.tensor_scalar(we[:, :, :], we[:, :, :], tg[:, 3:4], None, ALU.mult).then_inc(gates_ready, 1)
            dve.wait_ge(gates_ready, 1)

            def add_expert(u, e):
                wait(dve, acc_y, u * 16 + 4 * e)
                for t in range(4):
                    tile = flat(x[:, sl(u * 4 + t), :])
                    V.scalar_tensor_tensor(tile, c2[:, e, :], flat(we[:, sl(u * 4 + t), e:e + 1]), tile,
                                           ALU.mult, ALU.add).then_inc(acc_b, 1)
                dve.wait_ge(y1_done, u * 4 + (e + 1))
                for t in range(4):
                    tile = flat(x[:, sl(u * 4 + t), :])
                    dve.wait_ge(acc_b, u * 16 + (4 * e + t + 1))
                    V.scalar_tensor_tensor(tile, ps_p[:, e % 2, DM * t:DM * (t + 1)], flat(we[:, sl(u * 4 + t), e:e + 1]), tile,
                                           ALU.mult, ALU.add).then_inc(acc_y, 1)

            with dve.Fori(0, TILES // 4) as u:
                for e in range(E1):
                    add_expert(u, e)

        @block.tensor
        def _(pe):
            mm, turn = nc.tensor.matmul, nc.tensor.transpose

            def heads_turned(g):
                bank_free(pe, 6, g.plus(2), "OT")
                pe.wait_ge(on_ready, g.count(2, 2))
                for t in range(2):
                    ins = turn(bank6[:, P * t:P * t + P], On[g.par][:, t, :], ident)
                ins.then_inc(ot_done, 1)

            def scores(g):
                pe.wait_ge(q_ready, g.count(1, 1))
                pe.wait_ge(kbd_ready, g.count(1, 1))
                wait(pe, sub_done, g.count(4, 0))
                if g.layer == 1:
                    for q in range(4):
                        mm(ps_s[:, q, :].rearrange("p (t h k) -> p t h k", t=2, h=4), ind[:, :],
                           negm[:, sl(g.at(2), 2), :].unsqueeze(2).to_broadcast([2, 2, 4, S]),
                           start=True, stop=False, skip_group_check=True)
                for b in range(4):
                    for q in range(4):
                        r = slice(32 * q, 32 * q + 32)
                        ins = mm(ps_s[S * (b % 2):S * (b % 2) + S, q, GT * (b // 2):GT * (b // 2) + GT],
                                 qT[g.par][r, S * b:S * b + S], Kbd[g.par][r, b, :, :].rearrange("p h k -> p (h k)"),
                                 start=(g.layer == 0), stop=True, skip_group_check=True)
                        if b == 3:
                            ins.then_inc(s_done, 1)

            def tokens_turned(g):
                bank_free(pe, 7, g.plus(-1), "XT")
                pe.wait_ge(xn_ready, g.count(2, 2))
                for t in range(2):
                    ins = turn(bank7[:, P * t:P * t + P], xn[g.par][:, t, :], ident)
                ins.then_inc(xt_done, 1)

            def project_out(g):
                bank_free(pe, 6, g.plus(2), "OUT")
                pe.wait_ge(ot_ready, g.count(1, 1))
                for t in range(2):
                    ins = mm(bank6[:, P * t:P * t + P], OT[g.par][:, P * t:P * t + P], wo[g.layer][:, :], start=True, stop=True)
                ins.then_inc(out_done, 1)

            def probs_turned(g, c):
                pr, half = c // 2, c % 2
                pe.wait_ge(exp_done, g.count(4, 2 * half + 2))
                wait(pe, pt_ready, g.count(4, c - 1))
                for i in range(4):
                    j = 4 * half + i
                    col = GT * pr + P * (j % 2)
                    ins = turn(ps_p[:, c % 2, P * i:P * i + P], Pr[g.par][:, j // 2, col:col + P], ident)
                ins.then_inc(pt_done, 1)

            def probs_by_values(g, c):
                pr, half = c // 2, c % 2
                if half == 0:
                    bank_free(pe, 6 if pr else 7, g.plus(1), f"O{pr}")
                pe.wait_ge(pt_ready, g.count(4, c + 1))
                pe.wait_ge(v_ready, g.count(1, 1))
                for i in range(4):
                    j = 4 * half + i
                    ins = mm((bank7, bank6)[pr][:, 2 * VW * j:2 * VW * (j + 1)].rearrange("p (b c) -> p b c", b=2),
                             PT[c][:, P * i:P * i + P], Vbd[g.par][:, 2 * pr:2 * pr + 2, j, :], start=True, stop=True)
                ins.then_inc(pv_done, 1)

            def keys_queries(g):
                bank_free(pe, 7, g.plus(-1), "KQ")
                pe.wait_ge(ctx_in[g.par], g.half_count())
                mm(bank7[:, 0:GT], wk[g.layer][:, :], ctxg[g.par][:, :, 0, :], start=True, stop=True).then_inc(kq_done, 1)
                pe.wait_ge(xnT_ready, g.count(1, 1))
                mm(bank7[:, GT:2 * GT], wq[g.layer][:, :], xnT[g.par][:, :], start=True, stop=True).then_inc(kq_done, 1)

            def values(g):
                bank_free(pe, 6, g.plus(-1), "V")
                for b in range(4):
                    ins = mm(bank6[:, P * b:P * b + P],
                             ctxg[g.par][:, b, :, :].rearrange("p i k -> p (i k)"), wv[g.layer][:, :],
                             start=True, stop=True)
                ins.then_inc(v_done, 1)

            def tokens2_turned(g):
                bank_free(pe, 7, g.plus(2), "XT2")
                pe.wait_ge(xn2_ready, g.count(2, 2))
                for t in range(2):
                    ins = turn(bank7[:, P * t:P * t + P], xn2[g.par][:, t, :], ident)
                ins.then_inc(xt2_done, 1)

            def logits(g):
                bank_free(pe, 6, g.plus(2), "LG")
                pe.wait_ge(xn2T_ready, g.count(1, 1))
                w = (wr0, wr1)[g.layer]
                n = w.shape[1]
                for t in range(2):
                    ins = mm(bank6[:, n * t:n * t + n], xn2T[g.par][:, P * t:P * t + P], w[:, :], start=True, stop=True)
                ins.then_inc(lg_done, 1)

            def ranks(g):
                bank_free(pe, 6, g.plus(2), "RK")
                pe.wait_ge(hot_ready, g.block(1))
                wait(pe, seen_ready, g.block(0))
                o = bank6[:, 0:4 * E0].rearrange("p (t e) -> p t e", t=4)
                mm(o, tri[:, :], hotb[:, :, :], start=True, stop=False, skip_group_check=True)
                for i in range(1, 4):
                    mm(o[:, i:, :], ones[:, :], hotb[:, 0:4 - i, :], start=False, stop=False, skip_group_check=True)
                mm(o, ones[:, :], seenb[:, :].unsqueeze(1).to_broadcast([P, 4, E0]), start=False, stop=True,
                   skip_group_check=True).then_inc(rk_done, 1)

            def step(g):
                if g.plus(-2).real():
                    heads_turned(g.plus(-2))
                if g.real():
                    scores(g)
                if g.plus(1).real():
                    tokens_turned(g.plus(1))
                if g.plus(-2).real():
                    project_out(g.plus(-2))
                if g.plus(-1).real():
                    p = g.plus(-1)
                    probs_turned(p, 0)
                    probs_turned(p, 1)
                    probs_by_values(p, 0)
                    probs_turned(p, 2)
                    probs_by_values(p, 1)
                    probs_turned(p, 3)
                    probs_by_values(p, 2)
                    probs_by_values(p, 3)
                if g.plus(1).real():
                    keys_queries(g.plus(1))
                    values(g.plus(1))
                if g.plus(-2).real():
                    tokens2_turned(g.plus(-2))
                    logits(g.plus(-2))
                    if g.layer == 0 and g.par:
                        ranks(g.plus(-2))

            pe.wait_ge(setup_in, SETUP)
            pe.wait_ge(wo_scaled, 2)
            mm(bank6[:, 0:DM], bcol[:, 2:3].to_broadcast([P, P]), wo[0][:, :], start=True, stop=True).then_inc(bv_done, 1)
            pe.wait_ge(orow_done, 2)
            pe.wait_ge(consts_done, 1)
            steps(pe, 0, step)
            pe.wait_ge(seen_ready, TILES // 4)
            mm(bank6[:, 0:E0], ones[:, :], seenb[:, :], start=True, stop=True).then_inc(cnt_done, 1)

            def rows_turned(u, k):
                i = k % 2
                pe.wait_ge(rows_in[i], u * 16 + 16 * (k // 2 + 1))
                wait(pe, xinT_ready, at(u, k, 1, -1))
                for t in range(2):
                    ins = turn(ps_p[:, i, P * t:P * t + P], xin[i][:, t, :], ident)
                ins.then_inc(et_done, 1)

            def hidden(u, k):
                i = k % 2
                pe.wait_ge(w1_ready, at(u, k, 2, 2))
                pe.wait_ge(xinT_ready, at(u, k, 1, 1))
                wait(pe, gelu_done, at(u, k, FB0, -FB0))
                for f in range(FB0):
                    ins = mm(ps_s[:, 2 * i + f // 2, ET * (f % 2):ET * (f % 2 + 1)], w1s[i][:, P * f:P * f + P], xinT[i],
                             start=True, stop=True)
                    if f % 2:
                        ins.then_inc(h_done, 1)

            def rows_made(u, k):
                i = k % 2
                pe.wait_ge(w2_ready, at(u, k, 1, 1))
                pe.wait_ge(gelu_done, at(u, k, FB0, FB0))
                wait(pe, yo_ready, at(u, k, 1, -1))
                for t in range(2):
                    for f in range(FB0):
                        ins = mm(ps_m[:, i, P * t:P * t + P], hT[i][:, f, P * t:P * t + P], w2s[i][:, P * f:P * f + P],
                                 start=(f == 0), stop=(f == FB0 - 1))
                ins.then_inc(y_done, 1)

            def tile_step(u, k):
                pe_first = isinstance(u, int)
                if not pe_first or k + 1 < NT:
                    rows_turned(u, k + 1)
                if not pe_first or 0 <= k < NT:
                    hidden(u, k)
                if not pe_first or k >= 1:
                    rows_made(u, k - 1)

            pe.wait_ge(cnti_ready, 1)
            pe.wait_ge(xn2T_ready, GROUPS)
            for k in range(-1, 3):
                tile_step(0, k)
            with pe.Fori(1, NT // 2 - 1) as u:
                tile_step(u, 1)
                tile_step(u, 2)
            tile_step(0, NT - 1)
            tile_step(0, NT)

            pe.wait_ge(yo_ready, NT)
            steps(pe, 1, step)

            def hidden1(u, k):
                e = k % E1
                for f in range(FB1):
                    n = 2 * k + f
                    wait(pe, relu_done, u * 8 + (n - 3))
                    mm(ps_s[:, n % 4, :], v1[:, F1 * e + P * f:F1 * e + P * f + P],
                       xn3T[:, sl(u * 512 + 512 * (k // E1), 512)], start=True, stop=True).then_inc(h1_done, 1)

            def rows1(u, k):
                e = k % E1
                pe.wait_ge(relu_done, u * 8 + (2 * k + 2))
                wait(pe, acc_y, u * 16 + 4 * (k - 1))
                for t in range(4):
                    for f in range(FB1):
                        c = (e * FB1 + f) * P
                        ins = mm(ps_p[:, k % 2, P * t:P * t + P], hD[k % 2][:, f, P * t:P * t + P], v2[:, c:c + P],
                                 start=(f == 0), stop=(f == FB1 - 1))
                ins.then_inc(y1_done, 1)

            pe.wait_ge(xn2T_ready, 2 * GROUPS)
            pe.wait_ge(gate_step, 2 * GROUPS)
            hidden1(0, 0)
            for k in range(1, E1 + 1):
                hidden1(0, k)
                rows1(0, k - 1)
            with pe.Fori(1, TILES // 4 - 1) as u:
                for k in range(1, E1 + 1):
                    hidden1(u, k)
                    rows1(u, k - 1)
            for k in range(1, E1):
                hidden1(TILES // 4 - 1, k)
                rows1(TILES // 4 - 1, k - 1)
            rows1(TILES // 4 - 1, E1 - 1)


def kernel(**inputs):
    import concourse.bacc as bacc
    from concourse.bass_utils import run_bass_kernel_spmd

    f = {n: np.ascontiguousarray(v) for n, v in inputs.items()}

    def blocks(w):
        d = np.zeros((DM, DM), np.float32)
        for h in range(H):
            d[h * DK:(h + 1) * DK, h * DK:(h + 1) * DK] = w.T
        return d

    arrays = {n: f[n] for n in ("L0_xattn_Wq", "L0_xattn_Wk", "L0_xattn_Wv", "L0_xattn_Wo", "L0_xattn_bo", "L1_xattn_bo",
                                "L0_ffn_W1", "L0_ffn_W2", "L1_ffn_gate_b", "L1_ffn_dp_b1", "L1_ffn_dp_b2",
                                "L1_ffn_ew1", "L1_ffn_ew2")}
    arrays |= {
        "x": f["x"].reshape(TOK, DM),
        "ctxT": np.broadcast_to(f["ctx_1024"].transpose(2, 0, 1)[:, :, None, :], (DM, B, 2, S)).reshape(DM, 2 * TOK),
        "mask": f["mask_Bx1x1xS2_if1"].reshape(B, S),
        "consts": constants(),
        "bcol": np.stack([f["L0_xattn_bq"], f["L0_xattn_bk"], f["L0_xattn_bv"]], 1),
        "gates": np.concatenate([f["g_xattn"], f["g_ffn"]]),
        "wq1": blocks(f["L1_xattn_Wq"]), "wk1": blocks(f["L1_xattn_Wk"]), "wv1": blocks(f["L1_xattn_Wv"]),
        "wo1": f["L1_xattn_Wo"].T,
        "wr0": f["L0_ffn_router_w"].T,
        "wr1": np.concatenate([f["L1_ffn_gate_w"], f["L1_ffn_dp_w1"]], 1),
        "dw2": f["L1_ffn_dp_w2"].reshape(-1),
        "b1a": f["L0_ffn_b1"].reshape(E0 * FB0, P).T,
        "b2a": f["L0_ffn_b2"].reshape(-1),
        "c1": f["L1_ffn_eb1"].reshape(E1 * FB1, P).T,
        "c2": f["L1_ffn_eb2"].reshape(-1),
    }
    arrays = {n: np.ascontiguousarray(v) for n, v in arrays.items()}
    nc = bacc.Bacc("TRN2", target_bir_lowering=False, num_devices=1)
    ins = {n: nc.dram_tensor(f"in_{n}", v.shape, mybir.dt.from_np(v.dtype), kind="ExternalInput").ap()
           for n, v in arrays.items()}
    out = nc.dram_tensor("out", (TOK, DM), F32, kind="ExternalOutput").ap()
    build(nc, ins, out)
    r = run_bass_kernel_spmd(nc, [{f"in_{n}": v for n, v in arrays.items()}], core_ids=[0])
    return r.results[0]["out"].reshape(B, S, DM)
```

```python
import numpy as np
import concourse.bass as bass
from concourse import mybir
from contextlib import ExitStack

F32 = mybir.dt.float32
BF16 = mybir.dt.bfloat16
I32 = mybir.dt.int32
ALU = mybir.AluOpType
ACT = mybir.ActivationFunctionType
AX = mybir.AxisListType.X

P = 128
B, S, DM = 128, 64, 128
H, DK = 16, 8
TOK = B * S
TILES = TOK // P
GROUPS = TILES // 2
GT = 2 * P
VW = 2 * DK + 2
E0, F0 = 8, 512
FB0 = F0 // P
E1, F1 = 4, 256
FB1 = F1 // P
HD1 = DM // 2
ET = 256
NT = 2 * TOK // ET + E0
RE = TOK + ET * (E0 + 1)
EPS = 1e-5
BIG = 3e38
NEG = -1e20
SCALES = (DK ** -0.5, DM ** -0.5)
ROUND = 12582912.0

C_ID, C_TRI, C_IND = 0, 128, 256
C_BLK = 384
C_QUAD = C_BLK + 4
C_DESC = C_QUAD + 4
C_BASE = C_DESC + E0
C_ROW = C_BASE + E0
C_THR = C_ROW + NT
C_TIE = C_THR + TOK // ET
C_ALL = C_TIE + E1 * E1


def constants():
    c = np.zeros((P, C_ALL), np.float32)
    c[:, C_ID:C_ID + P] = np.eye(P)
    c[:, C_TRI:C_TRI + P] = np.triu(np.ones((P, P)), 1)
    c[0, C_IND:C_IND + S] = 1
    c[1, C_IND + S:C_IND + P] = 1
    for i in range(4):
        c[:, C_BLK + i] = (np.arange(P) % 32) // DK == i
        c[32 * i:32 * i + 32, C_QUAD + i] = 1
    c[:, C_DESC:C_DESC + E0] = E0 - np.arange(E0)
    c[:, C_BASE:C_BASE + E0] = RE * np.arange(E0)
    c[:, C_ROW:C_ROW + NT] = ET * np.arange(NT)
    c[:, C_THR:C_THR + TOK // ET] = ET * np.arange(TOK // ET)
    c[:, C_TIE:C_ALL] = np.tril(np.ones((E1, E1)), -1).reshape(-1)
    return c


def at(u, k, mult=1, add=0, per=2):
    if isinstance(u, int):
        return mult * (per * u + k) + add
    return u * (per * mult) + (mult * k + add)


SETUP = 16 * 20
LOOP0, LOOP1 = 6, GROUPS - 4


def carry(touch, value):
    if not isinstance(value, int):
        touch()


class Group:

    def __init__(self, u, k, layer):
        self.u, self.k, self.layer, self.par = u, k, layer, k % 2

    def plus(self, d):
        return Group(self.u, self.k + d, self.layer)

    def real(self):
        return not isinstance(self.u, int) or 0 <= self.k < GROUPS

    def at(self, mult=1, add=0):
        return at(self.u, self.k, mult, add)

    def count(self, mult=1, add=0):
        return at(self.u, self.k, mult, add + mult * GROUPS * self.layer)

    def half_count(self):
        return self.u * 16 + 16 * (self.k // 2 + 1 + GROUPS // 2 * self.layer)

    def block(self, add=0):
        return self.u + (self.k // 2 + add)


def ln_step(g):
    return at(g.u, g.k, 1, 3 + g.layer * (GROUPS + 4))


def wait(eng, sem, value):
    if not isinstance(value, int) or value > 0:
        eng.wait_ge(sem, value)


def build(nc, A, out):
    with ExitStack() as ctx:
        def sb(name, shape, dt=F32):
            return ctx.enter_context(nc.sbuf_tensor(name, shape, dt))

        def sem(name):
            return ctx.enter_context(nc.semaphore(name))

        ps_s = ctx.enter_context(nc.psum_tensor("ps_s", [P, 4, 512], F32))
        ps_p = ctx.enter_context(nc.psum_tensor("ps_p", [P, 2, 512], F32))
        ps_m = ctx.enter_context(nc.psum_tensor("ps_m", [P, 2, 512], F32))

        x = sb("x", [P, TILES, DM])
        xn3T = sb("xn3T", [P, TOK])
        cst = sb("cst", [P, C_ALL])
        tri = sb("tri", [P, P], BF16)
        ones = sb("ones", [P, P], BF16)
        ind = sb("ind", [2, P], BF16)
        negm = sb("negm", [2, TILES, S], BF16)
        wq = [sb(f"wq{i}", [P, DM]) for i in range(2)]
        wk = [sb(f"wk{i}", [P, DM]) for i in range(2)]
        wv = [sb(f"wv{i}", [P, DM]) for i in range(2)]
        wo = [sb(f"wo{i}", [P, DM]) for i in range(2)]
        bcol = sb("bcol", [P, 3])
        bo = [sb(f"bo{i}", [P, DM]) for i in range(2)]
        orow = [sb(f"orow{i}", [P, DM]) for i in range(2)]
        gates = sb("gates", [P, 4])
        tg = sb("tg", [P, 4])
        wr0 = sb("wr0", [P, E0])
        wr1 = sb("wr1", [P, E1 + HD1])
        gb1 = sb("gb1", [P, E1])
        db1 = sb("db1", [P, HD1])
        dw2 = sb("dw2", [P, HD1])
        db2 = sb("db2", [P, 1])
        w1a = sb("w1a", [P, E0 * F0])
        w2a = sb("w2a", [P, E0 * F0])
        b1a = sb("b1a", [P, E0 * FB0])
        b2a = sb("b2a", [P, E0, DM])
        v1 = sb("v1", [P, E1 * F1])
        v2 = sb("v2", [P, E1 * F1])
        c1 = sb("c1", [P, E1 * FB1])
        c2 = sb("c2", [P, E1, DM])
        ctxg = [sb(f"ctxg{i}", [P, 4, 2, S]) for i in range(2)]
        xn = [sb(f"xn{i}", [P, 2, DM]) for i in range(2)]
        xnT = [sb(f"xnT{i}", [P, GT]) for i in range(2)]
        qT = [sb(f"qT{i}", [P, 4, GT]) for i in range(2)]
        kq = sb("kq", [P, 2, GT])
        Kbd = [sb(f"Kbd{i}", [P, 4, 4, S]) for i in range(2)]
        Vbd = [sb(f"Vbd{i}", [P, 4, 8, VW]) for i in range(2)]
        Pr = [sb(f"Pr{i}", [P, 4, 512]) for i in range(2)]
        mx = [sb(f"mx{i}", [P, 4, 8]) for i in range(2)]
        PT = [sb(f"PT{i}", [P, 512]) for i in range(4)]
        rden = sb("rden", [P, 2, 8, 2])
        On = [sb(f"On{i}", [P, 2, DM]) for i in range(2)]
        OT = [sb(f"OT{i}", [P, GT]) for i in range(2)]
        xc = [sb(f"xc{i}", [P, 2, DM]) for i in range(2)]
        xn2 = [sb(f"xn2{i}", [P, 2, DM]) for i in range(2)]
        xn2T = [sb(f"xn2T{i}", [P, GT]) for i in range(2)]
        st, mv, ve, rs = sb("st", [P, 4, 6]), sb("mv", [P, 4, 2]), sb("ve", [P, 4]), sb("rs", [P, 4])
        mhalf, eps4, spare, spare_v = sb("mhalf", [P, 4]), sb("eps4", [P, 4]), sb("spare", [1, 5]), sb("spare_v", [1, 4])
        lgb = sb("lgb", [P, 4, E0])
        m1 = sb("m1", [P, 4])
        dlt = sb("dlt", [P, 4, E0])
        cand = sb("cand", [P, 4, E0])
        top = sb("top", [P, 4])
        hot = sb("hot", [P, 2, 4, E0])
        dl2 = sb("dl2", [P, 4, E0])
        m2 = sb("m2", [P, 4])
        hotb = sb("hotb", [P, 4, E0], BF16)
        seen = sb("seen", [P, E0])
        seenb = sb("seenb", [P, E0], BF16)
        hsum = sb("hsum", [P, E0])
        rank = sb("rank", [P, 4, E0])
        rsel = sb("rsel", [P, 2, 4, E0])
        posf = sb("posf", [P, 2, 4])
        pos = sb("pos", [P, 2, 4], I32)
        pos_all = sb("pos_all", [P, TILES // 4, 8])
        place = sb("place", [P, TILES // 4, 8], I32)
        d_all = sb("d_all", [P, TILES, E0])
        m2_all = sb("m2_all", [P, TILES])
        xs = sb("xs", [P, 4, DM])
        w_all = sb("w_all", [P, TILES, 2])
        p2 = sb("p2", [P, TILES])
        den = sb("den", [P, TILES])
        cnt = sb("cnt", [P, E0])
        cnti = sb("cnti", [1, E0], I32)
        ntl = sb("ntl", [P, E0])
        nend = sb("nend", [1, E0])
        oneE = sb("oneE", [1, E0])
        jump = sb("jump", [P, E0])
        moved = Pr[1][:, 0, 0:2 * TILES].rearrange("p (b n) -> p b n", n=8)
        cge = Pr[0][:, 2, 0:E0 * TOK // ET].rearrange("p (e n) -> p e n", e=E0)
        tge, tjump = (Pr[0][0:1, i, 0:NT * (E0 - 1)].rearrange("p (n e) -> p n e", e=E0 - 1) for i in range(2))
        tef = sb("tef", [1, NT])
        trf = sb("trf", [1, NT])
        tei = sb("tei", [1, NT], I32)
        tri_row = sb("tri_row", [1, NT], I32)
        zero = sb("zero", [P, ET])
        def late(col, n):
            return xn3T[:, col:col + n]

        w1s = [late(F0 * i, F0) for i in range(2)]
        w2s = [late(2 * F0 + F0 * i, F0) for i in range(2)]
        hT = [late(4 * F0 + FB0 * ET * i, FB0 * ET).rearrange("p (f t) -> p f t", f=FB0) for i in range(2)]
        EX = 4 * F0 + 2 * FB0 * ET
        xin = [late(EX + ET * i, ET).rearrange("p (t d) -> p t d", t=2) for i in range(4)]
        xinT = [late(EX + 4 * ET + ET * i, ET) for i in range(2)]
        yo = [late(EX + 6 * ET + ET * i, ET).rearrange("p (t d) -> p t d", t=2) for i in range(2)]
        maskn = xn3T[0:2, 0:TILES * S].bitcast(I32).rearrange("b (t k) -> b t k", t=TILES)
        b1s = [sb(f"b1s{i}", [P, FB0]) for i in range(2)]
        ysb = [w1a[:, 2 * GT * i:2 * GT * (i + 1)].rearrange("p (s t d) -> p s t d", s=2, t=2) for i in range(2)]
        gi = [sb(f"gi{i}", [P, 4], I32) for i in range(2)]
        t1 = sb("t1", [P, 2, HD1])
        t2 = sb("t2", [P, 2, HD1])
        z_all = sb("z_all", [P, TILES])
        gl = sb("gl", [P, TILES, E1])
        big = [Pr[i][:, 0:2, :].rearrange("p a (t e f) -> p (a t) e f", e=E1, f=E1) for i in range(2)]
        sel = Pr[0][:, 2, 0:TILES * E1].rearrange("p (t e) -> p t e", e=E1)
        we = sb("we", [P, TILES, E1])
        ent, ent2, gmx, kt = (sb(n, [P, TILES]) for n in ("ent", "ent2", "gmx", "kt"))
        hD = [Kbd[i][:, :, :, :].rearrange("p a b k -> p (a b k)").rearrange("p (f t) -> p f t", f=FB1)
              for i in range(2)]

        lists = nc.dram_tensor("lists", [E0 * RE, DM], F32, kind="Internal").ap()
        louts = nc.dram_tensor("louts", [NT * ET, DM], F32, kind="Internal").ap()

        ident = cst[:, C_ID:C_ID + P]
        blk, quad = cst[:, C_BLK:C_BLK + 4], cst[:, C_QUAD:C_QUAD + 4]
        desc = cst[:, C_DESC:C_DESC + E0]
        base = cst[:, C_BASE:C_BASE + E0]
        bank6, bank7 = ps_m[:, 0, :], ps_m[:, 1, :]
        kq_bank, v_bank = ps_s[:, 1, :], ps_s[:, 3, :]

        setup_in, x_in0, x_in1, experts_in, mask_in = (sem(n) for n in (
            "setup_in", "x_in0", "x_in1", "experts_in", "mask_in"))
        ctx_in = [sem("ctx_in0"), sem("ctx_in1")]
        tanh_done, consts_done, wo_scaled, bv_done, orow_done = (sem(n) for n in (
            "tanh_done", "consts_done", "wo_scaled", "bv_done", "orow_done"))
        lnq_st, lnq_mv, xn_ready = (sem(n) for n in ("lnq_st", "lnq_mv", "xn_ready"))
        lnf_st, lnf_mv, xn2_ready = (sem(n) for n in ("lnf_st", "lnf_mv", "xn2_ready"))
        ln_ve, ln_rs = sem("ln_ve"), sem("ln_rs")
        xt_done, kq_done, v_done, s_done, pt_done, pv_done = (sem(n) for n in (
            "xt_done", "kq_done", "v_done", "s_done", "pt_done", "pv_done"))
        ot_done, out_done, xt2_done, lg_done, rk_done = (sem(n) for n in (
            "ot_done", "out_done", "xt2_done", "lg_done", "rk_done"))
        xnT_ready, kq_ready, spread, v_ready = (sem(n) for n in ("xnT_ready", "kq_ready", "spread", "v_ready"))
        max_done, sub_done, exp_done, pt_ready = (sem(n) for n in ("max_done", "sub_done", "exp_done", "pt_ready"))
        rec_done, on_ready, ot_ready, xc_ready, x1_ready = (sem(n) for n in (
            "rec_done", "on_ready", "ot_ready", "xc_ready", "x1_ready"))
        xn2T_ready, lg_read, gate_step = (sem(n) for n in ("xn2T_ready", "lg_read", "gate_step"))
        route, hot_ready, rank_read, seen_ready, pos_ready, xs_ready, scattered = (sem(n) for n in (
            "route", "hot_ready", "rank_read", "seen_ready", "pos_ready", "xs_ready", "scattered"))
        place2, place_ready, move_step = sem("place2"), sem("place_ready"), sem("move_step")
        cnt_done, cnti_ready, plan_step, plan_ready, zeros_in = (sem(n) for n in (
            "cnt_done", "cnti_ready", "plan_step", "plan_ready", "zeros_in"))
        dexp_done, w_step, w_ready = (sem(n) for n in ("dexp_done", "w_step", "w_ready"))
        rows_in = [sem(f"rows_in{i}") for i in range(4)]
        rows_out = [sem("rows_out0"), sem("rows_out1")]
        w1_ready, w2_ready, xinT_ready, yo_ready = (sem(n) for n in ("w1_ready", "w2_ready", "xinT_ready", "yo_ready"))
        et_done, h_done, gelu_done, y_done = (sem(n) for n in ("et_done", "h_done", "gelu_done", "y_done"))
        gathered = [sem("gathered0"), sem("gathered1")]
        gi_ready, comb_step, comb_done = (sem(n) for n in ("gi_ready", "comb_step", "comb_done"))
        ent_step, ent_act, gates_step, gates_act, gates_ready = (sem(n) for n in (
            "ent_step", "ent_act", "gates_step", "gates_act", "gates_ready"))
        h1_done, relu_done, y1_done, acc_b, acc_y, out_st = (sem(n) for n in (
            "h1_done", "relu_done", "y1_done", "acc_b", "acc_y", "out_st"))

        drained = {
            "OT": (ot_ready, 1, 1), "OUT": (x1_ready, 1, 1), "O0": (on_ready, 2, 1), "O1": (on_ready, 2, 2),
            "LG": (lg_read, 1, 1), "XT": (xnT_ready, 1, 1),
            "XT2": (xn2T_ready, 1, 1)}

        def jobs(bank, g):
            if bank == 6:
                found = [("OT", g.plus(-2)), ("OUT", g.plus(-2)), ("O1", g.plus(-1))]
                if g.layer == 0 and g.par:
                    found.insert(0, ("RK", g.plus(-4)))
            else:
                found = [("XT", g.plus(1)), ("XT2", g.plus(-3)), ("LG", g.plus(-3)), ("O0", g.plus(-1))]
            return [j for j in found if j[1].real()]

        def bank_free(pe, bank, g, name):
            names = jobs(bank, g)
            i = [n for n, _ in names].index(name)
            before = names[:i]
            for back in range(1, 4):
                before = before or jobs(bank, g.plus(-back))
            if not before:
                return
            last, m = before[-1]
            if last == "RK":
                pe.wait_ge(rank_read, m.block(1))
            else:
                s_, mult, add = drained[last]
                pe.wait_ge(s_, m.count(mult, add))

        def steps(eng, layer, step):
            for s in range(-3, LOOP0):
                step(Group(0, s, layer))
            with eng.Fori(0, (LOOP1 - LOOP0) // 2) as u:
                step(Group(u, LOOP0, layer))
                step(Group(u, LOOP0 + 1, layer))
            for s in range(LOOP1, GROUPS + 5):
                step(Group(0, s, layer))

        def sl(t, n=1):
            return slice(t, t + n) if isinstance(t, int) else bass.ds(t, n)

        block = ctx.enter_context(nc.Block())

        @block.sync
        def _(sp):
            xv = A["x"].rearrange("(t p) d -> p t d", p=P)
            sp.dma_start(x[:, 0:8, :], xv[:, 0:8, :]).then_inc(x_in0, 16)
            for dst, src in ((cst[:, :], A["consts"]), (wk[0][:, :], A["L0_xattn_Wk"]), (wq[0][:, :], A["L0_xattn_Wq"]),
                             (wv[0][:, :], A["L0_xattn_Wv"]), (wo[0][:, :], A["L0_xattn_Wo"]),
                             (bcol[:, :], A["bcol"]), (gates[:, :], A["gates"].partition_broadcast(P)),
                             (bo[0][:, :], A["L0_xattn_bo"].partition_broadcast(P)),
                             (bo[1][:, :], A["L1_xattn_bo"].partition_broadcast(P)),
                             (wq[1][:, :], A["wq1"]), (wk[1][:, :], A["wk1"]), (wv[1][:, :], A["wv1"]),
                             (wo[1][:, :], A["wo1"]), (wr0[:, :], A["wr0"]), (wr1[:, :], A["wr1"]),
                             (gb1[:, :], A["L1_ffn_gate_b"].partition_broadcast(P)),
                             (db1[:, :], A["L1_ffn_dp_b1"].partition_broadcast(P)),
                             (dw2[:, :], A["dw2"].partition_broadcast(P)),
                             (db2[:, :], A["L1_ffn_dp_b2"].partition_broadcast(P)),
                             (maskn, A["mask"].rearrange("(t b) k -> b t k", b=2))):
                sp.dma_start(dst, src).then_inc(setup_in, 16)
            sp.dma_start(x[:, 8:TILES, :], xv[:, 8:TILES, :]).then_inc(x_in1, 16)

            def load_ctx(g):
                wait(sp, v_done, g.count(1, -1))
                sp.dma_start(ctxg[g.par][:, :, :, :].rearrange("p b i k -> p (b i k)"), A["ctxT"][:, sl(g.at(2 * GT), 2 * GT)]).then_inc(ctx_in[g.par], 16)

            def step(g):
                if g.plus(2).real():
                    load_ctx(g.plus(2))
                if g.layer == 0 and isinstance(g.u, int) and g.k == 0:
                    for dst, src in ((w1a[:, :].rearrange("p (e f) -> p e f", e=E0), A["L0_ffn_W1"].rearrange("e d f -> d e f")),
                                     (w2a[:, :].rearrange("p (e f d) -> p (e f) d", e=E0, f=FB0),
                                      A["L0_ffn_W2"].rearrange("e (f p) d -> p (e f) d", p=P)),
                                     (b1a[:, :], A["b1a"]),
                                     (b2a[:, :, :].rearrange("p e d -> p (e d)"), A["b2a"].partition_broadcast(P)),
                                     (v1[:, :].rearrange("p (e f) -> p e f", e=E1), A["L1_ffn_ew1"].rearrange("e d f -> d e f")),
                                     (v2[:, :].rearrange("p (e f d) -> p (e f) d", e=E1, f=FB1),
                                      A["L1_ffn_ew2"].rearrange("e (f p) d -> p (e f) d", p=P)),
                                     (c1[:, :], A["c1"]),
                                     (c2[:, :, :].rearrange("p e d -> p (e d)"), A["c2"].partition_broadcast(P))):
                        sp.dma_start(dst, src).then_inc(experts_in, 16)

            steps(sp, 0, step)
            sp.wait_ge(cnti_ready, 1)
            for e in range(E0):
                n = sp.value_load(cnti[0:1, e:e + 1], min_val=0, max_val=TOK)
                for i in range(1 if e < E0 - 1 else E0 + 1):
                    sp.dma_start(lists[bass.ds(n + (e * RE + i * ET), ET), :].rearrange("(p b) d -> p (b d)", p=P),
                                 zero[:, :]).then_inc(zeros_in, 16)
            sp.wait_ge(zeros_in, 16 * (2 * E0))
            sp.wait_ge(plan_ready, 1)
            sp.wait_ge(scattered, 16 * 8 * (TILES // 4))

            def load_rows(u, k):
                wait(sp, et_done, at(u, k, 1, -3, 4))
                r = sp.value_load(tri_row[0:1, sl(at(u, k, per=4))], min_val=0, max_val=E0 * RE - ET)
                sp.dma_start(xin[k % 4], lists[bass.ds(r, ET), :].rearrange("(t p) d -> p t d", p=P)).then_inc(
                    rows_in[k % 4], 16)

            for k in range(4):
                load_rows(0, k)
            with sp.Fori(1, NT // 4) as u:
                for k in range(4):
                    load_rows(u, k)
            sp.wait_ge(yo_ready, NT)

            steps(sp, 1, step)

            ov = out.rearrange("(t p) d -> p t d", p=P)

            def store_out(c):
                sp.wait_ge(acc_y, c * (4 * E1) + 4 * E1)
                sp.dma_start(ov[:, sl(c * 4, 4), :], x[:, sl(c * 4, 4), :]).then_inc(out_st, 16)

            with sp.Fori(0, TILES // 4) as c:
                store_out(c)
            sp.wait_ge(out_st, 16 * (TILES // 4))

        @block.gpsimd
        def _(pool):
            def touch(i):
                nc.gpsimd.tensor_tensor(spare[:, i:i + 1], spare[:, 4:5], spare[:, 4:5], ALU.add)

            def inverse_deviations(g):
                if g.plus(-2).real():
                    pool.wait_ge(lnf_mv, g.plus(-2).count(2, 2))
                if g.plus(2).real():
                    pool.wait_ge(lnq_mv, g.plus(2).count(2, 2))
                nc.gpsimd.tensor_tensor(ve[:, :], mv[:, :, 1], eps4[:, :], ALU.add).then_inc(ln_ve, 1)
                pool.wait_ge(ln_ve, ln_step(g))
                nc.gpsimd.tensor_tensor(rs[:, :], ve[:, :], mhalf[:, :], ALU.pow).then_inc(ln_rs, 1)

            def rows_plus_constant(g):
                if g.layer == 0:
                    if isinstance(g.u, int) and g.k == 4:
                        pool.wait_ge(x_in1, 16)
                else:
                    pool.wait_ge(comb_done, g.at(2, 2))
                wait(pool, x1_ready, g.count(1, -1))
                nc.gpsimd.tensor_tensor(xc[g.par][:, :, :], x[:, sl(g.at(2), 2), :],
                                        orow[g.layer][:, :].unsqueeze(1).to_broadcast([P, 2, DM]),
                                        ALU.add).then_inc(xc_ready, 1)

            def spread_keys_queries(g):
                pool.wait_ge(kq_ready, g.count(1, 1))
                wait(pool, s_done, g.count(4, -4))
                nc.gpsimd.tensor_tensor(Kbd[g.par][:, :, :, :],
                                        kq[:, 0, :].rearrange("p (b k) -> p b k", b=4).unsqueeze(2).to_broadcast([P, 4, 4, S]),
                                        blk.unsqueeze(1).unsqueeze(3).to_broadcast([P, 4, 4, S]), ALU.mult).then_inc(spread, 1)
                nc.gpsimd.tensor_tensor(qT[g.par][:, :, :], kq[:, 1, :].unsqueeze(1).to_broadcast([P, 4, GT]),
                                        quad.unsqueeze(2).to_broadcast([P, 4, GT]), ALU.mult).then_inc(spread, 1)

            def scatter(g, slot):
                pool.wait_ge(pos_ready, g.block(1))
                pool.wait_ge(xs_ready, g.block(1) * 2)
                carry(lambda: touch(slot), g.block(1))
                for t in range(4):
                    nc.gpsimd.indirect_dma_start(lists, bass.IndirectOffsetOnAxis(ap=pos[:, slot, t:t + 1], axis=0),
                                                 xs[:, t, :], None).then_inc(scattered, 16)

            def gather(g):
                i = g.par
                wait(pool, comb_done, g.at(2, -2))
                carry(lambda: touch(2), g.at())
                nc.gpsimd.tensor_copy(gi[i][:, :].rearrange("p (b s t) -> p b s t", b=1, s=2),
                                      place[:, sl(g.block(0)), :].rearrange("p b (s t) -> p b s t", s=2)[:, :, :, 2 * i:2 * i + 2]
                                      ).then_inc(gi_ready, 1)
                pool.wait_ge(gi_ready, g.at(1, 1))
                carry(lambda: touch(3), g.at())
                for s_ in range(2):
                    for t in range(2):
                        c = 2 * s_ + t
                        nc.gpsimd.indirect_dma_start(ysb[i][:, s_, t, :], None, louts,
                                                     bass.IndirectOffsetOnAxis(ap=gi[i][:, c:c + 1], axis=0)
                                                     ).then_inc(gathered[i], 16)

            def step(g):
                def have(d):
                    return g.plus(d).real()

                if have(-1):
                    rows_plus_constant(g.plus(-1))
                if g.layer == 0 and g.par == 0 and have(-5):
                    scatter(g.plus(-5), 1)
                if have(1):
                    spread_keys_queries(g.plus(1))
                if have(-2) or have(2):
                    inverse_deviations(g)
                if g.layer == 0 and g.par and have(-4):
                    scatter(g.plus(-4), 0)
                if g.layer == 1 and have(3):
                    gather(g.plus(3))

            pool.wait_ge(setup_in, SETUP)
            pool.wait_ge(x_in0, 16)
            pool.wait_ge(orow_done, 2)
            steps(pool, 0, step)

            def store_rows(u, k):
                pool.wait_ge(yo_ready, at(u, k, 1, 1, 4))
                pool.dma_start(louts[sl(at(u, k, ET, 0, 4), ET), :].rearrange("(t p) d -> p t d", p=P),
                               yo[k % 2]).then_inc(rows_out[k % 2], 16)

            with pool.Fori(0, NT // 4) as u:
                for k in range(4):
                    store_rows(u, k)
            pool.wait_ge(rows_out[0], 16 * (NT // 2))
            pool.wait_ge(rows_out[1], 16 * (NT // 2))
            pool.wait_ge(place_ready, 1)
            steps(pool, 1, step)

        @block.scalar
        def _(act):
            def copy(dst, src, bias=None):
                if bias is None:
                    return nc.scalar.activation(dst, src, ACT.Copy)
                return nc.scalar.activation(dst, src, ACT.Identity, bias=bias)

            def heads_out(g):
                act.wait_ge(ot_done, g.count(1, 1))
                wait(act, out_done, g.count(1, -1))
                copy(OT[g.par][:, :], bank6[:, 0:GT]).then_inc(ot_ready, 1)

            def tokens_in(g):
                act.wait_ge(xt_done, g.count(1, 1))
                wait(act, kq_done, g.count(2, -2))
                copy(xnT[g.par][:, :], bank7[:, 0:GT]).then_inc(xnT_ready, 1)

            def probs_out(g, c):
                act.wait_ge(pt_done, g.count(4, c + 1))
                wait(act, pv_done, g.count(4, c - 3))
                copy(PT[c][:, :], ps_p[:, c % 2, :]).then_inc(pt_ready, 1)

            def exps(g, q):
                act.wait_ge(sub_done, g.count(4, q + 1))
                nc.scalar.activation(Pr[g.par][:, q, :], Pr[g.par][:, q, :], ACT.Exp,
                                     scale=SCALES[g.layer]).then_inc(exp_done, 1)

            def keys_queries(g):
                act.wait_ge(kq_done, g.count(2, 2))
                wait(act, spread, g.count(2, 0))
                if g.layer == 0:
                    copy(kq[:, 0, :], kq_bank[:, 0:GT], bcol[:, 1:2])
                    copy(kq[:, 1, :], kq_bank[:, GT:2 * GT], bcol[:, 0:1]).then_inc(kq_ready, 1)
                else:
                    copy(kq[:, :, :].rearrange("p i t -> p (i t)"), kq_bank).then_inc(kq_ready, 1)

            def values(g):
                act.wait_ge(v_done, g.count(1, 1))
                wait(act, pv_done, g.count(4, -4))
                v = v_bank.rearrange("p (b j c) -> p b j c", b=4, j=8)
                for i in range(2):
                    r = slice(S * i, S * i + S)
                    c = slice(DK * i, DK * i + DK)
                    ins = copy(Vbd[g.par][r, :, :, c], v[r, :, :, c])
                ins.then_inc(v_ready, 1)

            def collect_rows(g):
                act.wait_ge(xn2_ready, g.count(2, 2))
                wait(act, scattered, g.block(0) * (16 * 8))
                for i in range(2):
                    copy(xs[:, 2 * i:2 * i + 2, :], xn2[i][:, :, :]).then_inc(xs_ready, 1)

            def tokens2(g):
                act.wait_ge(xt2_done, g.count(1, 1))
                wait(act, lg_done, g.count(1, -1))
                if g.layer == 1:
                    copy(xn3T[:, sl(g.at(GT), GT)], bank7[:, 0:GT])
                copy(xn2T[g.par][:, :], bank7[:, 0:GT]).then_inc(xn2T_ready, 1)

            def step(g):
                def have(d):
                    return g.plus(d).real()

                if have(1):
                    tokens_in(g.plus(1))
                if have(-3):
                    tokens2(g.plus(-3))
                if have(0):
                    exps(g, 0)
                    exps(g, 1)
                if have(-2):
                    heads_out(g.plus(-2))
                if have(1):
                    keys_queries(g.plus(1))
                for c in range(4):
                    if have(-1):
                        probs_out(g.plus(-1), c)
                    if have(0) and c in (1, 2):
                        exps(g, 1 + c)
                    if g.layer == 0 and g.par == 0 and have(-3) and c == 1:
                        collect_rows(g.plus(-3))
                if have(1):
                    values(g.plus(1))

            act.wait_ge(setup_in, SETUP)
            nc.scalar.activation(tg[:, :], gates[:, :], ACT.Tanh).then_inc(tanh_done, 1)
            act.wait_ge(consts_done, 1)
            act.wait_ge(plan_step, 1)
            steps(act, 0, step)

            act.wait_ge(place2, TILES // 4)
            nc.scalar.activation(d_all[:, :, :], d_all[:, :, :], ACT.Exp).then_inc(dexp_done, 1)
            nc.scalar.activation(p2[:, :], m2_all[:, :], ACT.Exp).then_inc(dexp_done, 1)

            def gelu(u, k):
                i = k % 2
                act.wait_ge(w1_ready, at(u, k, 2, 2, 4))
                wait(act, y_done, at(u, k, 1, -1, 4))
                for f in range(FB0):
                    if f % 2 == 0:
                        act.wait_ge(h_done, at(u, k, 2, 1 + f // 2, 4))
                    nc.scalar.activation(hT[i][:, f, :], ps_s[:, 2 * i + f // 2, ET * (f % 2):ET * (f % 2 + 1)],
                                         ACT.Gelu_apprx_tanh, bias=b1s[i][:, f:f + 1]).then_inc(gelu_done, 1)

            for k in range(4):
                gelu(0, k)
            with act.Fori(1, NT // 4) as u:
                for k in range(4):
                    gelu(u, k)

            act.wait_ge(rows_out[0], 16 * (NT // 2))
            act.wait_ge(rows_out[1], 16 * (NT // 2))
            steps(act, 1, step)

            act.wait_ge(ent_step, 2)
            nc.scalar.activation(ent2[:, :], ent2[:, :], ACT.Exp, scale=-1.0).then_inc(ent_act, 1)
            act.wait_ge(gates_step, 2)
            nc.scalar.activation(we[:, :, :], we[:, :, :], ACT.Exp).then_inc(gates_act, 1)
            act.wait_ge(ent_act, 1)
            nc.scalar.activation(ent2[:, :], ent2[:, :], ACT.Ln, bias=1.0).then_inc(ent_act, 1)

            def relu(u, k):
                wait(act, y1_done, u * 4 + (k - 1))
                for f in range(FB1):
                    act.wait_ge(h1_done, u * 8 + (2 * k + f + 1))
                    nc.scalar.activation(hD[k % 2][:, f, :], ps_s[:, (2 * k + f) % 4, :], ACT.Relu,
                                         bias=c1[:, (k % 4) * FB1 + f:(k % 4) * FB1 + f + 1]).then_inc(relu_done, 1)

            for k in range(E1):
                relu(0, k)
            with act.Fori(1, TILES // 4) as u:
                for k in range(E1):
                    relu(u, k)

        @block.vector
        def _(dve):
            V = nc.vector

            def touch(i):
                V.memset(spare_v[:, i:i + 1], 0.0)

            def flat(ap):
                return ap.rearrange("p a d -> p (a d)")

            def statistics(g, slot, s_st, s_mv):
                carry(lambda: touch(slot), g.at())
                for j in range(2):
                    V.bn_stats(st[:, slot + j, :], flat(x[:, sl(g.at(2, j)), :])).then_inc(s_st, 1)
                dve.wait_ge(s_st, g.count(2, 2))
                carry(lambda: touch(slot + 1), g.at())
                for j in range(2):
                    V.bn_aggr(mv[:, slot + j, :], st[:, slot + j, :]).then_inc(s_mv, 1)

            def normalise(g, slot, dst, step_, s_out):
                dve.wait_ge(ln_rs, ln_step(step_))
                for j in range(2):
                    V.tensor_scalar(dst[:, j, :], flat(x[:, sl(g.at(2, j)), :]), mv[:, slot + j, 0:1],
                                    rs[:, slot + j:slot + j + 1], ALU.subtract, ALU.mult).then_inc(s_out, 1)

            def statistics_in(g):
                if g.layer == 0:
                    if isinstance(g.u, int) and g.k in (0, 4):
                        dve.wait_ge(x_in0 if g.k == 0 else x_in1, 16)
                else:
                    dve.wait_ge(comb_done, g.at(2, 2))
                wait(dve, xn_ready, g.count(2, 0))
                statistics(g, 2, lnq_st, lnq_mv)

            def normalise_in(g, step_):
                wait(dve, xt_done, g.count(1, -1))
                normalise(g, 2, xn[g.par], step_, xn_ready)

            def statistics_mid(g):
                dve.wait_ge(x1_ready, g.count(1, 1))
                wait(dve, xn2_ready, g.count(2, 0))
                statistics(g, 0, lnf_st, lnf_mv)

            def normalise_mid(g, step_):
                wait(dve, xt2_done, g.count(1, -1))
                if g.layer == 0:
                    wait(dve, xs_ready, g.block(0) * 2)
                normalise(g, 0, xn2[g.par], step_, xn2_ready)

            def residual(g):
                dve.wait_ge(out_done, g.count(1, 1))
                dve.wait_ge(xc_ready, g.count(1, 1))
                V.tensor_tensor(x[:, sl(g.at(2), 2), :], bank6[:, 0:GT].rearrange("p (t d) -> p t d", t=2),
                                xc[g.par][:, :, :], ALU.add).then_inc(x1_ready, 1)

            def less_maximum(g, half):
                def view(ap):
                    return ap.rearrange("p (h k) -> p h k", k=S)

                def maximum(q):
                    dve.wait_ge(s_done, g.count(4, q + 1))
                    V.tensor_reduce(mx[g.par][:, q, :], view(ps_s[:, q, :]), AX, ALU.max).then_inc(max_done, 1)

                def subtract(q):
                    dve.wait_ge(max_done, g.count(4, q + 1))
                    wait(dve, pv_done, g.count(4, -4))
                    V.tensor_tensor(view(Pr[g.par][:, q, :]), view(ps_s[:, q, :]),
                                    mx[g.par][:, q, :].unsqueeze(2).to_broadcast([P, 8, S]),
                                    ALU.subtract).then_inc(sub_done, 1)

                for q in range(2 * half, 2 * half + 2):
                    maximum(q)
                    subtract(q)

            def heads(g, pr):
                o = (bank7, bank6)[pr][:, 0:8 * 2 * VW].rearrange("p (j b c) -> p j b c", j=8, b=2)
                dve.wait_ge(pv_done, g.count(4, 2 * pr + 2))
                V.reciprocal(rden[:, pr, :, :], o[:, :, 0, 2 * DK:VW]).then_inc(rec_done, 1)
                dve.wait_ge(rec_done, g.count(2, pr + 1))
                wait(dve, ot_done, g.count(1, -1))
                for b in range(2):
                    r = slice(S * b, S * b + S)
                    ins = V.tensor_tensor(On[g.par][r, pr, :].rearrange("p (j h d) -> p j h d", j=8, h=2),
                                          o[r, :, b, 0:2 * DK].rearrange("p j (h d) -> p j h d", h=2),
                                          rden[r, pr, :, :].unsqueeze(3).to_broadcast([S, 8, 2, DK]), ALU.mult)
                ins.then_inc(on_ready, 1)

            def router_logits(g):
                dve.wait_ge(lg_done, g.count(1, 1))
                V.tensor_copy(lgb[:, 2 * g.par:2 * g.par + 2, :],
                              bank7[:, 0:2 * E0].rearrange("p (t e) -> p t e", t=2)).then_inc(lg_read, 1)

            ROUTE = 15

            def chain(sem_, start):
                n = [0]

                def link(ins):
                    n[0] += 1
                    ins.then_inc(sem_, 1)
                    dve.wait_ge(sem_, start + n[0])
                return link

            def route_tops(g):
                link = chain(route, g.block(0) * ROUTE)
                desc4 = desc.unsqueeze(1).to_broadcast([P, 4, E0])

                def b4(ap):
                    return ap.unsqueeze(2).to_broadcast([P, 4, E0])

                dve.wait_ge(lg_read, g.count(1, 1))
                link(V.tensor_reduce(m1[:, :], lgb[:, :, :], AX, ALU.max))
                link(V.tensor_tensor(dlt[:, :, :], lgb[:, :, :], b4(m1[:, :]), ALU.subtract))
                link(V.scalar_tensor_tensor(cand[:, :, :], dlt[:, :, :], 0.0, desc4, ALU.is_equal, ALU.mult))
                link(V.tensor_reduce(top[:, :], cand[:, :, :], AX, ALU.max))
                link(V.tensor_tensor(hot[:, 0, :, :], desc4, b4(top[:, :]), ALU.is_equal))
                link(V.scalar_tensor_tensor(dl2[:, :, :], hot[:, 0, :, :], -BIG, dlt[:, :, :], ALU.mult, ALU.add))
                link(V.tensor_reduce(m2[:, :], dl2[:, :, :], AX, ALU.max))
                link(V.tensor_tensor(cand[:, :, :], dl2[:, :, :], b4(m2[:, :]), ALU.is_equal))
                link(V.tensor_tensor(cand[:, :, :], cand[:, :, :], desc4, ALU.mult))
                link(V.tensor_reduce(top[:, :], cand[:, :, :], AX, ALU.max))
                link(V.tensor_tensor(hot[:, 1, :, :], desc4, b4(top[:, :]), ALU.is_equal))
                V.tensor_tensor(hotb[:, :, :], hot[:, 0, :, :], hot[:, 1, :, :], ALU.add).then_inc(hot_ready, 1)
                V.tensor_reduce(hsum[:, :], hot[:, :, :, :].rearrange("p s t e -> p e (s t)"), AX, ALU.add).then_inc(route, 1)
                V.tensor_copy(d_all[:, sl(g.block(0) * 4, 4), :], dlt[:, :, :])
                V.tensor_copy(m2_all[:, sl(g.block(0) * 4, 4)], m2[:, :]).then_inc(place2, 1)

            def route_places(g):
                dve.wait_ge(rk_done, g.block(1))
                V.tensor_tensor(rank[:, :, :], bank6[:, 0:4 * E0].rearrange("p (t e) -> p t e", t=4),
                                base.unsqueeze(1).to_broadcast([P, 4, E0]), ALU.add).then_inc(rank_read, 1)
                dve.wait_ge(route, g.block(0) * ROUTE + 12)
                V.tensor_tensor(seen[:, :], seen[:, :], hsum[:, :], ALU.add).then_inc(route, 1)
                dve.wait_ge(rank_read, g.block(1))
                V.tensor_tensor(rsel[:, :, :, :].rearrange("p s t e -> p s (t e)"),
                                hot[:, :, :, :].rearrange("p s t e -> p s (t e)"),
                                rank[:, :, :].rearrange("p t e -> p (t e)").unsqueeze(1).to_broadcast([P, 2, 4 * E0]),
                                ALU.mult).then_inc(route, 1)
                dve.wait_ge(route, g.block(0) * ROUTE + 14)
                V.tensor_copy(seenb[:, :], seen[:, :]).then_inc(seen_ready, 1)
                V.tensor_reduce(posf[:, :, :], rsel[:, :, :, :], AX, ALU.add).then_inc(route, 1)
                dve.wait_ge(route, g.block(0) * ROUTE + 15)
                wait(dve, scattered, g.block(0) * (16 * 8))
                V.tensor_copy(pos[:, :, :], posf[:, :, :]).then_inc(pos_ready, 1)
                V.tensor_copy(pos_all[:, sl(g.block(0)), :], posf[:, :, :].rearrange("p (b s) t -> p b (s t)", b=1))

            def gate_logits(g):
                lg = bank7[:, 0:2 * (E1 + HD1)].rearrange("p (t e) -> p t e", t=2)
                dve.wait_ge(lg_done, g.count(1, 1))
                V.tensor_tensor(gl[:, sl(g.at(2), 2), :], lg[:, :, 0:E1],
                                gb1[:, :].unsqueeze(1).to_broadcast([P, 2, E1]), ALU.add)
                V.tensor_tensor(t1[:, :, :], lg[:, :, E1:], db1[:, :].unsqueeze(1).to_broadcast([P, 2, HD1]),
                                ALU.add).then_inc(lg_read, 1)
                dve.wait_ge(lg_read, g.count(1, 1))
                V.scalar_tensor_tensor(t2[:, :, :], t1[:, :, :], 0.0, dw2[:, :].unsqueeze(1).to_broadcast([P, 2, HD1]),
                                       ALU.max, ALU.mult).then_inc(gate_step, 1)
                dve.wait_ge(gate_step, g.at(2, 1))
                V.tensor_reduce(z_all[:, sl(g.at(2), 2)], t2[:, :, :], AX, ALU.add).then_inc(gate_step, 1)

            def combine(g):
                dve.wait_ge(gathered[g.par], g.u * 64 + 64 * (g.k // 2 + 1))
                for s_ in range(2):
                    for t in range(2):
                        tile = flat(x[:, sl(g.at(2, t)), :])
                        V.scalar_tensor_tensor(tile, ysb[g.par][:, s_, t, :], flat(w_all[:, sl(g.at(2, t)), s_:s_ + 1]), tile,
                                               ALU.mult, ALU.add).then_inc((comb_step, comb_done)[s_], 1)
                    if s_ == 0:
                        dve.wait_ge(comb_step, g.at(2, 2))

            def step(g):
                def have(d):
                    return g.plus(d).real()

                if have(0):
                    less_maximum(g, 0)
                if g.layer == 0 and g.par and have(-4):
                    route_places(g.plus(-4))
                if have(0):
                    less_maximum(g, 1)
                if have(-3):
                    (router_logits, gate_logits)[g.layer](g.plus(-3))
                if have(-2):
                    residual(g.plus(-2))
                if g.layer == 1 and have(2):
                    combine(g.plus(2))
                if have(-2):
                    statistics_mid(g.plus(-2))
                if have(2):
                    statistics_in(g.plus(2))
                if g.layer == 0 and g.par == 0 and have(-3):
                    route_tops(g.plus(-3))
                if have(-1):
                    heads(g.plus(-1), 0)
                if have(-2):
                    normalise_mid(g.plus(-2), g)
                if have(2):
                    normalise_in(g.plus(2), g)
                if have(-1):
                    heads(g.plus(-1), 1)

            for i in range(2):
                V.memset(Vbd[i][:, :, :, :], 0.0)
            V.memset(ones[:, :], 1.0)
            V.memset(mhalf[:, :], -0.5)
            V.memset(eps4[:, :], EPS)
            V.memset(mv[:, :, :], 1.0)
            V.memset(spare[:, :], 0.0)
            V.memset(zero[:, :], 0.0)
            V.memset(seen[:, :], 0.0)
            V.memset(seenb[:, :], 0.0)
            V.memset(oneE[:, :], 1.0).then_inc(plan_step, 1)
            dve.wait_ge(plan_step, 1)
            for i in range(2):
                V.memset(Vbd[i][0:S, :, :, 2 * DK:2 * DK + 1], 1.0)
                V.memset(Vbd[i][S:P, :, :, 2 * DK + 1:VW], 1.0)
            dve.wait_ge(setup_in, SETUP)
            V.tensor_copy(tri[:, :], cst[:, C_TRI:C_TRI + P])
            V.tensor_copy(ind[:, :], cst[0:2, C_IND:C_IND + P])
            V.tensor_scalar(negm[:, :, :], maskn, 0, NEG, ALU.is_equal, ALU.mult).then_inc(consts_done, 1)
            dve.wait_ge(tanh_done, 1)
            for i in range(2):
                V.tensor_scalar(wo[i][:, :], wo[i][:, :], tg[:, i:i + 1], None, ALU.mult).then_inc(wo_scaled, 1)
            V.tensor_scalar(orow[1][:, :], bo[1][:, :], tg[:, 1:2], None, ALU.mult).then_inc(orow_done, 1)
            dve.wait_ge(bv_done, 1)
            V.scalar_tensor_tensor(orow[0][:, :], bo[0][:, :], tg[:, 0:1], bank6[:, 0:DM],
                                   ALU.mult, ALU.add).then_inc(orow_done, 1)
            steps(dve, 0, step)

            link = chain(plan_step, 1)
            dve.wait_ge(cnt_done, 1)
            link(V.tensor_copy(cnt[:, :], bank6[:, 0:E0]))
            V.tensor_copy(cnti[:, :], cnt[0:1, :]).then_inc(cnti_ready, 1)
            link(V.tensor_tensor(cge, cnt[:, :].unsqueeze(2).to_broadcast([P, E0, TOK // ET]),
                                 cst[:, C_THR:C_THR + TOK // ET].unsqueeze(1).to_broadcast([P, E0, TOK // ET]), ALU.is_gt))
            link(V.tensor_reduce(ntl[:, :], cge, AX, ALU.add))
            link(V.tensor_tensor_scan(nend[:, :], oneE[:, :], ntl[0:1, :], 0.0, ALU.mult, ALU.add))
            link(V.tensor_scalar(nend[:, :], nend[:, :], float(ET), None, ALU.mult))
            link(V.tensor_scalar(jump[:, :], ntl[:, :], -float(ET), float(RE), ALU.mult, ALU.add))
            rows = cst[0:1, C_ROW:C_ROW + NT]
            link(V.tensor_tensor(tge, rows.unsqueeze(2).to_broadcast([1, NT, E0 - 1]),
                                 nend[:, 0:E0 - 1].unsqueeze(1).to_broadcast([1, NT, E0 - 1]), ALU.is_ge))
            link(V.tensor_tensor(tjump, tge,
                                 jump[0:1, 0:E0 - 1].unsqueeze(1).to_broadcast([1, NT, E0 - 1]), ALU.mult))
            link(V.tensor_reduce(tef[:, :], tge, AX, ALU.add))
            link(V.tensor_reduce(trf[:, :], tjump, AX, ALU.add))
            link(V.tensor_tensor(trf[:, :], trf[:, :], rows, ALU.add))
            link(V.tensor_copy(tei[:, :], tef[:, :]))
            V.tensor_copy(tri_row[:, :], trf[:, :]).then_inc(plan_ready, 1)

            link = chain(move_step, 0)
            link(V.tensor_copy(place[:, :, :], pos_all[:, :, :]))
            for e in range(1, E0):
                link(V.tensor_scalar(moved, pos_all[:, :, :], float(e * RE), jump[:, e - 1:e], ALU.is_ge, ALU.mult))
                link(V.tensor_tensor(place[:, :, :], place[:, :, :], moved, ALU.subtract))
            V.tensor_copy(place[:, :, :], place[:, :, :]).then_inc(place_ready, 1)

            link = chain(w_step, 0)
            dve.wait_ge(dexp_done, 2)
            link(V.tensor_reduce(den[:, :], d_all[:, :, :], AX, ALU.add))
            link(V.reciprocal(ent[:, :], den[:, :]))
            link(V.tensor_tensor(p2[:, :], p2[:, :], ent[:, :], ALU.mult))
            link(V.scalar_tensor_tensor(den[:, :], ent[:, :], 1e-8, p2[:, :], ALU.add, ALU.add))
            link(V.reciprocal(den[:, :], den[:, :]))
            V.scalar_tensor_tensor(w_all[:, :, 0], ent[:, :], tg[:, 2:3], den[:, :], ALU.mult, ALU.mult)
            V.scalar_tensor_tensor(w_all[:, :, 1], p2[:, :], tg[:, 2:3], den[:, :], ALU.mult, ALU.mult).then_inc(w_ready, 1)

            def expert_of(u, k):
                return dve.value_load(tei[0:1, sl(at(u, k, per=4))], min_val=0, max_val=E0 - 1)

            def stage_w1(u, k):
                i = k % 2
                e = expert_of(u, k)
                wait(dve, gelu_done, at(u, k, FB0, -FB0, 4))
                V.tensor_copy(w1s[i], w1a[:, bass.ds(e * F0, F0)]).then_inc(w1_ready, 1)
                V.tensor_copy(b1s[i][:, :], b1a[:, bass.ds(e * FB0, FB0)]).then_inc(w1_ready, 1)

            def stage_w2(u, k):
                e = expert_of(u, k)
                wait(dve, y_done, at(u, k, 1, -1, 4))
                V.tensor_copy(w2s[k % 2], w2a[:, bass.ds(e * F0, F0)]).then_inc(w2_ready, 1)

            def rows_turned(u, k):
                dve.wait_ge(et_done, at(u, k, 1, 1, 4))
                wait(dve, h_done, at(u, k, 2, -2, 4))
                V.tensor_copy(xinT[k % 2], ps_p[:, k % 2, 0:ET]).then_inc(xinT_ready, 1)

            def rows_made(u, k):
                i = k % 2
                e = expert_of(u, k)
                dve.wait_ge(y_done, at(u, k, 1, 1, 4))
                wait(dve, rows_out[i], u * 32 + 16 * (k // 2))
                V.tensor_tensor(yo[i], ps_m[:, i, 0:ET].rearrange("p (t d) -> p t d", t=2),
                                b2a[:, bass.ds(e, 1), :].to_broadcast([P, 2, DM]), ALU.add).then_inc(yo_ready, 1)

            def tile_step(u, k, first=False, more=True):
                if more:
                    stage_w1(u, k + 1)
                    rows_turned(u, k + 1)
                if not first:
                    rows_made(u, k - 1)
                if more:
                    stage_w2(u, k + 1)

            dve.wait_ge(experts_in, 16 * 8)
            tile_step(0, -1, first=True)
            tile_step(0, 0, first=True)
            for k in range(1, 4):
                tile_step(0, k)
            with dve.Fori(1, NT // 4 - 1) as u:
                for k in range(4):
                    tile_step(u, k)
            for k in range(NT - 4, NT - 1):
                tile_step(0, k)
            tile_step(0, NT - 1, more=False)
            tile_step(0, NT, more=False)

            steps(dve, 1, step)

            link = chain(ent_step, 0)
            dve.wait_ge(gate_step, 2 * GROUPS)
            link(V.tensor_scalar(ent[:, :], z_all[:, :], db2[:, 0:1], None, ALU.add))
            link(V.scalar_tensor_tensor(ent2[:, :], ent[:, :], -1.0, ent[:, :], ALU.mult, ALU.max))
            link = chain(gates_step, 0)

            def be(ap):
                return ap.unsqueeze(2).to_broadcast([P, TILES, E1])

            link(V.tensor_reduce(gmx[:, :], gl[:, :, :], AX, ALU.max))
            link(V.tensor_tensor(we[:, :, :], gl[:, :, :], be(gmx[:, :]), ALU.subtract))
            other = gl[:, :, :].unsqueeze(2).to_broadcast([P, TILES, E1, E1])
            own = gl[:, :, :].unsqueeze(3).to_broadcast([P, TILES, E1, E1])
            tie = cst[:, C_TIE:C_ALL].unsqueeze(1).to_broadcast([P, TILES, E1 * E1])
            link(V.tensor_tensor(big[0], other, own, ALU.is_gt))
            link(V.tensor_tensor(big[1], other, own, ALU.is_equal))
            flat1 = big[1].rearrange("p t e f -> p t (e f)")
            link(V.tensor_tensor(flat1, flat1, tie, ALU.mult))
            link(V.tensor_tensor(big[0], big[0], big[1], ALU.add))
            link(V.tensor_reduce(sel, big[0], AX, ALU.add))
            dve.wait_ge(ent_act, 2)
            link(V.scalar_tensor_tensor(ent[:, :], ent[:, :], 0.0, ent2[:, :], ALU.max, ALU.add))
            link(V.tensor_scalar(kt[:, :], ent[:, :], 0.5, 1 / 1.5, ALU.subtract, ALU.mult))
            link(V.tensor_scalar(kt[:, :], kt[:, :], 0.0, 1.0, ALU.max, ALU.min))
            link(V.tensor_scalar(kt[:, :], kt[:, :], float(E1 - 1), 1.0, ALU.mult, ALU.add))
            link(V.tensor_scalar(kt[:, :], kt[:, :], ROUND, None, ALU.add))
            link(V.tensor_scalar(kt[:, :], kt[:, :], ROUND, None, ALU.subtract))
            link(V.tensor_tensor(sel, sel, be(kt[:, :]), ALU.is_lt))
            dve.wait_ge(gates_act, 1)
            link(V.tensor_tensor(we[:, :, :], we[:, :, :], sel, ALU.mult))
            link(V.tensor_reduce(gmx[:, :], we[:, :, :], AX, ALU.add))
            link(V.reciprocal(gmx[:, :], gmx[:, :]))
            link(V.tensor_tensor(we[:, :, :], we[:, :, :], be(gmx[:, :]), ALU.mult))
            V.tensor_scalar(we[:, :, :], we[:, :, :], tg[:, 3:4], None, ALU.mult).then_inc(gates_ready, 1)
            dve.wait_ge(gates_ready, 1)

            def add_expert(u, e):
                wait(dve, acc_y, u * 16 + 4 * e)
                for t in range(4):
                    tile = flat(x[:, sl(u * 4 + t), :])
                    V.scalar_tensor_tensor(tile, c2[:, e, :], flat(we[:, sl(u * 4 + t), e:e + 1]), tile,
                                           ALU.mult, ALU.add).then_inc(acc_b, 1)
                dve.wait_ge(y1_done, u * 4 + (e + 1))
                for t in range(4):
                    tile = flat(x[:, sl(u * 4 + t), :])
                    dve.wait_ge(acc_b, u * 16 + (4 * e + t + 1))
                    V.scalar_tensor_tensor(tile, ps_p[:, e % 2, DM * t:DM * (t + 1)], flat(we[:, sl(u * 4 + t), e:e + 1]), tile,
                                           ALU.mult, ALU.add).then_inc(acc_y, 1)

            with dve.Fori(0, TILES // 4) as u:
                for e in range(E1):
                    add_expert(u, e)

        @block.tensor
        def _(pe):
            mm, turn = nc.tensor.matmul, nc.tensor.transpose

            def heads_turned(g):
                bank_free(pe, 6, g.plus(2), "OT")
                pe.wait_ge(on_ready, g.count(2, 2))
                for t in range(2):
                    ins = turn(bank6[:, P * t:P * t + P], On[g.par][:, t, :], ident)
                ins.then_inc(ot_done, 1)

            def scores(g, q):
                if q == 0:
                    pe.wait_ge(spread, g.count(2, 2))
                elif q == 2:
                    pe.wait_ge(v_ready, g.count(1, 1))
                if g.layer == 1:
                    if q % 2 == 0:
                        carry(lambda: mm(ps_s[:, q, 0:1], ones[:, :], ones[:, 0:1], start=True, stop=True,
                                         skip_group_check=True), g.at())
                    mm(ps_s[:, q, :].rearrange("p (t h k) -> p t h k", t=2, h=4), ind[:, :],
                       negm[:, sl(g.at(2), 2), :].unsqueeze(2).to_broadcast([2, 2, 4, S]),
                       start=True, stop=False, skip_group_check=True)
                for b in range(4):
                    ins = mm(ps_s[S * (b % 2):S * (b % 2) + S, q, GT * (b // 2):GT * (b // 2) + GT],
                             qT[g.par][:, q, S * b:S * b + S], Kbd[g.par][:, b, :, :].rearrange("p h k -> p (h k)"),
                             start=(g.layer == 0), stop=True, skip_group_check=True)
                ins.then_inc(s_done, 1)

            def tokens_turned(g):
                bank_free(pe, 7, g.plus(-1), "XT")
                pe.wait_ge(xn_ready, g.count(2, 2))
                for t in range(2):
                    ins = turn(bank7[:, P * t:P * t + P], xn[g.par][:, t, :], ident)
                ins.then_inc(xt_done, 1)

            def project_out(g):
                bank_free(pe, 6, g.plus(2), "OUT")
                pe.wait_ge(ot_ready, g.count(1, 1))
                for t in range(2):
                    ins = mm(bank6[:, P * t:P * t + P], OT[g.par][:, P * t:P * t + P], wo[g.layer][:, :], start=True, stop=True)
                ins.then_inc(out_done, 1)

            def probs_turned(g, c):
                pr, half = c // 2, c % 2
                pe.wait_ge(exp_done, g.count(4, 2 * half + 2))
                wait(pe, pt_ready, g.count(4, c - 1))
                for i in range(4):
                    j = 4 * half + i
                    col = GT * pr + P * (j % 2)
                    ins = turn(ps_p[:, c % 2, P * i:P * i + P], Pr[g.par][:, j // 2, col:col + P], ident)
                ins.then_inc(pt_done, 1)

            def probs_by_values(g, c):
                pr, half = c // 2, c % 2
                if half == 0:
                    bank_free(pe, 6 if pr else 7, g.plus(1), f"O{pr}")
                pe.wait_ge(pt_ready, g.count(4, c + 1))
                pe.wait_ge(v_ready, g.count(1, 1))
                for i in range(4):
                    j = 4 * half + i
                    ins = mm((bank7, bank6)[pr][:, 2 * VW * j:2 * VW * (j + 1)].rearrange("p (b c) -> p b c", b=2),
                             PT[c][:, P * i:P * i + P], Vbd[g.par][:, 2 * pr:2 * pr + 2, j, :], start=True, stop=True)
                ins.then_inc(pv_done, 1)

            def keys_queries(g):
                wait(pe, sub_done, g.count(4, -2))
                pe.wait_ge(ctx_in[g.par], g.half_count())
                mm(kq_bank[:, 0:GT], wk[g.layer][:, :], ctxg[g.par][:, :, 0, :], start=True, stop=True).then_inc(kq_done, 1)
                pe.wait_ge(xnT_ready, g.count(1, 1))
                mm(kq_bank[:, GT:2 * GT], wq[g.layer][:, :], xnT[g.par][:, :], start=True, stop=True).then_inc(kq_done, 1)

            def values(g):
                wait(pe, sub_done, g.count(4, 0))
                for b in range(4):
                    ins = mm(v_bank[:, P * b:P * b + P],
                             ctxg[g.par][:, b, :, :].rearrange("p i k -> p (i k)"), wv[g.layer][:, :],
                             start=True, stop=True)
                ins.then_inc(v_done, 1)

            def tokens2_turned(g):
                bank_free(pe, 7, g.plus(3), "XT2")
                pe.wait_ge(xn2_ready, g.count(2, 2))
                for t in range(2):
                    ins = turn(bank7[:, P * t:P * t + P], xn2[g.par][:, t, :], ident)
                ins.then_inc(xt2_done, 1)

            def logits(g):
                bank_free(pe, 7, g.plus(3), "LG")
                pe.wait_ge(xn2T_ready, g.count(1, 1))
                w = (wr0, wr1)[g.layer]
                n = w.shape[1]
                for t in range(2):
                    ins = mm(bank7[:, n * t:n * t + n], xn2T[g.par][:, P * t:P * t + P], w[:, :], start=True, stop=True)
                ins.then_inc(lg_done, 1)

            def ranks(g):
                bank_free(pe, 6, g.plus(4), "RK")
                pe.wait_ge(hot_ready, g.block(1))
                wait(pe, seen_ready, g.block(0))
                o = bank6[:, 0:4 * E0].rearrange("p (t e) -> p t e", t=4)
                mm(o, tri[:, :], hotb[:, :, :], start=True, stop=False, skip_group_check=True)
                for i in range(1, 4):
                    mm(o[:, i:, :], ones[:, :], hotb[:, 0:4 - i, :], start=False, stop=False, skip_group_check=True)
                mm(o, ones[:, :], seenb[:, :].unsqueeze(1).to_broadcast([P, 4, E0]), start=False, stop=True,
                   skip_group_check=True).then_inc(rk_done, 1)

            def step(g):
                def have(d):
                    return g.plus(d).real()

                p = g.plus(-1)
                if have(0):
                    scores(g, 0)
                if have(1):
                    tokens_turned(g.plus(1))
                if have(0):
                    scores(g, 1)
                if g.layer == 0 and g.par and have(-4):
                    ranks(g.plus(-4))
                if have(-3):
                    tokens2_turned(g.plus(-3))
                if have(0):
                    scores(g, 2)
                    scores(g, 3)
                if have(-2):
                    heads_turned(g.plus(-2))
                if have(1):
                    keys_queries(g.plus(1))
                if have(-3):
                    logits(g.plus(-3))
                if have(-1):
                    probs_turned(p, 0)
                if have(-2):
                    project_out(g.plus(-2))
                if have(-1):
                    probs_turned(p, 1)
                    probs_by_values(p, 0)
                    probs_turned(p, 2)
                    probs_by_values(p, 1)
                if have(1):
                    values(g.plus(1))
                if have(-1):
                    probs_turned(p, 3)
                    probs_by_values(p, 2)
                    probs_by_values(p, 3)

            pe.wait_ge(setup_in, SETUP)
            pe.wait_ge(wo_scaled, 2)
            mm(bank6[:, 0:DM], bcol[:, 2:3].to_broadcast([P, P]), wo[0][:, :], start=True, stop=True).then_inc(bv_done, 1)
            pe.wait_ge(orow_done, 2)
            pe.wait_ge(consts_done, 1)
            steps(pe, 0, step)
            pe.wait_ge(seen_ready, TILES // 4)
            mm(bank6[:, 0:E0], ones[:, :], seenb[:, :], start=True, stop=True).then_inc(cnt_done, 1)

            def rows_turned(u, k):
                i = k % 2
                pe.wait_ge(rows_in[k % 4], u * 16 + 16 * (k // 4 + 1))
                wait(pe, xinT_ready, at(u, k, 1, -1, 4))
                for t in range(2):
                    ins = turn(ps_p[:, i, P * t:P * t + P], xin[k % 4][:, t, :], ident)
                ins.then_inc(et_done, 1)

            def hidden(u, k):
                i = k % 2
                pe.wait_ge(w1_ready, at(u, k, 2, 2, 4))
                pe.wait_ge(xinT_ready, at(u, k, 1, 1, 4))
                wait(pe, gelu_done, at(u, k, FB0, -FB0, 4))
                for f in range(FB0):
                    ins = mm(ps_s[:, 2 * i + f // 2, ET * (f % 2):ET * (f % 2 + 1)], w1s[i][:, P * f:P * f + P], xinT[i],
                             start=True, stop=True)
                    if f % 2:
                        ins.then_inc(h_done, 1)

            def rows_made(u, k):
                i = k % 2
                pe.wait_ge(w2_ready, at(u, k, 1, 1, 4))
                pe.wait_ge(gelu_done, at(u, k, FB0, FB0, 4))
                wait(pe, yo_ready, at(u, k, 1, -1, 4))
                for t in range(2):
                    for f in range(FB0):
                        ins = mm(ps_m[:, i, P * t:P * t + P], hT[i][:, f, P * t:P * t + P], w2s[i][:, P * f:P * f + P],
                                 start=(f == 0), stop=(f == FB0 - 1))
                ins.then_inc(y_done, 1)

            def tile_step(u, k):
                pe_first = isinstance(u, int)
                if not pe_first or k + 1 < NT:
                    rows_turned(u, k + 1)
                if not pe_first or 0 <= k < NT:
                    hidden(u, k)
                if not pe_first or k >= 1:
                    rows_made(u, k - 1)

            pe.wait_ge(cnti_ready, 1)
            pe.wait_ge(xn2T_ready, GROUPS)
            for k in range(-1, 4):
                tile_step(0, k)
            with pe.Fori(1, NT // 4 - 1) as u:
                for k in range(4):
                    tile_step(u, k)
            for k in range(NT - 4, NT + 1):
                tile_step(0, k)

            pe.wait_ge(yo_ready, NT)
            steps(pe, 1, step)

            def hidden1(u, k):
                e = k % E1
                for f in range(FB1):
                    n = 2 * k + f
                    wait(pe, relu_done, u * 8 + (n - 3))
                    mm(ps_s[:, n % 4, :], v1[:, F1 * e + P * f:F1 * e + P * f + P],
                       xn3T[:, sl(u * 512 + 512 * (k // E1), 512)], start=True, stop=True).then_inc(h1_done, 1)

            def rows1(u, k):
                e = k % E1
                pe.wait_ge(relu_done, u * 8 + (2 * k + 2))
                wait(pe, acc_y, u * 16 + 4 * (k - 1))
                for t in range(4):
                    for f in range(FB1):
                        c = (e * FB1 + f) * P
                        ins = mm(ps_p[:, k % 2, P * t:P * t + P], hD[k % 2][:, f, P * t:P * t + P], v2[:, c:c + P],
                                 start=(f == 0), stop=(f == FB1 - 1))
                ins.then_inc(y1_done, 1)

            pe.wait_ge(xn2T_ready, 2 * GROUPS)
            pe.wait_ge(gate_step, 2 * GROUPS)
            hidden1(0, 0)
            for k in range(1, E1 + 1):
                hidden1(0, k)
                rows1(0, k - 1)
            with pe.Fori(1, TILES // 4 - 1) as u:
                for k in range(1, E1 + 1):
                    hidden1(u, k)
                    rows1(u, k - 1)
            for k in range(1, E1):
                hidden1(TILES // 4 - 1, k)
                rows1(TILES // 4 - 1, k - 1)
            rows1(TILES // 4 - 1, E1 - 1)


def kernel(**inputs):
    import concourse.bacc as bacc
    from concourse.bass_utils import run_bass_kernel_spmd

    f = {n: np.ascontiguousarray(v) for n, v in inputs.items()}

    def blocks(w):
        d = np.zeros((DM, DM), np.float32)
        for h in range(H):
            d[h * DK:(h + 1) * DK, h * DK:(h + 1) * DK] = w.T
        return d

    arrays = {n: f[n] for n in ("L0_xattn_Wq", "L0_xattn_Wk", "L0_xattn_Wv", "L0_xattn_Wo", "L0_xattn_bo", "L1_xattn_bo",
                                "L0_ffn_W1", "L0_ffn_W2", "L1_ffn_gate_b", "L1_ffn_dp_b1", "L1_ffn_dp_b2",
                                "L1_ffn_ew1", "L1_ffn_ew2")}
    arrays |= {
        "x": f["x"].reshape(TOK, DM),
        "ctxT": np.broadcast_to(f["ctx_1024"].transpose(2, 0, 1)[:, :, None, :], (DM, B, 2, S)).reshape(DM, 2 * TOK),
        "mask": f["mask_Bx1x1xS2_if1"].reshape(B, S),
        "consts": constants(),
        "bcol": np.stack([f["L0_xattn_bq"], f["L0_xattn_bk"], f["L0_xattn_bv"]], 1),
        "gates": np.concatenate([f["g_xattn"], f["g_ffn"]]),
        "wq1": blocks(f["L1_xattn_Wq"]), "wk1": blocks(f["L1_xattn_Wk"]), "wv1": blocks(f["L1_xattn_Wv"]),
        "wo1": f["L1_xattn_Wo"].T,
        "wr0": f["L0_ffn_router_w"].T,
        "wr1": np.concatenate([f["L1_ffn_gate_w"], f["L1_ffn_dp_w1"]], 1),
        "dw2": f["L1_ffn_dp_w2"].reshape(-1),
        "b1a": f["L0_ffn_b1"].reshape(E0 * FB0, P).T,
        "b2a": f["L0_ffn_b2"].reshape(-1),
        "c1": f["L1_ffn_eb1"].reshape(E1 * FB1, P).T,
        "c2": f["L1_ffn_eb2"].reshape(-1),
    }
    arrays = {n: np.ascontiguousarray(v) for n, v in arrays.items()}
    nc = bacc.Bacc("TRN2", target_bir_lowering=False, num_devices=1)
    ins = {n: nc.dram_tensor(f"in_{n}", v.shape, mybir.dt.from_np(v.dtype), kind="ExternalInput").ap()
           for n, v in arrays.items()}
    out = nc.dram_tensor("out", (TOK, DM), F32, kind="ExternalOutput").ap()
    build(nc, ins, out)
    r = run_bass_kernel_spmd(nc, [{f"in_{n}": v for n, v in arrays.items()}], core_ids=[0])
    return r.results[0]["out"].reshape(B, S, DM)
```

```python
import numpy as np
import concourse.bass as bass
from concourse import mybir
from contextlib import ExitStack

F32 = mybir.dt.float32
F32R = mybir.dt.float32r
BF16 = mybir.dt.bfloat16
I32 = mybir.dt.int32
ALU = mybir.AluOpType
ACT = mybir.ActivationFunctionType
AX = mybir.AxisListType.X

P = 128
B, S, DM = 128, 64, 128
H, DK = 16, 8
TOK = B * S
TILES = TOK // P
GROUPS = TILES // 2
GT = 2 * P
VW = 2 * DK + 2
E0, F0 = 8, 512
FB0 = F0 // P
E1, F1 = 4, 256
FB1 = F1 // P
CH = 512
HD1 = DM // 2
ET = 256
NT = 2 * TOK // ET + E0
RE = TOK + ET
EPS = 1e-5
BIG = 3e38
NEG = -1e20
SCALES = (DK ** -0.5, DM ** -0.5)
ROUND = 12582912.0

C_ID, C_TRI, C_IND = 0, 128, 256
C_BLK = 384
C_QUAD = C_BLK + 4
C_DESC = C_QUAD + 4
C_BASE = C_DESC + E0
C_ROW = C_BASE + E0
C_THR = C_ROW + NT
C_TIE = C_THR + TOK // ET
C_ALL = C_TIE + E1 * E1


def constants():
    c = np.zeros((P, C_ALL), np.float32)
    c[:, C_ID:C_ID + P] = np.eye(P)
    c[:, C_TRI:C_TRI + P] = np.triu(np.ones((P, P)), 1)
    c[0, C_IND:C_IND + S] = 1
    c[1, C_IND + S:C_IND + P] = 1
    for i in range(4):
        c[:, C_BLK + i] = (np.arange(P) % 32) // DK == i
        c[32 * i:32 * i + 32, C_QUAD + i] = 1
    c[:, C_DESC:C_DESC + E0] = E0 - np.arange(E0)
    c[:, C_BASE:C_BASE + E0] = RE * np.arange(E0)
    c[:, C_ROW:C_ROW + NT] = ET * np.arange(NT)
    c[:, C_THR:C_THR + TOK // ET] = ET * np.arange(TOK // ET)
    c[:, C_TIE:C_ALL] = np.tril(np.ones((E1, E1)), -1).reshape(-1)
    return c


def at(u, k, mult=1, add=0, per=2):
    if isinstance(u, int):
        return mult * (per * u + k) + add
    return u * (per * mult) + (mult * k + add)


SETUP, LATE = 16 * 8, 16 * 12
LOOP0, LOOP1 = 6, GROUPS - 4


def carry(touch, value):
    if not isinstance(value, int):
        touch()


class Group:

    def __init__(self, u, k, layer):
        self.u, self.k, self.layer, self.par = u, k, layer, k % 2

    def plus(self, d):
        return Group(self.u, self.k + d, self.layer)

    def real(self):
        return not isinstance(self.u, int) or 0 <= self.k < GROUPS

    def at(self, mult=1, add=0):
        return at(self.u, self.k, mult, add)

    def count(self, mult=1, add=0):
        return at(self.u, self.k, mult, add + mult * GROUPS * self.layer)

    def half_count(self):
        return self.u * 16 + 16 * (self.k // 2 + 1 + GROUPS // 2 * self.layer)

    def block(self, add=0):
        return self.u + (self.k // 2 + add)


def ln_step(g):
    return at(g.u, g.k, 1, 3 + g.layer * (GROUPS + 4))


def wait(eng, sem, value):
    if not isinstance(value, int) or value > 0:
        eng.wait_ge(sem, value)


def build(nc, A, out):
    with ExitStack() as ctx:
        def sb(name, shape, dt=F32):
            return ctx.enter_context(nc.sbuf_tensor(name, shape, dt))

        def sem(name):
            return ctx.enter_context(nc.semaphore(name))

        ps_s = ctx.enter_context(nc.psum_tensor("ps_s", [P, 4, 512], F32))
        ps_p = ctx.enter_context(nc.psum_tensor("ps_p", [P, 2, 512], F32))
        ps_m = ctx.enter_context(nc.psum_tensor("ps_m", [P, 2, 512], F32))

        x = sb("x", [P, TILES, DM])
        xn3T = sb("xn3T", [P, TOK])
        cst = sb("cst", [P, C_ALL])
        tri = sb("tri", [P, P], BF16)
        ones = sb("ones", [P, P], BF16)
        ind = sb("ind", [2, P], BF16)
        negm = sb("negm", [2, TILES, S], BF16)
        wq = [sb(f"wq{i}", [P, DM]) for i in range(2)]
        wk = [sb(f"wk{i}", [P, DM]) for i in range(2)]
        wv = [sb(f"wv{i}", [P, DM]) for i in range(2)]
        wo = [sb(f"wo{i}", [P, DM]) for i in range(2)]
        bcol = sb("bcol", [P, 3])
        bo = [sb(f"bo{i}", [P, DM]) for i in range(2)]
        orow = [sb(f"orow{i}", [P, DM]) for i in range(2)]
        gates = sb("gates", [P, 4])
        tg = sb("tg", [P, 4])
        wr0 = sb("wr0", [P, E0])
        wr1 = sb("wr1", [P, E1 + HD1])
        gb1 = sb("gb1", [P, E1])
        db1 = sb("db1", [P, HD1])
        dw2 = sb("dw2", [P, HD1])
        db2 = sb("db2", [P, 1])
        w1a = sb("w1a", [P, E0 * F0])
        w2a = sb("w2a", [P, E0 * F0])
        b1a = sb("b1a", [P, E0 * FB0])
        v1, v2 = (w1a[:, E0 * F0 // 2 + E1 * F1 * i:E0 * F0 // 2 + E1 * F1 * (i + 1)] for i in range(2))
        c1 = sb("c1", [P, E1 * FB1])
        c2 = sb("c2", [P, E1, DM])
        ctxg = [sb(f"ctxg{i}", [P, 4, 2, S]) for i in range(2)]
        xn = [sb(f"xn{i}", [P, 2, DM]) for i in range(2)]
        xnT = [sb(f"xnT{i}", [P, GT]) for i in range(2)]
        qT = [sb(f"qT{i}", [P, 4, GT]) for i in range(2)]
        kq = sb("kq", [P, 2, GT])
        Kbd = [sb(f"Kbd{i}", [P, 4, 4, S]) for i in range(2)]
        Vbd = [sb(f"Vbd{i}", [P, 4, 8, VW]) for i in range(2)]
        Pr = [sb(f"Pr{i}", [P, 4, 512]) for i in range(2)]
        mx = [sb(f"mx{i}", [P, 4, 8]) for i in range(2)]
        PT = [sb(f"PT{i}", [P, 512]) for i in range(4)]
        rden = sb("rden", [P, 2, 8, 2])
        On = [sb(f"On{i}", [P, 2, DM]) for i in range(2)]
        OT = [sb(f"OT{i}", [P, GT]) for i in range(2)]
        xc = [sb(f"xc{i}", [P, 2, DM]) for i in range(2)]
        xn2 = [sb(f"xn2{i}", [P, 2, DM]) for i in range(2)]
        xn2T = [sb(f"xn2T{i}", [P, GT]) for i in range(2)]
        st, mv, ve, rs = sb("st", [P, 4, 6]), sb("mv", [P, 4, 2]), sb("ve", [P, 4]), sb("rs", [P, 4])
        mhalf, eps4, spare, spare_v = sb("mhalf", [P, 4]), sb("eps4", [P, 4]), sb("spare", [1, 5]), sb("spare_v", [1, 4])
        lgb = sb("lgb", [P, 4, E0])
        m1 = sb("m1", [P, 4])
        dlt = sb("dlt", [P, 4, E0])
        cand = sb("cand", [P, 4, E0])
        top = sb("top", [P, 4])
        hot = sb("hot", [P, 2, 4, E0])
        dl2 = sb("dl2", [P, 4, E0])
        m2 = sb("m2", [P, 4])
        hotb = sb("hotb", [P, 4, E0], BF16)
        seen = sb("seen", [P, E0])
        seenb = sb("seenb", [P, E0], BF16)
        hsum = sb("hsum", [P, E0])
        rank = sb("rank", [P, 4, E0])
        rsel = sb("rsel", [P, 2, 4, E0])
        posf = sb("posf", [P, 2, 4])
        pos = sb("pos", [P, 2, 4], I32)
        pos_all = sb("pos_all", [P, TILES // 4, 8])
        place = sb("place", [P, TILES // 4, 8], I32)
        m2_all = sb("m2_all", [P, TILES])
        w_all = sb("w_all", [P, TILES, 2])
        p2 = sb("p2", [P, TILES])
        den = sb("den", [P, TILES])
        cnt = sb("cnt", [P, E0])
        cnti = sb("cnti", [1, E0], I32)
        ntl = sb("ntl", [P, E0])
        nend = sb("nend", [1, E0])
        oneE = sb("oneE", [1, E0])
        jump = sb("jump", [P, E0])
        moved = Pr[1][:, 0, 0:2 * TILES].rearrange("p (b n) -> p b n", n=8)
        cge = Pr[0][:, 2, 0:E0 * TOK // ET].rearrange("p (e n) -> p e n", e=E0)
        tge, tjump = (Pr[0][0:1, i, 0:NT * (E0 - 1)].rearrange("p (n e) -> p n e", e=E0 - 1) for i in range(2))
        tef = sb("tef", [1, NT])
        trf = sb("trf", [1, NT])
        last = sb("last", [1, 1])
        tei = sb("tei", [1, NT], I32)
        tri_row = sb("tri_row", [1, NT], I32)
        zero = sb("zero", [P, ET])
        rounded = sb("rounded", [P, 8 * CH], F32R)

        def part(col, n):
            return rounded[:, col:col + n]

        w1h, w1l = ([part(F0 * (2 * j + i), F0) for i in range(2)] for j in range(2))
        xinTh, xinTl = ([part(4 * F0 + ET * (2 * j + i), ET) for i in range(2)] for j in range(2))
        v1h, v1l = part(0, E1 * F1), part(E1 * F1, E1 * F1)
        xh, xl = ([part(2 * E1 * F1 + CH * (2 * j + i), CH) for i in range(2)] for j in range(2))

        def late(col, n):
            return xn3T[:, col:col + n]

        w2s = [late(F0 * i, F0) for i in range(2)]
        hT = [late(2 * F0 + FB0 * ET * i, FB0 * ET).rearrange("p (f t) -> p f t", f=FB0) for i in range(2)]
        EX = 2 * F0 + 2 * FB0 * ET
        xin = [late(EX + ET * i, ET).rearrange("p (t d) -> p t d", t=2) for i in range(4)]
        yo = [late(EX + 4 * ET + ET * i, ET).rearrange("p (t d) -> p t d", t=2) for i in range(2)]
        b2s = [late(EX + 6 * ET + DM * i, DM) for i in range(4)]
        EX += 6 * ET + 4 * DM
        b2a = late(EX, E0 * DM)
        xs = late(EX + E0 * DM, 4 * DM).rearrange("p (t d) -> p t d", t=4)
        d_all = late(EX + (E0 + 4) * DM, TILES * E0).rearrange("p (t e) -> p t e", e=E0)
        assert TILES * S <= EX and EX + (E0 + 4) * DM + TILES * E0 <= TOK
        maskn = xn3T[0:2, 0:TILES * S].bitcast(I32).rearrange("b (t k) -> b t k", t=TILES)
        b1s = [sb(f"b1s{i}", [P, FB0]) for i in range(4)]
        ysb = [w1a[:, 2 * GT * i:2 * GT * (i + 1)].rearrange("p (s t d) -> p s t d", s=2, t=2) for i in range(2)]
        gi = [sb(f"gi{i}", [P, 4], I32) for i in range(2)]
        t1 = sb("t1", [P, 2, HD1])
        t2 = sb("t2", [P, 2, HD1])
        z_all = sb("z_all", [P, TILES])
        gl = sb("gl", [P, TILES, E1])
        big = [Pr[i][:, 0:2, :].rearrange("p a (t e f) -> p (a t) e f", e=E1, f=E1) for i in range(2)]
        sel = Pr[0][:, 2, 0:TILES * E1].rearrange("p (t e) -> p t e", e=E1)
        we = sb("we", [P, TILES, E1])
        ent, ent2, gmx, kt = (sb(n, [P, TILES]) for n in ("ent", "ent2", "gmx", "kt"))
        hD = [Kbd[i][:, :, :, :].rearrange("p a b k -> p (a b k)").rearrange("p (f t) -> p f t", f=FB1)
              for i in range(2)]

        lists = nc.dram_tensor("lists", [E0 * RE, DM], F32, kind="Internal").ap()
        louts = nc.dram_tensor("louts", [NT * ET, DM], F32, kind="Internal").ap()

        ident = cst[:, C_ID:C_ID + P]
        blk, quad = cst[:, C_BLK:C_BLK + 4], cst[:, C_QUAD:C_QUAD + 4]
        desc = cst[:, C_DESC:C_DESC + E0]
        base = cst[:, C_BASE:C_BASE + E0]
        bank6, bank7 = ps_m[:, 0, :], ps_m[:, 1, :]
        lg_bank, kq_bank, rk_bank, v_bank = (ps_s[:, i, :] for i in range(4))

        setup_in, late_in, x_in0, x_in1, experts_in = (sem(n) for n in (
            "setup_in", "late_in", "x_in0", "x_in1", "experts_in"))
        ctx_in = [sem("ctx_in0"), sem("ctx_in1")]
        folded_done, folded_ready = sem("folded_done"), sem("folded_ready")
        tanh_done, consts_done, wo_scaled, bv_done, orow_done = (sem(n) for n in (
            "tanh_done", "consts_done", "wo_scaled", "bv_done", "orow_done"))
        lnq_st, lnq_mv, xn_ready = (sem(n) for n in ("lnq_st", "lnq_mv", "xn_ready"))
        lnf_st, lnf_mv, xn2_ready = (sem(n) for n in ("lnf_st", "lnf_mv", "xn2_ready"))
        ln_ve, ln_rs = sem("ln_ve"), sem("ln_rs")
        xt_done, kq_done, v_done, s_done, pt_done, pv_done = (sem(n) for n in (
            "xt_done", "kq_done", "v_done", "s_done", "pt_done", "pv_done"))
        ot_done, out_done, xt2_done, lg_done, rk_done = (sem(n) for n in (
            "ot_done", "out_done", "xt2_done", "lg_done", "rk_done"))
        xnT_ready, kq_ready, spread, v_ready = (sem(n) for n in ("xnT_ready", "kq_ready", "spread", "v_ready"))
        max_done, sub_done, exp_done, pt_ready = (sem(n) for n in ("max_done", "sub_done", "exp_done", "pt_ready"))
        rec_done, on_ready, ot_ready, xc_ready, x1_ready = (sem(n) for n in (
            "rec_done", "on_ready", "ot_ready", "xc_ready", "x1_ready"))
        xn2T_ready, lg_read, gate_step = (sem(n) for n in ("xn2T_ready", "lg_read", "gate_step"))
        route, hot_ready, rank_read, seen_ready, pos_ready, xs_ready, scattered = (sem(n) for n in (
            "route", "hot_ready", "rank_read", "seen_ready", "pos_ready", "xs_ready", "scattered"))
        place2, place_ready, move_step = sem("place2"), sem("place_ready"), sem("move_step")
        cnt_done, cnti_ready, plan_step, plan_ready, zeros_in = (sem(n) for n in (
            "cnt_done", "cnti_ready", "plan_step", "plan_ready", "zeros_in"))
        dexp_done, w_step, w_ready = (sem(n) for n in ("dexp_done", "w_step", "w_ready"))
        rows_in = [sem(f"rows_in{i}") for i in range(4)]
        rows_out = [sem("rows_out0"), sem("rows_out1")]
        w1_ready, w2_ready, xinT_ready, yo_ready = (sem(n) for n in ("w1_ready", "w2_ready", "xinT_ready", "yo_ready"))
        b2_ready = sem("b2_ready")
        et_done, h_done, gelu_done, y_done = (sem(n) for n in ("et_done", "h_done", "gelu_done", "y_done"))
        gathered = [sem("gathered0"), sem("gathered1")]
        gi_ready, comb_step, comb_done = (sem(n) for n in ("gi_ready", "comb_step", "comb_done"))
        ent_step, ent_act, gates_step, gates_act, gates_ready = (sem(n) for n in (
            "ent_step", "ent_act", "gates_step", "gates_act", "gates_ready"))
        xinTh_ready, w1l_ready = sem("xinTh_ready"), sem("w1l_ready")
        v_in = sem("v_in")
        v1_split, x_split = sem("v1_split"), sem("x_split")
        h1_done, relu_done, y1_done, acc_b, acc_y, out_st = (sem(n) for n in (
            "h1_done", "relu_done", "y1_done", "acc_b", "acc_y", "out_st"))

        drained = {
            "OT": (ot_ready, 1, 1), "OUT": (x1_ready, 1, 1), "O0": (on_ready, 2, 1), "O1": (on_ready, 2, 2),
            "XT": (xnT_ready, 1, 1),
            "XT2": (xn2T_ready, 1, 1)}

        def jobs(bank, g):
            if bank == 6:
                found = [("OT", g.plus(-2)), ("OUT", g.plus(-2)), ("O1", g.plus(-1))]
            else:
                found = [("XT", g.plus(1)), ("XT2", g.plus(-3)), ("O0", g.plus(-1))]
            return [j for j in found if j[1].real()]

        def bank_free(pe, bank, g, name):
            names = jobs(bank, g)
            i = [n for n, _ in names].index(name)
            before = names[:i]
            for back in range(1, 4):
                before = before or jobs(bank, g.plus(-back))
            if not before:
                return
            last, m = before[-1]
            s_, mult, add = drained[last]
            pe.wait_ge(s_, m.count(mult, add))

        def scores_read(pe, g, q):
            pe.wait_ge(sub_done, (g if g.real() else Group(0, GROUPS - 1, g.layer)).count(4, q + 1))

        def steps(eng, layer, step):
            for s in range(-3, LOOP0):
                step(Group(0, s, layer))
            with eng.Fori(0, (LOOP1 - LOOP0) // 2) as u:
                step(Group(u, LOOP0, layer))
                step(Group(u, LOOP0 + 1, layer))
            for s in range(LOOP1, GROUPS + 4):
                step(Group(0, s, layer))

        def sl(t, n=1):
            return slice(t, t + n) if isinstance(t, int) else bass.ds(t, n)

        block = ctx.enter_context(nc.Block())

        @block.sync
        def _(sp):
            def load_ctx(g):
                if g.layer == 0:
                    wait(sp, v_done, g.count(1, -1))
                else:
                    sp.wait_ge(s_done, g.count(4, -4))
                sp.dma_start(ctxg[g.par][:, :, :, :].rearrange("p b i k -> p (b i k)"),
                             A["ctxT"][:, sl(g.at(2 * GT), 2 * GT)]).then_inc(ctx_in[g.par], 16)

            xv = A["x"].rearrange("(t p) d -> p t d", p=P)
            sp.dma_start(x[:, 0:8, :], xv[:, 0:8, :]).then_inc(x_in0, 16)
            for dst, src in ((cst[:, :], A["consts"]), (gates[:, :], A["gates"].partition_broadcast(P)),
                             (wo[0][:, :], A["L0_xattn_Wo"]), (bcol[:, :], A["bcol"]),
                             (bo[0][:, :], A["L0_xattn_bo"].partition_broadcast(P)), (wk[0][:, :], A["L0_xattn_Wk"]),
                             (wq[0][:, :], A["L0_xattn_Wq"]), (wv[0][:, :], A["L0_xattn_Wv"])):
                sp.dma_start(dst, src).then_inc(setup_in, 16)
            for par in range(2):
                load_ctx(Group(0, par, 0))
            sp.dma_start(x[:, 8:TILES, :], xv[:, 8:TILES, :]).then_inc(x_in1, 16)
            for dst, src in ((wr0[:, :], A["wr0"]), (maskn, A["mask"].rearrange("(t b) k -> b t k", b=2)),
                             (bo[1][:, :], A["L1_xattn_bo"].partition_broadcast(P)), (wo[1][:, :], A["wo1"]),
                             (wq[1][:, :], A["wq1"]), (wk[1][:, :], A["wk1"]), (wv[1][:, :], A["wv1"]),
                             (wr1[:, :], A["wr1"]),
                             (gb1[:, :], A["L1_ffn_gate_b"].partition_broadcast(P)),
                             (db1[:, :], A["L1_ffn_dp_b1"].partition_broadcast(P)),
                             (dw2[:, :], A["dw2"].partition_broadcast(P)),
                             (db2[:, :], A["L1_ffn_dp_b2"].partition_broadcast(P))):
                sp.dma_start(dst, src).then_inc(late_in, 16)

            def step(g):
                if g.plus(2).real() and (g.layer or not isinstance(g.u, int) or g.k >= 0):
                    load_ctx(g.plus(2))
                if g.layer == 0 and isinstance(g.u, int) and g.k == 0:
                    for dst, src in ((w1a[:, :].rearrange("p (e f) -> p e f", e=E0), A["L0_ffn_W1"].rearrange("e d f -> d e f")),
                                     (w2a[:, :].rearrange("p (e f d) -> p (e f) d", e=E0, f=FB0),
                                      A["L0_ffn_W2"].rearrange("e (f p) d -> p (e f) d", p=P)),
                                     (b1a[:, :], A["b1a"]),
                                     (b2a, A["b2a"].partition_broadcast(P)),
                                     (c1[:, :], A["c1"]),
                                     (c2[:, :, :].rearrange("p e d -> p (e d)"), A["c2"].partition_broadcast(P))):
                        sp.dma_start(dst, src).then_inc(experts_in, 16)

            steps(sp, 0, step)
            sp.wait_ge(cnti_ready, 1)
            for e in range(E0):
                n = sp.value_load(cnti[0:1, e:e + 1], min_val=0, max_val=TOK)
                sp.dma_start(lists[bass.ds(n + e * RE, ET), :].rearrange("(p b) d -> p (b d)", p=P),
                             zero[:, :]).then_inc(zeros_in, 16)
            sp.wait_ge(zeros_in, 16 * E0)
            sp.wait_ge(plan_ready, 1)
            sp.wait_ge(scattered, 16 * 8 * (TILES // 4))

            def load_rows(u, k):
                wait(sp, et_done, at(u, k, 1, -3, 4))
                r = sp.value_load(tri_row[0:1, sl(at(u, k, per=4))], min_val=0, max_val=E0 * RE - ET)
                sp.dma_start(xin[k % 4], lists[bass.ds(r, ET), :].rearrange("(t p) d -> p t d", p=P)).then_inc(
                    rows_in[k % 4], 16)

            for k in range(4):
                load_rows(0, k)
            with sp.Fori(1, NT // 4) as u:
                for k in range(4):
                    load_rows(u, k)
            sp.wait_ge(yo_ready, NT)

            for dst, src in ((v1.rearrange("p (e f) -> p e f", e=E1), A["L1_ffn_ew1"].rearrange("e d f -> d e f")),
                             (v2.rearrange("p (e f d) -> p (e f) d", e=E1, f=FB1),
                              A["L1_ffn_ew2"].rearrange("e (f p) d -> p (e f) d", p=P))):
                sp.dma_start(dst, src).then_inc(v_in, 16)
            steps(sp, 1, step)

            ov = out.rearrange("(t p) d -> p t d", p=P)

            def store_out(c):
                sp.wait_ge(acc_y, c * (4 * E1) + 4 * E1)
                sp.dma_start(ov[:, sl(c * 4, 4), :], x[:, sl(c * 4, 4), :]).then_inc(out_st, 16)

            with sp.Fori(0, TILES // 4) as c:
                store_out(c)
            sp.wait_ge(out_st, 16 * (TILES // 4))

        @block.gpsimd
        def _(pool):
            def touch(i):
                nc.gpsimd.tensor_tensor(spare[:, i:i + 1], spare[:, 4:5], spare[:, 4:5], ALU.add)

            def inverse_deviations(g):
                if g.plus(-2).real():
                    pool.wait_ge(lnf_mv, g.plus(-2).count(2, 2))
                if g.plus(2).real():
                    pool.wait_ge(lnq_mv, g.plus(2).count(2, 2))
                nc.gpsimd.tensor_tensor(ve[:, :], mv[:, :, 1], eps4[:, :], ALU.add).then_inc(ln_ve, 1)
                pool.wait_ge(ln_ve, ln_step(g))
                nc.gpsimd.tensor_tensor(rs[:, :], ve[:, :], mhalf[:, :], ALU.pow).then_inc(ln_rs, 1)

            def rows_plus_constant(g):
                if g.layer == 0:
                    if isinstance(g.u, int) and g.k == 4:
                        pool.wait_ge(x_in1, 16)
                else:
                    pool.wait_ge(comb_done, g.at(2, 2))
                wait(pool, x1_ready, g.count(1, -1))
                nc.gpsimd.tensor_tensor(xc[g.par][:, :, :], x[:, sl(g.at(2), 2), :],
                                        orow[g.layer][:, :].unsqueeze(1).to_broadcast([P, 2, DM]),
                                        ALU.add).then_inc(xc_ready, 1)

            def spread_keys(g):
                if g.layer == 0:
                    pool.wait_ge(kq_ready, g.count(1, 1))
                    keys = kq[:, 0, :].rearrange("p (b k) -> p b k", b=4)
                else:
                    pool.wait_ge(ctx_in[g.par], g.half_count())
                    keys = ctxg[g.par][:, :, 0, :]
                wait(pool, s_done, g.count(4, -4))
                nc.gpsimd.tensor_tensor(Kbd[g.par][:, :, :, :], keys.unsqueeze(2).to_broadcast([P, 4, 4, S]),
                                        blk.unsqueeze(1).unsqueeze(3).to_broadcast([P, 4, 4, S]), ALU.mult).then_inc(spread, 1)

            def spread_queries(g):
                pool.wait_ge(kq_ready, g.count(1, 1))
                nc.gpsimd.tensor_tensor(qT[g.par][:, :, :], kq[:, 1, :].unsqueeze(1).to_broadcast([P, 4, GT]),
                                        quad.unsqueeze(2).to_broadcast([P, 4, GT]), ALU.mult).then_inc(spread, 1)

            def scatter(g, slot):
                pool.wait_ge(pos_ready, g.block(1))
                pool.wait_ge(xs_ready, g.block(1) * 2)
                carry(lambda: touch(slot), g.block(1))
                for t in range(4):
                    nc.gpsimd.indirect_dma_start(lists, bass.IndirectOffsetOnAxis(ap=pos[:, slot, t:t + 1], axis=0),
                                                 xs[:, t, :], None).then_inc(scattered, 16)

            def gather(g):
                i = g.par
                wait(pool, comb_done, g.at(2, -2))
                carry(lambda: touch(2), g.at())
                nc.gpsimd.tensor_copy(gi[i][:, :].rearrange("p (b s t) -> p b s t", b=1, s=2),
                                      place[:, sl(g.block(0)), :].rearrange("p b (s t) -> p b s t", s=2)[:, :, :, 2 * i:2 * i + 2]
                                      ).then_inc(gi_ready, 1)
                pool.wait_ge(gi_ready, g.at(1, 1))
                carry(lambda: touch(3), g.at())
                for s_ in range(2):
                    for t in range(2):
                        c = 2 * s_ + t
                        nc.gpsimd.indirect_dma_start(ysb[i][:, s_, t, :], None, louts,
                                                     bass.IndirectOffsetOnAxis(ap=gi[i][:, c:c + 1], axis=0)
                                                     ).then_inc(gathered[i], 16)

            def step(g):
                def have(d):
                    return g.plus(d).real()

                if have(-1):
                    rows_plus_constant(g.plus(-1))
                if g.layer == 0 and g.par and have(-4):
                    scatter(g.plus(-4), 0)
                if have(1):
                    spread_keys(g.plus(1))
                if g.layer == 1 and have(1):
                    spread_queries(g.plus(1))
                if have(-2) or have(2):
                    inverse_deviations(g)
                if g.layer == 0 and have(1):
                    spread_queries(g.plus(1))
                if g.layer == 0 and g.par and have(-4):
                    scatter(g.plus(-4), 1)
                if g.layer == 1 and have(3):
                    gather(g.plus(3))

            pool.wait_ge(setup_in, SETUP)
            pool.wait_ge(x_in0, 16)
            pool.wait_ge(orow_done, 1)
            steps(pool, 0, step)

            def store_rows(u, k):
                pool.wait_ge(yo_ready, at(u, k, 1, 1, 4))
                pool.dma_start(louts[sl(at(u, k, ET, 0, 4), ET), :].rearrange("(t p) d -> p t d", p=P),
                               yo[k % 2]).then_inc(rows_out[k % 2], 16)

            def low_weights(u, k):
                e = pool.value_load(tei[0:1, sl(at(u, k, per=4))], min_val=0, max_val=E0 - 1)
                pool.wait_ge(w1_ready, at(u, k, 2, 1, 4))
                touch(k % 4)
                nc.gpsimd.tensor_tensor(w1l[k % 2], w1a[:, bass.ds(e * F0, F0)], w1h[k % 2].bitcast(F32),
                                        ALU.subtract).then_inc(w1l_ready, 1)

            pool.wait_ge(plan_ready, 1)
            low_weights(0, 0)
            low_weights(0, 1)
            with pool.Fori(0, NT // 4 - 1) as u:
                for k in range(4):
                    low_weights(u, k + 2)
                    store_rows(u, k)
            for k in range(NT - 4, NT):
                if k + 2 < NT:
                    low_weights(0, k + 2)
                store_rows(0, k)
            pool.wait_ge(rows_out[0], 16 * (NT // 2))
            pool.wait_ge(rows_out[1], 16 * (NT // 2))
            pool.wait_ge(place_ready, 1)
            pool.wait_ge(orow_done, 2)
            steps(pool, 1, step)

            def split(src, high, low, out_sem, number, spot=0):
                n = src.shape[1]
                none = zero[:, :].unsqueeze(1).to_broadcast([P, n // ET, ET])
                nc.gpsimd.tensor_tensor(high.rearrange("p (a b) -> p a b", b=ET), src.rearrange("p (a b) -> p a b", b=ET),
                                        none, ALU.add).then_inc(out_sem, 1)
                pool.wait_ge(out_sem, number)
                carry(lambda: touch(spot), number)
                nc.gpsimd.tensor_tensor(low, src, high.bitcast(F32), ALU.subtract).then_inc(out_sem, 1)

            pool.wait_ge(v_in, 16 * 2)
            split(v1, v1h, v1l, v1_split, 1)
            pool.wait_ge(xn2T_ready, 2 * GROUPS)

            def split_chunk(u, k):
                if not isinstance(u, int):
                    pool.wait_ge(h1_done, u * (4 * E1) + (2 * E1 * (k + 1 - 2)))
                    touch(k)
                split(xn3T[:, sl(at(u, k, CH), CH)], xh[k], xl[k], x_split, at(u, k, 2, 1), 2 + k)

            split_chunk(0, 0)
            split_chunk(0, 1)
            with pool.Fori(1, TOK // CH // 2) as u:
                split_chunk(u, 0)
                split_chunk(u, 1)

        @block.scalar
        def _(act):
            def copy(dst, src, bias=None):
                if bias is None:
                    return nc.scalar.activation(dst, src, ACT.Copy)
                return nc.scalar.activation(dst, src, ACT.Identity, bias=bias)

            def heads_out(g):
                act.wait_ge(ot_done, g.count(1, 1))
                wait(act, out_done, g.count(1, -1))
                copy(OT[g.par][:, :], bank6[:, 0:GT]).then_inc(ot_ready, 1)

            def tokens_in(g):
                act.wait_ge(xt_done, g.count(1, 1))
                wait(act, kq_done, g.count(1, -1))
                copy(xnT[g.par][:, :], bank7[:, 0:GT]).then_inc(xnT_ready, 1)

            def probs_out(g, c):
                act.wait_ge(pt_done, g.count(4, c + 1))
                wait(act, pv_done, g.count(4, c - 3))
                copy(PT[c][:, :], ps_p[:, c % 2, :]).then_inc(pt_ready, 1)

            def exps(g, q):
                act.wait_ge(sub_done, g.count(4, q + 1))
                nc.scalar.activation(Pr[g.par][:, q, :], Pr[g.par][:, q, :], ACT.Exp,
                                     scale=SCALES[g.layer]).then_inc(exp_done, 1)

            def keys_queries(g):
                act.wait_ge(kq_done, g.count(1, 1))
                wait(act, spread, g.count(2, 0))
                if g.layer == 0:
                    copy(kq[:, 0, :], kq_bank[:, 0:GT], bcol[:, 1:2])
                    copy(kq[:, 1, :], kq_bank[:, GT:2 * GT], bcol[:, 0:1]).then_inc(kq_ready, 1)
                else:
                    copy(kq[:, 1, :], kq_bank[:, GT:2 * GT]).then_inc(kq_ready, 1)

            def values(g):
                act.wait_ge(v_done, g.count(1, 1))
                v = v_bank.rearrange("p (b j c) -> p b j c", b=4, j=8)
                wait(act, pv_done, g.count(4, -4))
                for i in range(2):
                    r = slice(S * i, S * i + S)
                    c = slice(DK * i, DK * i + DK)
                    ins = copy(Vbd[g.par][r, :, :, c], v[r, :, :, c])
                ins.then_inc(v_ready, 1)

            def collect_rows(g):
                act.wait_ge(xn2_ready, g.count(2, 2))
                wait(act, scattered, g.block(0) * (16 * 8))
                for i in range(2):
                    copy(xs[:, 2 * i:2 * i + 2, :], xn2[i][:, :, :]).then_inc(xs_ready, 1)

            def tokens2(g):
                act.wait_ge(xt2_done, g.count(1, 1))
                wait(act, lg_done, g.count(1, -1))
                if g.layer == 1:
                    copy(xn3T[:, sl(g.at(GT), GT)], bank7[:, 0:GT])
                copy(xn2T[g.par][:, :], bank7[:, 0:GT]).then_inc(xn2T_ready, 1)

            def step(g):
                def have(d):
                    return g.plus(d).real()

                if have(1):
                    tokens_in(g.plus(1))
                if have(-3):
                    tokens2(g.plus(-3))
                if have(0):
                    exps(g, 0)
                    exps(g, 1)
                if have(-2):
                    heads_out(g.plus(-2))
                if have(1):
                    keys_queries(g.plus(1))
                for c in range(4):
                    if have(-1):
                        probs_out(g.plus(-1), c)
                    if have(0) and c in (1, 2):
                        exps(g, 1 + c)
                    if g.layer == 0 and g.par == 0 and have(-3) and c == 2:
                        collect_rows(g.plus(-3))
                if have(1):
                    values(g.plus(1))

            act.wait_ge(setup_in, SETUP)
            nc.scalar.activation(tg[:, :], gates[:, :], ACT.Tanh).then_inc(tanh_done, 1)
            act.wait_ge(consts_done, 1)
            act.wait_ge(plan_step, 1)
            steps(act, 0, step)

            act.wait_ge(place2, TILES // 4)
            nc.scalar.activation(d_all, d_all, ACT.Exp).then_inc(dexp_done, 1)
            nc.scalar.activation(p2[:, :], m2_all[:, :], ACT.Exp).then_inc(dexp_done, 1)

            def high_rows(u, k):
                act.wait_ge(et_done, at(u, k, 1, 1, 4))
                wait(act, h_done, at(u, k, 2, -2, 4))
                copy(xinTh[k % 2], ps_p[:, k % 2, 0:ET]).then_inc(xinTh_ready, 1)

            def gelu(u, k):
                i = k % 2
                act.wait_ge(w1_ready, at(u, k, 2, 2, 4))
                wait(act, y_done, at(u, k, 1, -1, 4))
                for f in range(FB0):
                    if f % 2 == 0:
                        act.wait_ge(h_done, at(u, k, 2, 1 + f // 2, 4))
                    nc.scalar.activation(hT[i][:, f, :], ps_s[:, 2 * i + f // 2, ET * (f % 2):ET * (f % 2 + 1)],
                                         ACT.Gelu_apprx_tanh, bias=b1s[k % 4][:, f:f + 1]).then_inc(gelu_done, 1)

            high_rows(0, 0)
            for k in range(4):
                high_rows(0, k + 1)
                gelu(0, k)
            with act.Fori(1, NT // 4 - 1) as u:
                for k in range(4):
                    high_rows(u, k + 1)
                    gelu(u, k)
            for k in range(NT - 4, NT):
                if k + 1 < NT:
                    high_rows(0, k + 1)
                gelu(0, k)

            act.wait_ge(rows_out[0], 16 * (NT // 2))
            act.wait_ge(rows_out[1], 16 * (NT // 2))
            steps(act, 1, step)

            act.wait_ge(ent_step, 2)
            nc.scalar.activation(ent2[:, :], ent2[:, :], ACT.Exp, scale=-1.0).then_inc(ent_act, 1)
            act.wait_ge(gates_step, 2)
            nc.scalar.activation(we[:, :, :], we[:, :, :], ACT.Exp).then_inc(gates_act, 1)
            act.wait_ge(ent_act, 1)
            nc.scalar.activation(ent2[:, :], ent2[:, :], ACT.Ln, bias=1.0).then_inc(ent_act, 1)

            def relu(u, k):
                wait(act, y1_done, u * 4 + (k - 1))
                for f in range(FB1):
                    act.wait_ge(h1_done, u * 8 + (2 * k + f + 1))
                    nc.scalar.activation(hD[k % 2][:, f, :], ps_s[:, (2 * k + f) % 4, :], ACT.Relu,
                                         bias=c1[:, (k % 4) * FB1 + f:(k % 4) * FB1 + f + 1]).then_inc(relu_done, 1)

            for k in range(E1):
                relu(0, k)
            with act.Fori(1, TILES // 4) as u:
                for k in range(E1):
                    relu(u, k)

        @block.vector
        def _(dve):
            V = nc.vector

            def touch(i):
                V.memset(spare_v[:, i:i + 1], 0.0)

            def flat(ap):
                return ap.rearrange("p a d -> p (a d)")

            def statistics(g, slot, s_st, s_mv):
                carry(lambda: touch(slot), g.at())
                for j in range(2):
                    V.bn_stats(st[:, slot + j, :], flat(x[:, sl(g.at(2, j)), :])).then_inc(s_st, 1)
                dve.wait_ge(s_st, g.count(2, 2))
                carry(lambda: touch(slot + 1), g.at())
                for j in range(2):
                    V.bn_aggr(mv[:, slot + j, :], st[:, slot + j, :]).then_inc(s_mv, 1)

            def normalise(g, slot, dst, step_, s_out):
                dve.wait_ge(ln_rs, ln_step(step_))
                for j in range(2):
                    V.tensor_scalar(dst[:, j, :], flat(x[:, sl(g.at(2, j)), :]), mv[:, slot + j, 0:1],
                                    rs[:, slot + j:slot + j + 1], ALU.subtract, ALU.mult).then_inc(s_out, 1)

            def statistics_in(g):
                if g.layer == 0:
                    if isinstance(g.u, int) and g.k in (0, 4):
                        dve.wait_ge(x_in0 if g.k == 0 else x_in1, 16)
                else:
                    dve.wait_ge(comb_done, g.at(2, 2))
                wait(dve, xn_ready, g.count(2, 0))
                statistics(g, 2, lnq_st, lnq_mv)

            def normalise_in(g, step_):
                wait(dve, xt_done, g.count(1, -1))
                normalise(g, 2, xn[g.par], step_, xn_ready)

            def statistics_mid(g):
                dve.wait_ge(x1_ready, g.count(1, 1))
                wait(dve, xn2_ready, g.count(2, 0))
                statistics(g, 0, lnf_st, lnf_mv)

            def normalise_mid(g, step_):
                wait(dve, xt2_done, g.count(1, -1))
                if g.layer == 0:
                    wait(dve, xs_ready, g.block(0) * 2)
                normalise(g, 0, xn2[g.par], step_, xn2_ready)

            def residual(g):
                dve.wait_ge(out_done, g.count(1, 1))
                dve.wait_ge(xc_ready, g.count(1, 1))
                V.tensor_tensor(x[:, sl(g.at(2), 2), :], bank6[:, 0:GT].rearrange("p (t d) -> p t d", t=2),
                                xc[g.par][:, :, :], ALU.add).then_inc(x1_ready, 1)

            def less_maximum(g, half):
                def view(ap):
                    return ap.rearrange("p (h k) -> p h k", k=S)

                def maximum(q):
                    dve.wait_ge(s_done, g.count(4, q + 1))
                    V.tensor_reduce(mx[g.par][:, q, :], view(ps_s[:, q, :]), AX, ALU.max).then_inc(max_done, 1)

                def subtract(q):
                    dve.wait_ge(max_done, g.count(4, q + 1))
                    wait(dve, pv_done, g.count(4, -4))
                    V.tensor_tensor(view(Pr[g.par][:, q, :]), view(ps_s[:, q, :]),
                                    mx[g.par][:, q, :].unsqueeze(2).to_broadcast([P, 8, S]),
                                    ALU.subtract).then_inc(sub_done, 1)

                for q in range(2 * half, 2 * half + 2):
                    maximum(q)
                    subtract(q)

            def heads(g, pr):
                o = (bank7, bank6)[pr][:, 0:8 * 2 * VW].rearrange("p (j b c) -> p j b c", j=8, b=2)
                dve.wait_ge(pv_done, g.count(4, 2 * pr + 2))
                V.reciprocal(rden[:, pr, :, :], o[:, :, 0, 2 * DK:VW]).then_inc(rec_done, 1)
                dve.wait_ge(rec_done, g.count(2, pr + 1))
                wait(dve, ot_done, g.count(1, -1))
                for b in range(2):
                    r = slice(S * b, S * b + S)
                    ins = V.tensor_tensor(On[g.par][r, pr, :].rearrange("p (j h d) -> p j h d", j=8, h=2),
                                          o[r, :, b, 0:2 * DK].rearrange("p j (h d) -> p j h d", h=2),
                                          rden[r, pr, :, :].unsqueeze(3).to_broadcast([S, 8, 2, DK]), ALU.mult)
                ins.then_inc(on_ready, 1)

            def router_logits(g):
                dve.wait_ge(lg_done, g.count(1, 1))
                V.tensor_copy(lgb[:, 2 * g.par:2 * g.par + 2, :],
                              lg_bank[:, 0:2 * E0].rearrange("p (t e) -> p t e", t=2)).then_inc(lg_read, 1)

            ROUTE = 15

            def chain(sem_, start):
                n = [0]

                def link(ins):
                    n[0] += 1
                    ins.then_inc(sem_, 1)
                    dve.wait_ge(sem_, start + n[0])
                return link

            def route_tops(g):
                link = chain(route, g.block(0) * ROUTE)
                desc4 = desc.unsqueeze(1).to_broadcast([P, 4, E0])

                def b4(ap):
                    return ap.unsqueeze(2).to_broadcast([P, 4, E0])

                dve.wait_ge(lg_read, g.count(1, 1))
                link(V.tensor_reduce(m1[:, :], lgb[:, :, :], AX, ALU.max))
                link(V.tensor_tensor(dlt[:, :, :], lgb[:, :, :], b4(m1[:, :]), ALU.subtract))
                link(V.scalar_tensor_tensor(cand[:, :, :], dlt[:, :, :], 0.0, desc4, ALU.is_equal, ALU.mult))
                link(V.tensor_reduce(top[:, :], cand[:, :, :], AX, ALU.max))
                link(V.tensor_tensor(hot[:, 0, :, :], desc4, b4(top[:, :]), ALU.is_equal))
                link(V.scalar_tensor_tensor(dl2[:, :, :], hot[:, 0, :, :], -BIG, dlt[:, :, :], ALU.mult, ALU.add))
                link(V.tensor_reduce(m2[:, :], dl2[:, :, :], AX, ALU.max))
                link(V.tensor_tensor(cand[:, :, :], dl2[:, :, :], b4(m2[:, :]), ALU.is_equal))
                link(V.tensor_tensor(cand[:, :, :], cand[:, :, :], desc4, ALU.mult))
                link(V.tensor_reduce(top[:, :], cand[:, :, :], AX, ALU.max))
                link(V.tensor_tensor(hot[:, 1, :, :], desc4, b4(top[:, :]), ALU.is_equal))
                V.tensor_tensor(hotb[:, :, :], hot[:, 0, :, :], hot[:, 1, :, :], ALU.add).then_inc(hot_ready, 1)
                V.tensor_reduce(hsum[:, :], hot[:, :, :, :].rearrange("p s t e -> p e (s t)"), AX, ALU.add).then_inc(route, 1)
                V.tensor_copy(d_all[:, sl(g.block(0) * 4, 4), :], dlt[:, :, :])
                V.tensor_copy(m2_all[:, sl(g.block(0) * 4, 4)], m2[:, :]).then_inc(place2, 1)

            def route_places(g):
                dve.wait_ge(rk_done, g.block(1))
                V.tensor_tensor(rank[:, :, :], rk_bank[:, 0:4 * E0].rearrange("p (t e) -> p t e", t=4),
                                base.unsqueeze(1).to_broadcast([P, 4, E0]), ALU.add).then_inc(rank_read, 1)
                dve.wait_ge(route, g.block(0) * ROUTE + 12)
                V.tensor_tensor(seen[:, :], seen[:, :], hsum[:, :], ALU.add).then_inc(route, 1)
                dve.wait_ge(rank_read, g.block(1))
                V.tensor_tensor(rsel[:, :, :, :].rearrange("p s t e -> p s (t e)"),
                                hot[:, :, :, :].rearrange("p s t e -> p s (t e)"),
                                rank[:, :, :].rearrange("p t e -> p (t e)").unsqueeze(1).to_broadcast([P, 2, 4 * E0]),
                                ALU.mult).then_inc(route, 1)
                dve.wait_ge(route, g.block(0) * ROUTE + 14)
                V.tensor_copy(seenb[:, :], seen[:, :]).then_inc(seen_ready, 1)
                V.tensor_reduce(posf[:, :, :], rsel[:, :, :, :], AX, ALU.add).then_inc(route, 1)
                dve.wait_ge(route, g.block(0) * ROUTE + 15)
                wait(dve, scattered, g.block(0) * (16 * 8))
                V.tensor_copy(pos[:, :, :], posf[:, :, :]).then_inc(pos_ready, 1)
                V.tensor_copy(pos_all[:, sl(g.block(0)), :], posf[:, :, :].rearrange("p (b s) t -> p b (s t)", b=1))

            def gate_logits(g):
                lg = lg_bank[:, 0:2 * (E1 + HD1)].rearrange("p (t e) -> p t e", t=2)
                dve.wait_ge(lg_done, g.count(1, 1))
                V.tensor_tensor(gl[:, sl(g.at(2), 2), :], lg[:, :, 0:E1],
                                gb1[:, :].unsqueeze(1).to_broadcast([P, 2, E1]), ALU.add)
                V.tensor_tensor(t1[:, :, :], lg[:, :, E1:], db1[:, :].unsqueeze(1).to_broadcast([P, 2, HD1]),
                                ALU.add).then_inc(lg_read, 1)
                dve.wait_ge(lg_read, g.count(1, 1))
                V.scalar_tensor_tensor(t2[:, :, :], t1[:, :, :], 0.0, dw2[:, :].unsqueeze(1).to_broadcast([P, 2, HD1]),
                                       ALU.max, ALU.mult).then_inc(gate_step, 1)
                dve.wait_ge(gate_step, g.at(2, 1))
                V.tensor_reduce(z_all[:, sl(g.at(2), 2)], t2[:, :, :], AX, ALU.add).then_inc(gate_step, 1)

            def combine(g):
                dve.wait_ge(gathered[g.par], g.u * 64 + 64 * (g.k // 2 + 1))
                for s_ in range(2):
                    for t in range(2):
                        tile = flat(x[:, sl(g.at(2, t)), :])
                        V.scalar_tensor_tensor(tile, ysb[g.par][:, s_, t, :], flat(w_all[:, sl(g.at(2, t)), s_:s_ + 1]), tile,
                                               ALU.mult, ALU.add).then_inc((comb_step, comb_done)[s_], 1)
                    if s_ == 0:
                        dve.wait_ge(comb_step, g.at(2, 2))

            def step(g):
                def have(d):
                    return g.plus(d).real()

                if g.layer == 0 and isinstance(g.u, int) and g.k == 3:
                    layer1_constants()
                if g.layer == 0 and g.par and have(-4):
                    route_places(g.plus(-4))
                if have(0):
                    less_maximum(g, 0)
                if have(0):
                    less_maximum(g, 1)
                if have(-3):
                    (router_logits, gate_logits)[g.layer](g.plus(-3))
                if have(-2):
                    residual(g.plus(-2))
                if g.layer == 1 and have(2):
                    combine(g.plus(2))
                if have(-2):
                    statistics_mid(g.plus(-2))
                if have(2):
                    statistics_in(g.plus(2))
                if g.layer == 0 and g.par == 0 and have(-3):
                    route_tops(g.plus(-3))
                if have(-1):
                    heads(g.plus(-1), 0)
                if have(-2):
                    normalise_mid(g.plus(-2), g)
                if have(2):
                    normalise_in(g.plus(2), g)
                if have(-1):
                    heads(g.plus(-1), 1)

            def layer1_constants():
                dve.wait_ge(late_in, LATE)
                V.tensor_scalar(negm[:, :, :], maskn, 0, NEG, ALU.is_equal, ALU.mult)
                V.tensor_scalar(wo[1][:, :], wo[1][:, :], tg[:, 1:2], None, ALU.mult).then_inc(wo_scaled, 1)
                V.tensor_scalar(orow[1][:, :], bo[1][:, :], tg[:, 1:2], None, ALU.mult).then_inc(orow_done, 1)

            for i in range(2):
                V.memset(Vbd[i][:, :, :, :], 0.0)
            V.memset(ones[:, :], 1.0)
            V.memset(mhalf[:, :], -0.5)
            V.memset(eps4[:, :], EPS)
            V.memset(mv[:, :, :], 1.0)
            V.memset(spare[:, :], 0.0)
            V.memset(zero[:, :], 0.0)
            V.memset(seen[:, :], 0.0)
            V.memset(seenb[:, :], 0.0)
            V.memset(oneE[:, :], 1.0).then_inc(plan_step, 1)
            dve.wait_ge(plan_step, 1)
            for i in range(2):
                V.memset(Vbd[i][0:S, :, :, 2 * DK:2 * DK + 1], 1.0)
                V.memset(Vbd[i][S:P, :, :, 2 * DK + 1:VW], 1.0)
            dve.wait_ge(setup_in, SETUP)
            V.tensor_copy(tri[:, :], cst[:, C_TRI:C_TRI + P])
            V.tensor_copy(ind[:, :], cst[0:2, C_IND:C_IND + P]).then_inc(consts_done, 1)
            dve.wait_ge(tanh_done, 1)
            V.tensor_scalar(wo[0][:, :], wo[0][:, :], tg[:, 0:1], None, ALU.mult).then_inc(wo_scaled, 1)
            dve.wait_ge(bv_done, 1)
            V.scalar_tensor_tensor(orow[0][:, :], bo[0][:, :], tg[:, 0:1], bank6[:, 0:DM],
                                   ALU.mult, ALU.add).then_inc(orow_done, 1)
            steps(dve, 0, step)

            link = chain(plan_step, 1)
            dve.wait_ge(cnt_done, 1)
            link(V.tensor_copy(cnt[:, :], bank6[:, 0:E0]))
            V.tensor_copy(cnti[:, :], cnt[0:1, :]).then_inc(cnti_ready, 1)
            link(V.tensor_tensor(cge, cnt[:, :].unsqueeze(2).to_broadcast([P, E0, TOK // ET]),
                                 cst[:, C_THR:C_THR + TOK // ET].unsqueeze(1).to_broadcast([P, E0, TOK // ET]), ALU.is_gt))
            link(V.tensor_reduce(ntl[:, :], cge, AX, ALU.add))
            link(V.tensor_tensor_scan(nend[:, :], oneE[:, :], ntl[0:1, :], 0.0, ALU.mult, ALU.add))
            link(V.tensor_scalar(nend[:, :], nend[:, :], float(ET), None, ALU.mult))
            link(V.tensor_scalar(jump[:, :], ntl[:, :], -float(ET), float(RE), ALU.mult, ALU.add))
            rows = cst[0:1, C_ROW:C_ROW + NT]
            link(V.tensor_tensor(tge, rows.unsqueeze(2).to_broadcast([1, NT, E0 - 1]),
                                 nend[:, 0:E0 - 1].unsqueeze(1).to_broadcast([1, NT, E0 - 1]), ALU.is_ge))
            link(V.tensor_tensor(tjump, tge,
                                 jump[0:1, 0:E0 - 1].unsqueeze(1).to_broadcast([1, NT, E0 - 1]), ALU.mult))
            link(V.tensor_reduce(tef[:, :], tge, AX, ALU.add))
            link(V.tensor_reduce(trf[:, :], tjump, AX, ALU.add))
            link(V.tensor_tensor(trf[:, :], trf[:, :], rows, ALU.add))
            link(V.tensor_scalar(last[:, :], ntl[0:1, E0 - 1:E0], -1.0, 0.0, ALU.add, ALU.max))
            link(V.tensor_scalar(last[:, :], last[:, :], float(ET), float((E0 - 1) * RE), ALU.mult, ALU.add))
            link(V.tensor_scalar(trf[:, :], trf[:, :], last[:, 0:1], None, ALU.min))
            link(V.tensor_copy(tei[:, :], tef[:, :]))
            V.tensor_copy(tri_row[:, :], trf[:, :]).then_inc(plan_ready, 1)

            link = chain(move_step, 0)
            link(V.tensor_copy(place[:, :, :], pos_all[:, :, :]))
            for e in range(1, E0):
                link(V.tensor_scalar(moved, pos_all[:, :, :], float(e * RE), jump[:, e - 1:e], ALU.is_ge, ALU.mult))
                link(V.tensor_tensor(place[:, :, :], place[:, :, :], moved, ALU.subtract))
            V.tensor_copy(place[:, :, :], place[:, :, :]).then_inc(place_ready, 1)

            link = chain(w_step, 0)
            dve.wait_ge(dexp_done, 2)
            link(V.tensor_reduce(den[:, :], d_all, AX, ALU.add))
            link(V.reciprocal(ent[:, :], den[:, :]))
            link(V.tensor_tensor(p2[:, :], p2[:, :], ent[:, :], ALU.mult))
            link(V.scalar_tensor_tensor(den[:, :], ent[:, :], 1e-8, p2[:, :], ALU.add, ALU.add))
            link(V.reciprocal(den[:, :], den[:, :]))
            V.scalar_tensor_tensor(w_all[:, :, 0], ent[:, :], tg[:, 2:3], den[:, :], ALU.mult, ALU.mult)
            V.scalar_tensor_tensor(w_all[:, :, 1], p2[:, :], tg[:, 2:3], den[:, :], ALU.mult, ALU.mult).then_inc(w_ready, 1)

            def expert_of(u, k):
                return dve.value_load(tei[0:1, sl(at(u, k, per=4))], min_val=0, max_val=E0 - 1)

            def stage_w1(u, k, e):
                wait(dve, h_done, at(u, k, 2, -2, 4))
                V.tensor_copy(w1h[k % 2], w1a[:, bass.ds(e * F0, F0)]).then_inc(w1_ready, 1)
                wait(dve, gelu_done, at(u, k, FB0, -3 * FB0, 4))
                V.tensor_copy(b1s[k % 4][:, :], b1a[:, bass.ds(e * FB0, FB0)]).then_inc(w1_ready, 1)
                wait(dve, yo_ready, at(u, k, 1, -3, 4))
                V.tensor_copy(b2s[k % 4], b2a[:, bass.ds(e * DM, DM)]).then_inc(b2_ready, 1)

            def stage_w2(u, k, e):
                wait(dve, y_done, at(u, k, 1, -1, 4))
                V.tensor_copy(w2s[k % 2], w2a[:, bass.ds(e * F0, F0)]).then_inc(w2_ready, 1)

            def rows_turned(u, k):
                dve.wait_ge(xinTh_ready, at(u, k, 1, 1, 4))
                V.tensor_tensor(xinTl[k % 2], ps_p[:, k % 2, 0:ET], xinTh[k % 2].bitcast(F32), ALU.subtract).then_inc(xinT_ready, 1)

            def rows_made(u, k):
                i = k % 2
                dve.wait_ge(b2_ready, at(u, k, 1, 1, 4))
                dve.wait_ge(y_done, at(u, k, 1, 1, 4))
                wait(dve, rows_out[i], u * 32 + 16 * (k // 2))
                V.tensor_tensor(yo[i], ps_m[:, i, 0:ET].rearrange("p (t d) -> p t d", t=2),
                                b2s[k % 4].unsqueeze(1).to_broadcast([P, 2, DM]), ALU.add).then_inc(yo_ready, 1)

            def tile_step(u, k, first=False, more=True):
                if more:
                    e = expert_of(u, k + 1)
                    stage_w1(u, k + 1, e)
                    rows_turned(u, k + 1)
                if not first:
                    rows_made(u, k - 1)
                if more:
                    stage_w2(u, k + 1, e)

            dve.wait_ge(experts_in, 16 * 6)
            tile_step(0, -1, first=True)
            tile_step(0, 0, first=True)
            for k in range(1, 4):
                tile_step(0, k)
            with dve.Fori(1, NT // 4 - 1) as u:
                for k in range(4):
                    tile_step(u, k)
            for k in range(NT - 4, NT - 1):
                tile_step(0, k)
            tile_step(0, NT - 1, more=False)
            tile_step(0, NT, more=False)

            dve.wait_ge(folded_done, 1)
            V.tensor_copy(wq[1][:, :], bank6[:, 0:DM]).then_inc(folded_ready, 1)
            steps(dve, 1, step)

            link = chain(ent_step, 0)
            dve.wait_ge(gate_step, 2 * GROUPS)
            link(V.tensor_scalar(ent[:, :], z_all[:, :], db2[:, 0:1], None, ALU.add))
            link(V.scalar_tensor_tensor(ent2[:, :], ent[:, :], -1.0, ent[:, :], ALU.mult, ALU.max))
            link = chain(gates_step, 0)

            def be(ap):
                return ap.unsqueeze(2).to_broadcast([P, TILES, E1])

            link(V.tensor_reduce(gmx[:, :], gl[:, :, :], AX, ALU.max))
            link(V.tensor_tensor(we[:, :, :], gl[:, :, :], be(gmx[:, :]), ALU.subtract))
            other = gl[:, :, :].unsqueeze(2).to_broadcast([P, TILES, E1, E1])
            own = gl[:, :, :].unsqueeze(3).to_broadcast([P, TILES, E1, E1])
            tie = cst[:, C_TIE:C_ALL].unsqueeze(1).to_broadcast([P, TILES, E1 * E1])
            link(V.tensor_tensor(big[0], other, own, ALU.is_gt))
            link(V.tensor_tensor(big[1], other, own, ALU.is_equal))
            flat1 = big[1].rearrange("p t e f -> p t (e f)")
            link(V.tensor_tensor(flat1, flat1, tie, ALU.mult))
            link(V.tensor_tensor(big[0], big[0], big[1], ALU.add))
            link(V.tensor_reduce(sel, big[0], AX, ALU.add))
            dve.wait_ge(ent_act, 2)
            link(V.scalar_tensor_tensor(ent[:, :], ent[:, :], 0.0, ent2[:, :], ALU.max, ALU.add))
            link(V.tensor_scalar(kt[:, :], ent[:, :], 0.5, 1 / 1.5, ALU.subtract, ALU.mult))
            link(V.tensor_scalar(kt[:, :], kt[:, :], 0.0, 1.0, ALU.max, ALU.min))
            link(V.tensor_scalar(kt[:, :], kt[:, :], float(E1 - 1), 1.0, ALU.mult, ALU.add))
            link(V.tensor_scalar(kt[:, :], kt[:, :], ROUND, None, ALU.add))
            link(V.tensor_scalar(kt[:, :], kt[:, :], ROUND, None, ALU.subtract))
            link(V.tensor_tensor(sel, sel, be(kt[:, :]), ALU.is_lt))
            dve.wait_ge(gates_act, 1)
            link(V.tensor_tensor(we[:, :, :], we[:, :, :], sel, ALU.mult))
            link(V.tensor_reduce(gmx[:, :], we[:, :, :], AX, ALU.add))
            link(V.reciprocal(gmx[:, :], gmx[:, :]))
            link(V.tensor_tensor(we[:, :, :], we[:, :, :], be(gmx[:, :]), ALU.mult))
            V.tensor_scalar(we[:, :, :], we[:, :, :], tg[:, 3:4], None, ALU.mult).then_inc(gates_ready, 1)
            dve.wait_ge(gates_ready, 1)

            def add_expert(u, e):
                wait(dve, acc_y, u * 16 + 4 * e)
                for t in range(4):
                    tile = flat(x[:, sl(u * 4 + t), :])
                    V.scalar_tensor_tensor(tile, c2[:, e, :], flat(we[:, sl(u * 4 + t), e:e + 1]), tile,
                                           ALU.mult, ALU.add).then_inc(acc_b, 1)
                dve.wait_ge(y1_done, u * 4 + (e + 1))
                for t in range(4):
                    tile = flat(x[:, sl(u * 4 + t), :])
                    dve.wait_ge(acc_b, u * 16 + (4 * e + t + 1))
                    V.scalar_tensor_tensor(tile, ps_p[:, e % 2, DM * t:DM * (t + 1)], flat(we[:, sl(u * 4 + t), e:e + 1]), tile,
                                           ALU.mult, ALU.add).then_inc(acc_y, 1)

            with dve.Fori(0, TILES // 4) as u:
                for e in range(E1):
                    add_expert(u, e)

        @block.tensor
        def _(pe):
            mm, turn = nc.tensor.matmul, nc.tensor.transpose

            def heads_turned(g):
                bank_free(pe, 6, g.plus(2), "OT")
                pe.wait_ge(on_ready, g.count(2, 2))
                for t in range(2):
                    ins = turn(bank6[:, P * t:P * t + P], On[g.par][:, t, :], ident)
                ins.then_inc(ot_done, 1)

            def scores(g, q):
                if q == 0:
                    if g.plus(-4).real():
                        pe.wait_ge(lg_read, g.plus(-4).count(1, 1))
                    pe.wait_ge(spread, g.count(2, 2))
                elif q == 2:
                    if g.layer == 0 and g.par and g.plus(-4).real():
                        pe.wait_ge(rank_read, g.plus(-4).block(1))
                    pe.wait_ge(v_ready, g.count(1, 1))
                if g.layer == 1:
                    if q % 2 == 0:
                        carry(lambda: mm(ps_s[:, q, 0:1], ones[:, :], ones[:, 0:1], start=True, stop=True,
                                         skip_group_check=True), g.at())
                    mm(ps_s[:, q, :].rearrange("p (t h k) -> p t h k", t=2, h=4), ind[:, :],
                       negm[:, sl(g.at(2), 2), :].unsqueeze(2).to_broadcast([2, 2, 4, S]),
                       start=True, stop=False, skip_group_check=True)
                for b in range(4):
                    ins = mm(ps_s[S * (b % 2):S * (b % 2) + S, q, GT * (b // 2):GT * (b // 2) + GT],
                             qT[g.par][:, q, S * b:S * b + S], Kbd[g.par][:, b, :, :].rearrange("p h k -> p (h k)"),
                             start=(g.layer == 0), stop=True, skip_group_check=True)
                ins.then_inc(s_done, 1)

            def tokens_turned(g):
                bank_free(pe, 7, g.plus(-1), "XT")
                pe.wait_ge(xn_ready, g.count(2, 2))
                for t in range(2):
                    ins = turn(bank7[:, P * t:P * t + P], xn[g.par][:, t, :], ident)
                ins.then_inc(xt_done, 1)

            def project_out(g):
                bank_free(pe, 6, g.plus(2), "OUT")
                pe.wait_ge(ot_ready, g.count(1, 1))
                for t in range(2):
                    ins = mm(bank6[:, P * t:P * t + P], OT[g.par][:, P * t:P * t + P], wo[g.layer][:, :], start=True, stop=True)
                ins.then_inc(out_done, 1)

            def probs_turned(g, c):
                pr, half = c // 2, c % 2
                pe.wait_ge(exp_done, g.count(4, 2 * half + 2))
                wait(pe, pt_ready, g.count(4, c - 1))
                for i in range(4):
                    j = 4 * half + i
                    col = GT * pr + P * (j % 2)
                    ins = turn(ps_p[:, c % 2, P * i:P * i + P], Pr[g.par][:, j // 2, col:col + P], ident)
                ins.then_inc(pt_done, 1)

            def probs_by_values(g, c):
                pr, half = c // 2, c % 2
                if half == 0:
                    bank_free(pe, 6 if pr else 7, g.plus(1), f"O{pr}")
                pe.wait_ge(pt_ready, g.count(4, c + 1))
                pe.wait_ge(v_ready, g.count(1, 1))
                for i in range(4):
                    j = 4 * half + i
                    ins = mm((bank7, bank6)[pr][:, 2 * VW * j:2 * VW * (j + 1)].rearrange("p (b c) -> p b c", b=2),
                             PT[c][:, P * i:P * i + P], Vbd[g.par][:, 2 * pr:2 * pr + 2, j, :], start=True, stop=True)
                ins.then_inc(pv_done, 1)

            def keys_queries(g):
                wait(pe, sub_done, g.count(4, -2))
                if g.layer == 0:
                    pe.wait_ge(ctx_in[g.par], g.half_count())
                    mm(kq_bank[:, 0:GT], wk[0][:, :], ctxg[g.par][:, :, 0, :], start=True, stop=True)
                pe.wait_ge(xnT_ready, g.count(1, 1))
                mm(kq_bank[:, GT:2 * GT], wq[g.layer][:, :], xnT[g.par][:, :], start=True, stop=True).then_inc(kq_done, 1)

            def values(g):
                wait(pe, sub_done, g.count(4, 0))
                pe.wait_ge(ctx_in[g.par], g.half_count())
                for b in range(4):
                    ins = mm(v_bank[:, P * b:P * b + P],
                             ctxg[g.par][:, b, :, :].rearrange("p i k -> p (i k)"), wv[g.layer][:, :],
                             start=True, stop=True)
                ins.then_inc(v_done, 1)

            def tokens2_turned(g):
                bank_free(pe, 7, g.plus(3), "XT2")
                pe.wait_ge(xn2_ready, g.count(2, 2))
                for t in range(2):
                    ins = turn(bank7[:, P * t:P * t + P], xn2[g.par][:, t, :], ident)
                ins.then_inc(xt2_done, 1)

            def logits(g):
                scores_read(pe, g.plus(3), 0)
                pe.wait_ge(xn2T_ready, g.count(1, 1))
                w = (wr0, wr1)[g.layer]
                n = w.shape[1]
                for t in range(2):
                    ins = mm(lg_bank[:, n * t:n * t + n], xn2T[g.par][:, P * t:P * t + P], w[:, :], start=True, stop=True)
                ins.then_inc(lg_done, 1)

            def ranks(g):
                scores_read(pe, g.plus(3), 2)
                pe.wait_ge(hot_ready, g.block(1))
                wait(pe, seen_ready, g.block(0))
                o = rk_bank[:, 0:4 * E0].rearrange("p (t e) -> p t e", t=4)
                mm(o, tri[:, :], hotb[:, :, :], start=True, stop=False, skip_group_check=True)
                for i in range(1, 4):
                    mm(o[:, i:, :], ones[:, :], hotb[:, 0:4 - i, :], start=False, stop=False, skip_group_check=True)
                mm(o, ones[:, :], seenb[:, :].unsqueeze(1).to_broadcast([P, 4, E0]), start=False, stop=True,
                   skip_group_check=True).then_inc(rk_done, 1)

            def step(g):
                def have(d):
                    return g.plus(d).real()

                if g.layer == 0 and isinstance(g.u, int) and g.k == 3:
                    pe.wait_ge(late_in, LATE)
                p = g.plus(-1)
                if have(0):
                    scores(g, 0)
                if have(1):
                    tokens_turned(g.plus(1))
                if have(0):
                    scores(g, 1)
                if have(-3):
                    tokens2_turned(g.plus(-3))
                if have(0):
                    scores(g, 2)
                    scores(g, 3)
                if have(-2):
                    heads_turned(g.plus(-2))
                if have(1):
                    keys_queries(g.plus(1))
                if have(-3):
                    logits(g.plus(-3))
                if have(-1):
                    probs_turned(p, 0)
                if have(-2):
                    project_out(g.plus(-2))
                if have(-1):
                    probs_turned(p, 1)
                    probs_by_values(p, 0)
                    probs_turned(p, 2)
                    probs_by_values(p, 1)
                if have(1):
                    values(g.plus(1))
                if have(-1):
                    probs_turned(p, 3)
                    probs_by_values(p, 2)
                    probs_by_values(p, 3)
                if g.layer == 0 and g.par == 0 and have(-3):
                    ranks(g.plus(-3))

            pe.wait_ge(setup_in, SETUP)
            pe.wait_ge(wo_scaled, 1)
            mm(bank6[:, 0:DM], bcol[:, 2:3].to_broadcast([P, P]), wo[0][:, :], start=True, stop=True).then_inc(bv_done, 1)
            pe.wait_ge(orow_done, 1)
            pe.wait_ge(consts_done, 1)
            steps(pe, 0, step)
            pe.wait_ge(seen_ready, TILES // 4)
            mm(bank6[:, 0:E0], ones[:, :], seenb[:, :], start=True, stop=True).then_inc(cnt_done, 1)

            def rows_turned(u, k):
                i = k % 2
                pe.wait_ge(rows_in[k % 4], u * 16 + 16 * (k // 4 + 1))
                wait(pe, xinT_ready, at(u, k, 1, -1, 4))
                for t in range(2):
                    ins = turn(ps_p[:, i, P * t:P * t + P], xin[k % 4][:, t, :], ident)
                ins.then_inc(et_done, 1)

            def hidden(u, k):
                i = k % 2
                pe.wait_ge(w1l_ready, at(u, k, 1, 1, 4))
                pe.wait_ge(xinT_ready, at(u, k, 1, 1, 4))
                wait(pe, gelu_done, at(u, k, FB0, -FB0, 4))
                for f in range(FB0):
                    o = ps_s[:, 2 * i + f // 2, ET * (f % 2):ET * (f % 2 + 1)]
                    w = slice(P * f, P * f + P)
                    mm(o, w1h[i][:, w], xinTh[i], start=True, stop=False, skip_group_check=True)
                    mm(o, w1h[i][:, w], xinTl[i], start=False, stop=False, skip_group_check=True)
                    ins = mm(o, w1l[i][:, w], xinTh[i], start=False, stop=True, skip_group_check=True)
                    if f % 2:
                        ins.then_inc(h_done, 1)

            def rows_made(u, k):
                i = k % 2
                pe.wait_ge(w2_ready, at(u, k, 1, 1, 4))
                pe.wait_ge(gelu_done, at(u, k, FB0, FB0, 4))
                wait(pe, yo_ready, at(u, k, 1, -1, 4))
                for t in range(2):
                    for f in range(FB0):
                        ins = mm(ps_m[:, i, P * t:P * t + P], hT[i][:, f, P * t:P * t + P], w2s[i][:, P * f:P * f + P],
                                 start=(f == 0), stop=(f == FB0 - 1))
                ins.then_inc(y_done, 1)

            def tile_step(u, k):
                pe_first = isinstance(u, int)
                if not pe_first or k + 1 < NT:
                    rows_turned(u, k + 1)
                if not pe_first or 0 <= k < NT:
                    hidden(u, k)
                if not pe_first or k >= 1:
                    rows_made(u, k - 1)

            pe.wait_ge(cnti_ready, 1)
            pe.wait_ge(xn2T_ready, GROUPS)
            for k in range(-1, 4):
                tile_step(0, k)
            with pe.Fori(1, NT // 4 - 1) as u:
                for k in range(4):
                    tile_step(u, k)
            for k in range(NT - 4, NT + 1):
                tile_step(0, k)

            pe.wait_ge(yo_ready, NT)
            pe.wait_ge(wo_scaled, 2)
            mm(bank6[:, 0:DM], wq[1][:, :], wk[1][:, :], start=True, stop=True).then_inc(folded_done, 1)
            pe.wait_ge(folded_ready, 1)
            steps(pe, 1, step)

            def hidden1(u, k):
                e, c = k % E1, k // E1
                if e == 0:
                    pe.wait_ge(x_split, u * 4 + (2 * c + 2))
                for f in range(FB1):
                    n = 2 * k + f
                    wait(pe, relu_done, u * (4 * E1) + (n - 3))
                    w = slice(F1 * e + P * f, F1 * e + P * f + P)
                    mm(ps_s[:, n % 4, :], v1h[:, w], xh[c % 2], start=True, stop=False)
                    mm(ps_s[:, n % 4, :], v1h[:, w], xl[c % 2], start=False, stop=False)
                    mm(ps_s[:, n % 4, :], v1l[:, w], xh[c % 2], start=False, stop=True).then_inc(h1_done, 1)

            def rows1(u, k):
                e = k % E1
                pe.wait_ge(relu_done, u * (4 * E1) + (2 * k + 2))
                wait(pe, acc_y, u * (8 * E1) + 4 * (k - 1))
                for t in range(4):
                    for f in range(FB1):
                        c = (e * FB1 + f) * P
                        ins = mm(ps_p[:, k % 2, P * t:P * t + P], hD[k % 2][:, f, P * t:P * t + P], v2[:, c:c + P],
                                 start=(f == 0), stop=(f == FB1 - 1))
                ins.then_inc(y1_done, 1)

            pe.wait_ge(xn2T_ready, 2 * GROUPS)
            pe.wait_ge(gate_step, 2 * GROUPS)
            pe.wait_ge(v1_split, 2)
            pe.wait_ge(v_in, 16 * 2)
            hidden1(0, 0)
            for k in range(1, 2 * E1 + 1):
                hidden1(0, k)
                rows1(0, k - 1)
            with pe.Fori(1, TOK // CH // 2 - 1) as u:
                for k in range(1, 2 * E1 + 1):
                    hidden1(u, k)
                    rows1(u, k - 1)
            for k in range(1, 2 * E1):
                hidden1(TOK // CH // 2 - 1, k)
                rows1(TOK // CH // 2 - 1, k - 1)
            rows1(TOK // CH // 2 - 1, 2 * E1 - 1)


def kernel(**inputs):
    import concourse.bacc as bacc
    from concourse.bass_utils import run_bass_kernel_spmd

    f = {n: np.ascontiguousarray(v) for n, v in inputs.items()}

    def blocks(w):
        d = np.zeros((DM, DM), np.float32)
        for h in range(H):
            d[h * DK:(h + 1) * DK, h * DK:(h + 1) * DK] = w
        return d

    arrays = {n: f[n] for n in ("L0_xattn_Wq", "L0_xattn_Wk", "L0_xattn_Wv", "L0_xattn_Wo", "L0_xattn_bo", "L1_xattn_bo",
                                "L0_ffn_W1", "L0_ffn_W2", "L1_ffn_gate_b", "L1_ffn_dp_b1", "L1_ffn_dp_b2",
                                "L1_ffn_ew1", "L1_ffn_ew2")}
    arrays |= {
        "x": f["x"].reshape(TOK, DM),
        "ctxT": np.broadcast_to(f["ctx_1024"].transpose(2, 0, 1)[:, :, None, :], (DM, B, 2, S)).reshape(DM, 2 * TOK),
        "mask": f["mask_Bx1x1xS2_if1"].reshape(B, S),
        "consts": constants(),
        "bcol": np.stack([f["L0_xattn_bq"], f["L0_xattn_bk"], f["L0_xattn_bv"]], 1),
        "gates": np.concatenate([f["g_xattn"], f["g_ffn"]]),
        "wq1": blocks(f["L1_xattn_Wq"]), "wk1": blocks(f["L1_xattn_Wk"]), "wv1": blocks(f["L1_xattn_Wv"]).T,
        "wo1": f["L1_xattn_Wo"].T,
        "wr0": f["L0_ffn_router_w"].T,
        "wr1": np.concatenate([f["L1_ffn_gate_w"], f["L1_ffn_dp_w1"]], 1),
        "dw2": f["L1_ffn_dp_w2"].reshape(-1),
        "b1a": f["L0_ffn_b1"].reshape(E0 * FB0, P).T,
        "b2a": f["L0_ffn_b2"].reshape(-1),
        "c1": f["L1_ffn_eb1"].reshape(E1 * FB1, P).T,
        "c2": f["L1_ffn_eb2"].reshape(-1),
    }
    arrays = {n: np.ascontiguousarray(v) for n, v in arrays.items()}
    nc = bacc.Bacc("TRN2", target_bir_lowering=False, num_devices=1)
    ins = {n: nc.dram_tensor(f"in_{n}", v.shape, mybir.dt.from_np(v.dtype), kind="ExternalInput").ap()
           for n, v in arrays.items()}
    out = nc.dram_tensor("out", (TOK, DM), F32, kind="ExternalOutput").ap()
    build(nc, ins, out)
    r = run_bass_kernel_spmd(nc, [{f"in_{n}": v for n, v in arrays.items()}], core_ids=[0])
    return r.results[0]["out"].reshape(B, S, DM)
```
